# Optimizing a Trainium2 kernel written in Bass

```python
import numpy as np
import jax
import jax.numpy as jnp

def _softmax(x, axis=-1):
    return jax.nn.softmax(x, axis=axis)

def _gelu(x):
    return jax.nn.gelu(x, approximate=True)

def _silu(x):
    return jax.nn.silu(x)

def _sigmoid(x):
    return jax.nn.sigmoid(x)

def _layernorm(x, axis=-1, eps=1e-05):
    m = jnp.mean(x, axis=axis, keepdims=True)
    v = jnp.var(x, axis=axis, keepdims=True)
    return (x - m) / jnp.sqrt(v + eps)

def _scatter_add(tgt, idx, src, axis=0):
    return tgt.at[idx].add(src)

def _segment_sum(src, seg, n):
    return jax.ops.segment_sum(src, seg, n)
kernel_name = 'mk_decoder_preln_d1_seqx_r8_62151f'

def setup_inputs(seed: int=0):
    np.random.seed(seed)
    _w = jnp.asarray

    def _rec_inputs():
        import jax
        import jax.numpy as jnp
        _rk = jax.random.key(seed)
        x = -0.0003929 + 0.9999 * jax.random.normal(jax.random.fold_in(_rk, 1), (8, 128, 128), jnp.float32)
        _lenS = 128 - jax.random.randint(jax.random.fold_in(_rk, 7), (8,), 0, max(1, 128 // 4) + 1, jnp.int32)
        _lenS2 = 128 - jax.random.randint(jax.random.fold_in(_rk, 8), (8,), 0, max(1, 128 // 4) + 1, jnp.int32)
        _ctx_1024P = jax.random.normal(jax.random.fold_in(_rk, 11), (8, 16, 128), jnp.float32)
        _ctx_1024c = jax.random.dirichlet(jax.random.fold_in(_rk, 511), 0.3 * jnp.ones((16,), jnp.float32), (8, 128))
        _ctx_1024t = jnp.einsum('bsk,bkd->bsd', _ctx_1024c, _ctx_1024P)
        _ctx_1024t = _ctx_1024t * jax.lax.rsqrt(jnp.mean(jnp.square(_ctx_1024t)) + 1e-12) * 0.953939
        ctx_1024 = 2.81802e-05 + 1.00001 * (_ctx_1024t + 0.3 * jax.random.normal(jax.random.fold_in(_rk, 611), (8, 128, 128), jnp.float32))
        _validS = jnp.arange(128)[None, :] < _lenS[:, None]
        _validS2 = jnp.arange(128)[None, :] < _lenS2[:, None]
        _causal = jnp.tril(jnp.ones((128, 128), dtype=bool))
        mask_BxSxS2_fk0 = jnp.where(jnp.broadcast_to(_validS2[:, None, :], (8, 128, 128)), -1000000000.0, 0.0).astype(jnp.float32)
        return (x, ctx_1024, mask_BxSxS2_fk0)
    x, ctx_1024, mask_BxSxS2_fk0 = _rec_inputs()

    def _L0_attn_setup():
        import jax, jax.numpy as jnp
        import numpy as np
        B, S, HID = (4, 128, 128)
        H = 8
        HD = HID // H
        NQ = 8
        RATIO = 0.5
        FF = 4 * HID
        EPS_COS = 1e-08
        LN_EPS = 1e-05

        def _layernorm(x, g, b):
            m = jnp.mean(x, axis=-1, keepdims=True)
            v = jnp.var(x, axis=-1, keepdims=True)
            return (x - m) * jax.lax.rsqrt(v + LN_EPS) * g + b
        key = jax.random.key(seed)
        ks = jax.random.split(key, 24)
        sc = 0.02
        inp = {'x': jax.random.normal(ks[0], (B, S, HID), jnp.float32), 'Wq': jax.random.normal(ks[1], (H, HID, HD)) * sc, 'bq': jnp.zeros((H, HD)), 'Wk': jax.random.normal(ks[2], (H, HID, HD)) * sc, 'bk': jnp.zeros((H, HD)), 'Wv': jax.random.normal(ks[3], (H, HID, HD)) * sc, 'bv': jnp.zeros((H, HD)), 'Wc2q': jax.random.normal(ks[4], (H, HD, NQ)) * sc, 'bc2q': jnp.zeros((H, NQ)), 'Wo': jax.random.normal(ks[5], (HID, HID)) * sc, 'bo': jnp.zeros((HID,)), 'g1': jnp.ones((HID,)), 'beta1': jnp.zeros((HID,)), 'g2': jnp.ones((HID,)), 'beta2': jnp.zeros((HID,)), 'W1': jax.random.normal(ks[6], (HID, FF)) * sc, 'b1': jnp.zeros((FF,)), 'Wm': jax.random.normal(ks[7], (FF, NQ)) * sc, 'bm': jnp.zeros((NQ,)), 'Wqo': jax.random.normal(ks[8], (NQ, FF)) * sc, 'bqo': jnp.zeros((FF,)), 'W2': jax.random.normal(ks[9], (FF, HID)) * sc, 'b2': jnp.zeros((HID,))}
        return inp
    _L0_attn_all = _L0_attn_setup()
    _L0_attn_in = {k: v for k, v in _L0_attn_all.items() if k in ('Wq', 'bq', 'Wk', 'bk', 'Wv', 'bv', 'Wc2q', 'bc2q', 'Wo', 'bo', 'g1', 'beta1', 'g2', 'beta2', 'W1', 'b1', 'Wm', 'bm', 'Wqo', 'bqo', 'W2', 'b2')}
    del _L0_attn_all

    def _L0_xattn_setup():
        import jax, jax.numpy as jnp
        import numpy as np
        B, NQ, NK, DQ, DV = (8, 256, 256, 128, 128)
        NEG = -1000000000.0
        key = jax.random.key(seed)
        kq, kk, kv = jax.random.split(key, 3)
        queries = jax.random.normal(kq, (B, NQ, DQ), dtype=jnp.float32)
        keys = jax.random.normal(kk, (B, NK, DQ), dtype=jnp.float32)
        values = jax.random.normal(kv, (B, NK, DV), dtype=jnp.float32)
        i = jnp.arange(NQ)[:, None]
        j = jnp.arange(NK)[None, :]
        attention_mask = jnp.where(j > i, jnp.float32(NEG), jnp.float32(0.0))
        attention_mask = jnp.broadcast_to(attention_mask, (B, NQ, NK)).copy()
        return {'queries': queries, 'keys': keys, 'values': values, 'attention_mask': attention_mask}
    _L0_xattn_all = _L0_xattn_setup()
    _L0_xattn_in = {k: v for k, v in _L0_xattn_all.items() if k in ()}
    del _L0_xattn_all

    def _L0_ffn_setup():
        import jax, jax.numpy as jnp
        import numpy as np
        import math
        D_MODEL = 128
        N_EXPERTS = 16
        D_FF = 512
        CAP_FACTOR = 1.25
        MIN_CAPACITY = 4

        def _capacity(num_tokens, num_experts):
            cap = math.floor(CAP_FACTOR * num_tokens / num_experts)
            cap += cap % 2
            return max(cap, MIN_CAPACITY)

        def _top1_router(gate_logits, capacity):
            s, e = gate_logits.shape
            probs = jax.nn.softmax(gate_logits, axis=-1)
            top1 = jnp.argmax(gate_logits, axis=-1)
            mask = jax.nn.one_hot(top1, e, dtype=jnp.int32)
            ranks = jnp.cumsum(mask, axis=0) - 1
            mask = mask * (ranks < capacity).astype(jnp.int32)
            rank1 = jnp.sum(mask * ranks, axis=-1)
            ranks_oh = jax.nn.one_hot(rank1, capacity, dtype=probs.dtype)
            weight = mask.astype(probs.dtype) * probs
            combine_weights = weight[:, :, None] * ranks_oh[:, None, :]
            sec_mask = combine_weights > 0
            return (combine_weights, sec_mask)
        key = jax.random.key(seed)
        k1, k2, k3, k4 = jax.random.split(key, 4)
        x = jax.random.normal(k1, (4, 256, D_MODEL), dtype=jnp.float32)
        gate_w = jax.random.normal(k2, (N_EXPERTS, D_MODEL), dtype=jnp.float32) * math.sqrt(0.1 / D_MODEL)
        w1 = jax.random.normal(k3, (N_EXPERTS, D_MODEL, D_FF), dtype=jnp.float32) * (1.0 / math.sqrt(D_MODEL))
        w2 = jax.random.normal(k4, (N_EXPERTS, D_FF, D_MODEL), dtype=jnp.float32) * (1.0 / math.sqrt(D_FF))
        return {'x': x, 'gate_w': gate_w, 'w1': w1, 'w2': w2}
    _L0_ffn_all = _L0_ffn_setup()
    _L0_ffn_in = {k: v for k, v in _L0_ffn_all.items() if k in ('gate_w', 'w1', 'w2')}
    del _L0_ffn_all
    return {'x': x, 'ctx_1024': ctx_1024, 'mask_BxSxS2_fk0': mask_BxSxS2_fk0, 'L0_attn_Wq': _L0_attn_in['Wq'], 'L0_attn_bq': _L0_attn_in['bq'], 'L0_attn_Wk': _L0_attn_in['Wk'], 'L0_attn_bk': _L0_attn_in['bk'], 'L0_attn_Wv': _L0_attn_in['Wv'], 'L0_attn_bv': _L0_attn_in['bv'], 'L0_attn_Wc2q': _L0_attn_in['Wc2q'], 'L0_attn_bc2q': _L0_attn_in['bc2q'], 'L0_attn_Wo': _L0_attn_in['Wo'], 'L0_attn_bo': _L0_attn_in['bo'], 'L0_attn_g1': _L0_attn_in['g1'], 'L0_attn_beta1': _L0_attn_in['beta1'], 'L0_attn_g2': _L0_attn_in['g2'], 'L0_attn_beta2': _L0_attn_in['beta2'], 'L0_attn_W1': _L0_attn_in['W1'], 'L0_attn_b1': _L0_attn_in['b1'], 'L0_attn_Wm': _L0_attn_in['Wm'], 'L0_attn_bm': _L0_attn_in['bm'], 'L0_attn_Wqo': _L0_attn_in['Wqo'], 'L0_attn_bqo': _L0_attn_in['bqo'], 'L0_attn_W2': _L0_attn_in['W2'], 'L0_attn_b2': _L0_attn_in['b2'], 'L0_ffn_gate_w': _L0_ffn_in['gate_w'], 'L0_ffn_w1': _L0_ffn_in['w1'], 'L0_ffn_w2': _L0_ffn_in['w2']}

def reference(x, ctx_1024, mask_BxSxS2_fk0, L0_attn_Wq, L0_attn_bq, L0_attn_Wk, L0_attn_bk, L0_attn_Wv, L0_attn_bv, L0_attn_Wc2q, L0_attn_bc2q, L0_attn_Wo, L0_attn_bo, L0_attn_g1, L0_attn_beta1, L0_attn_g2, L0_attn_beta2, L0_attn_W1, L0_attn_b1, L0_attn_Wm, L0_attn_bm, L0_attn_Wqo, L0_attn_bqo, L0_attn_W2, L0_attn_b2, L0_ffn_gate_w, L0_ffn_w1, L0_ffn_w2):
    import jax
    import jax.numpy as jnp

    def _L0_attn_ref(x, Wq, bq, Wk, bk, Wv, bv, Wc2q, bc2q, Wo, bo, g1, beta1, g2, beta2, W1, b1, Wm, bm, Wqo, bqo, W2, b2):
        import jax, jax.numpy as jnp
        import numpy as np
        B, S, HID = (4, 128, 128)
        H = 8
        HD = HID // H
        NQ = 8
        RATIO = 0.5
        FF = 4 * HID
        EPS_COS = 1e-08
        LN_EPS = 1e-05

        def _layernorm(x, g, b):
            m = jnp.mean(x, axis=-1, keepdims=True)
            v = jnp.var(x, axis=-1, keepdims=True)
            return (x - m) * jax.lax.rsqrt(v + LN_EPS) * g + b
        Q = jnp.einsum('bsh,nhd->bnsd', x, Wq) + bq[None, :, None, :]
        K = jnp.einsum('bsh,nhd->bnsd', x, Wk) + bk[None, :, None, :]
        V = jnp.einsum('bsh,nhd->bnsd', x, Wv) + bv[None, :, None, :]
        qq = jnp.einsum('bnsd,ndq->bnsq', Q, Wc2q) + bc2q[None, :, None, :]
        kq = jnp.einsum('bnsd,ndq->bnsq', K, Wc2q) + bc2q[None, :, None, :]
        qn = jnp.linalg.norm(qq, axis=-1)
        kn = jnp.linalg.norm(kq, axis=-1)
        dots = jnp.einsum('bnsq,bntq->bnst', qq, kq)
        fid = dots / jnp.maximum(qn[..., :, None] * kn[..., None, :], EPS_COS)
        qw = fid * (1.0 + 0.1 * jnp.sin(fid * jnp.pi))
        cw = jnp.einsum('bnsd,bntd->bnst', Q, K) / np.sqrt(HD).astype(np.float32)
        aw = RATIO * qw + (1.0 - RATIO) * cw
        probs = jax.nn.softmax(aw, axis=-1)
        heads = jnp.einsum('bnst,bntd->bnsd', probs, V)
        attn = heads.transpose(0, 2, 1, 3).reshape(x.shape[0], x.shape[1], HID)
        attn = attn @ Wo + bo
        x1 = _layernorm(x + attn, g1, beta1)
        h = x1 @ W1 + b1
        qm = h @ Wm + bm
        qe = jnp.tanh(qm) * jnp.cos(qm * (jnp.pi / 4))
        ha = qe @ Wqo + bqo
        ff = ha @ W2 + b2
        out = _layernorm(x1 + ff, g2, beta2)
        return out

    def _L0_xattn_ref(queries, keys, values, attention_mask):
        import jax, jax.numpy as jnp
        import numpy as np
        B, NQ, NK, DQ, DV = (8, 256, 256, 128, 128)
        NEG = -1000000000.0
        d_keys = jnp.sqrt(jnp.float32(keys.shape[-1]))
        logits = jnp.einsum('bqd,bkd->bqk', queries, keys) / d_keys
        logits = jnp.where(attention_mask < -1.0, attention_mask, logits)
        attn = jax.nn.softmax(logits, axis=-1)
        attn = jnp.where(jnp.isnan(attn), jnp.float32(0.0), attn)
        return jnp.einsum('bqk,bkv->bqv', attn, values)

    def _L0_ffn_ref(x, gate_w, w1, w2):
        import jax, jax.numpy as jnp
        import numpy as np
        import math
        D_MODEL = 128
        N_EXPERTS = 16
        D_FF = 512
        CAP_FACTOR = 1.25
        MIN_CAPACITY = 4

        def _capacity(num_tokens, num_experts):
            cap = math.floor(CAP_FACTOR * num_tokens / num_experts)
            cap += cap % 2
            return max(cap, MIN_CAPACITY)

        def _top1_router(gate_logits, capacity):
            s, e = gate_logits.shape
            probs = jax.nn.softmax(gate_logits, axis=-1)
            top1 = jnp.argmax(gate_logits, axis=-1)
            mask = jax.nn.one_hot(top1, e, dtype=jnp.int32)
            ranks = jnp.cumsum(mask, axis=0) - 1
            mask = mask * (ranks < capacity).astype(jnp.int32)
            rank1 = jnp.sum(mask * ranks, axis=-1)
            ranks_oh = jax.nn.one_hot(rank1, capacity, dtype=probs.dtype)
            weight = mask.astype(probs.dtype) * probs
            combine_weights = weight[:, :, None] * ranks_oh[:, None, :]
            sec_mask = combine_weights > 0
            return (combine_weights, sec_mask)
        tokens = x.reshape(-1, D_MODEL)
        s = tokens.shape[0]
        capacity = _capacity(s, N_EXPERTS)
        gate_logits = tokens.astype(jnp.float32) @ gate_w.T
        combine_weights, sec_mask = _top1_router(gate_logits, capacity)
        dispatch = jnp.einsum('sec,sd->ecd', sec_mask.astype(tokens.dtype), tokens)
        h = jax.nn.gelu(jnp.einsum('ecd,edf->ecf', dispatch, w1))
        expert_out = jnp.einsum('ecf,efd->ecd', h, w2)
        out = jnp.einsum('sec,ecd->sd', combine_weights.astype(tokens.dtype), expert_out)
        return out.reshape(x.shape)
    x = x + _L0_attn_ref(_layernorm(x, axis=-1), L0_attn_Wq, L0_attn_bq, L0_attn_Wk, L0_attn_bk, L0_attn_Wv, L0_attn_bv, L0_attn_Wc2q, L0_attn_bc2q, L0_attn_Wo, L0_attn_bo, L0_attn_g1, L0_attn_beta1, L0_attn_g2, L0_attn_beta2, L0_attn_W1, L0_attn_b1, L0_attn_Wm, L0_attn_bm, L0_attn_Wqo, L0_attn_bqo, L0_attn_W2, L0_attn_b2)
    x = x + _L0_xattn_ref(_layernorm(x, axis=-1), ctx_1024, ctx_1024, mask_BxSxS2_fk0)
    x = x + _L0_ffn_ref(_layernorm(x, axis=-1), L0_ffn_gate_w, L0_ffn_w1, L0_ffn_w2)
    return x

_drawn_inputs = setup_inputs


def setup_inputs(seed=0):
    import zlib

    import numpy as np

    out = dict(_drawn_inputs(seed))
    spreads = {'L0_attn_bq': (0.0, 0.8),
     'L0_attn_bk': (0.0, 0.8),
     'L0_attn_bv': (0.0, 0.753),
     'L0_attn_bc2q': (0.0, 0.8),
     'L0_attn_bo': (0.0, 0.1),
     'L0_attn_g1': (1.0, 0.2),
     'L0_attn_beta1': (0.0, 0.1),
     'L0_attn_g2': (1.0, 0.2),
     'L0_attn_beta2': (0.0, 0.1),
     'L0_attn_b1': (0.0, 0.8),
     'L0_attn_bm': (0.0, 0.8),
     'L0_attn_bqo': (0.0, 0.336),
     'L0_attn_b2': (0.0, 0.1)}
    factors = {'L0_attn_Wq': 8.0,
     'L0_attn_Wk': 8.0,
     'L0_attn_Wv': 8.0,
     'L0_attn_Wc2q': 8.0,
     'L0_attn_Wo': 5.38,
     'L0_attn_W1': 8.0,
     'L0_attn_Wm': 8.0,
     'L0_attn_Wqo': 8.0,
     'L0_attn_W2': 2.68}
    for name, (base, spread) in spreads.items():
        noise = np.random.default_rng([zlib.crc32(name.encode()), seed]).standard_normal(out[name].shape)
        drawn = base * np.exp(spread * noise) if base else spread * noise
        out[name] = jnp.asarray(drawn.astype(out[name].dtype))
    for name, factor in factors.items():
        out[name] = (out[name] * factor).astype(out[name].dtype)
    return out
```

```python
import math
from contextlib import ExitStack

import numpy as np

import concourse.bass as bass
from concourse import mybir

F32 = mybir.dt.float32
BF16 = mybir.dt.bfloat16
I32 = mybir.dt.int32
U8 = mybir.dt.uint8
U32 = mybir.dt.uint32
ALU = mybir.AluOpType
ACT = mybir.ActivationFunctionType
X = mybir.AxisListType.X
XY = mybir.AxisListType.XY

B, S, D = 8, 128, 128
NH, HD, NQ = 8, 16, 8
FF = 512
NE, DFF = 16, 512
TOK = B * S
CAP = math.floor(1.25 * TOK / NE)
CAP = max(CAP + CAP % 2, 4)
SLOTS = NE * CAP
SC = SLOTS // 128
CW = 96
HALF = 4
HC = HALF * S
NHALF = B // HALF
HG = 4
GROUPS = B * NH // HG
LN_EPS = 1e-05
COS_EPS = 1e-08
PI_IN = float(np.float32(math.pi * (1 - 2.0 ** -21)))
ROUND = 12582912.0


def decoder_block(nc, x, ctx_in, mask, Wq, bq, Wk, bk, Wv, bv, Wc, bc, Wo, bo, g1, beta1, g2, beta2,
                  W1, b1, Wm, bm, Wqo, bqo, W2, b2, gate_w, w1, w2, out):
    st = ExitStack()
    with st:
        def sb(name, shape, dt=F32):
            return st.enter_context(nc.sbuf_tensor(name, shape, dt))

        def sem(name):
            return st.enter_context(nc.semaphore(name))

        xs = sb("xs", [128, B, D])
        cx = sb("cx", [128, B, D])
        mk = sb("mk", [128, B, S])
        mlow = sb("mlow", [128, B, S], U8)
        xn = sb("xn", [128, B, D])
        tT = sb("tT", [128, B, S])
        qT = sb("qT", [128, B, S])
        kT = sb("kT", [128, B, S])
        qTb = sb("qTb", [128, B, S], BF16)
        kTb = sb("kTb", [128, 2, B, S], BF16)
        qh = sb("qh", [128, B, S])
        kh = sb("kh", [128, B, S])
        cxT = kh
        va = sb("va", [128, B, NH, 32])
        md = sb("md", [128, 3 * HALF * NH * S])
        G = sb("G", [128, B, NH, S])
        w1s = sb("w1s", [128, NE, DFF])
        w2s = sb("w2s", [128, NE, DFF // 128, D])

        def group(k):
            return G[:, k // 2, HG * (k % 2):HG * (k % 2) + HG, :].rearrange("p n s -> p (n s)")

        def slot(i):
            return md[:, i * HALF * NH * S:(i + 1) * HALF * NH * S]

        def heads(i):
            return slot(i).rearrange("p (b n s) -> p b n s", b=HALF, n=NH)
        cosm = [heads(0), heads(1)]
        dotm = [heads(2), heads(0)]
        early = slot(2).rearrange("p (a b c) -> p a b c", a=4, b=B)
        qk, sq, qpad, kpad = (early[:, i] for i in range(4))
        late = slot(1).rearrange("p (a b c) -> p a b c", a=4, b=B)
        y1, x1, lg_, pT = (late[:, i] for i in range(4))

        wq, wk, wv, wqk, bqkr, bvr = (G[:, B - 3, i, :] for i in range(6))
        wqT = G[:, B - 3, 6:8, :]
        gw = G[0:NE, B - 4, 0, :]
        wc = sb("wc", [128, 64])
        bcr = G[:, 3, 3, 0:64]
        bcols = sb("bcols", [128, 4])
        bor = sb("bor", [128, 128])
        g1r = sb("g1r", [128, 128]); be1r = sb("be1r", [128, 128])
        g2r = sb("g2r", [128, 128]); be2r = sb("be2r", [128, 128])
        wo = sb("wo", [128, 128])
        fw1, fwqo = G[:, B - 2, 0:4, :].rearrange("p n s -> p (n s)"), G[0:NQ, B - 1, 0:4, :].rearrange("p n s -> p (n s)")
        fw1T, fw2 = G[:, B - 2, 4:8, :], G[:, B - 1, 4:8, :]
        fwm = sb("fwm", [128, 4, NQ]); fb1 = sb("fb1", [128, 4]); fbm = sb("fbm", [NQ, 2])
        fwqoT = sb("fwqoT", [128, NQ + 1, 4])
        w1m = sb("w1m", [128, NQ])
        w2f = sb("w2f", [128, 128])
        fb2 = sb("fb2", [NQ + 1, 128])
        gwT = sb("gwT", [128, NE])
        ident = sb("ident", [128, 128]); zero = w2f
        tri = sb("tri", [128, 128], BF16); onesb = sb("onesb", [128, 128], BF16)
        hm = sb("hm", [128, 2, NH])
        evod = sb("evod", [128, 2])
        diag = sb("diag", [32, NH])
        negsel = sb("negsel", [32, HALF, 128], BF16)
        revi = sb("revi", [128, NE])
        trash = sb("trash", [128, B])
        half_pi = sb("half_pi", [128, 1])
        mhalf = sb("mhalf", [128, 8])

        bns = sb("bns", [128, B, 6]); mv = sb("mv", [128, 5, B, 2])
        ve = sb("ve", [128, 5, B]); rstd = sb("rstd", [128, 5, B])
        nr = G[:, 3, 0:3, :].rearrange("p a s -> p (a s)").rearrange("p (i b c) -> p i b c", i=6, b=HALF)
        nrm = sb("nrm", [128, B, 16])
        mx = sb("mx", [128, B, NH])
        bd = kTb[0:32].rearrange("p a b s -> p (a b s)").rearrange("p (h n s) -> p h n s", h=NHALF, n=NH)
        ob = qh[:, 0:4, :].rearrange("p (r g) s -> p r g s", r=2)
        at, atT = qh[:, 4:6, :], qh[:, 6:8, :]
        rec = sb("rec", [128, 2, NH])
        qe = sb("qe", [128, HC])
        ffs = slot(2)[0:NQ, 0:5 * HC].rearrange("p (i c) -> p i c", i=5)
        ngm = sb("ngm", [128, B]); sume = sb("sume", [128, B]); rsum = sb("rsum", [128, B])
        okr = sb("okr", [128, B])
        ohb = sb("ohb", [128, B, NE], BF16)
        r1 = sb("r1", [128, 8, B]); si = sb("si", [128, 2, B], U32)

        least = sb("least", [128, 2]); least2 = sb("least2", [1, 4]); small = sb("small", [1, 1], I32)
        redo = slot(1).rearrange("p (i c) -> p i c", i=8)
        masked, scaled, fval = redo[:, 0], redo[:, 1], redo[:, 2]
        kn, an = redo[0:NH, 3, 0:128], redo[0:NH, 4]

        Gf = G[:].rearrange("p b n s -> p (b n s)")
        xd = Gf[:, 0:SC * 128].rearrange("p (c d) -> p c d", c=SC)
        xdT = Gf[:, 1280:1280 + SLOTS + 128]
        hT = Gf[:, 2688:2688 + 3 * 4 * CAP].rearrange("p (r c k) -> p r c k", r=3, c=4)
        eo = Gf[:, 3648:3648 + NE * 128].rearrange("p (e d) -> p e d", e=NE)
        got = Gf[:, 5696:5696 + B * D].rearrange("p (b d) -> p b d", b=B)
        rt = Gf[:, 6720:6720 + 4 * B * NE].rearrange("p (i b e) -> p i b e", i=4, b=B)
        res = Gf[:, 0:B * D].rearrange("p (b d) -> p b d", b=B)

        ps = [st.enter_context(nc.psum_tensor(f"bank{i}", [128, 512], F32)) for i in range(8)]

        def quads(i):
            return ps[i][:].rearrange("p (b s) -> p b s", b=4)

        toks = nc.dram_tensor("slot_tokens", [SLOTS + TOK, D], F32, kind="Internal")
        outs = nc.dram_tensor("slot_outputs", [SLOTS + 1, D], F32, kind="Internal")
        toks, outs = toks.ap(), outs.ap()

        names = """l_x l_qkv l_wc l_bias l_rows l_wo l_ffw l_ctx l_mask l_gate l_w1 l_w2 l_b2 zrow
            c_ident c_pool c_mask c_pad ve_done rstd_done pool_step
            xn_done tT_ps tT_sb wT_ps wT_sb wc_ps wc_sb
            qk_ps qk_sb proj_ps q_sb k_sb v_ps v_sb lowp pad_done hT_ps hT_sb cosm0 cosm1 dotm0 dotm1
            cos_ps sin_sb cos_g max_ps max_sb mT_ps bd_sb
            dot_ps arg_sb exp_sb o_ps o_sb oT_ps at_sb atT_ps atT_sb y_ps y_sb xb_done
            ln_st x1_sb x1T_ps x1T_sb qm_ps th_sb ra_sb cos_sb qe_sb ff_ps y2_sb x2_sb xn3_sb x3T_ps x3T_sb
            lg_ps lg_sb ex_sb pT_ps pT_sb pv_ps x3_sb xn4_sb x4T_ps x4T_sb gt_ps gt_sb
            fw_ps fw_sb fu_ps fu_sb ctxT_ps ctxT_sb
            rx_sb re_sb oh_sb rk_ps si_sb sent back xdT_ps xdT_sb hid_ps hid_sb eo_ps eo_sb eo_out
            got_in res_sb stored dch ach
            least_sb least_ps small_known small_ops small_ps small_f small_sin small_g""".split()
        s = {n: sem(n) for n in names}

        block = st.enter_context(nc.Block())

        WITHIN = {12: [0], 13: [1], 14: [2], 15: [3, 4]}
        TAIL = [(0, 1), (5, 0), (1, 1), (6, 0), (2, 1), (7, 0), (3, 1), (8, 0), (4, 1), (9, 0), (5, 1), (10, 0)] \
            + [(j, 1) for j in range(6, 11)]
        NORM_OF_STEP = {0: 1, 4: 2, 5: 3, 8: 4}
        NORMS = [(0, h) for h in range(NHALF)] + [(NORM_OF_STEP[j], h) for j, h in
                 [(j, 0) for js in WITHIN.values() for j in js] + TAIL if j in NORM_OF_STEP]

        def norm_count(i, h):
            return NORMS.index((i, h)) + 1

        BK = [(6, 7), (2, 3)]

        @block.sync
        def _(sp):
            for h in range(NHALF):
                hb = slice(h * HALF, (h + 1) * HALF)
                sp.dma_start(xs[:, hb, :], x[hb].rearrange("b s d -> s b d")).then_inc(s["l_x"], 16)
            for dst, src in ((wq, Wq), (wk, Wk), (wv, Wv)):
                sp.dma_start(dst[:].rearrange("p (n d) -> p n d", n=NH),
                             src.rearrange("n h d -> h n d")).then_inc(s["l_qkv"], 16)
            sp.dma_start(cx[:], ctx_in.rearrange("b t d -> t b d")).then_inc(s["l_ctx"], 16)
            sp.dma_start(wo[:], Wo).then_inc(s["l_wo"], 16)
            sp.dma_start(mk[:], mask.rearrange("b s t -> s b t")).then_inc(s["l_mask"], 16)
            for e in range(0, NE, 4):
                sp.dma_start(w1s[:, e:e + 4, :], w1[e:e + 4].rearrange("e d f -> d e f")).then_inc(s["l_w1"], 16)
                sp.dma_start(w2s[:, e:e + 4], w2[e:e + 4].rearrange("e (c p) d -> p e c d", p=128)).then_inc(s["l_w2"], 16)
            for e in range(0, NE, 4):
                sp.wait_ge(s["eo_sb"], e // 4 + 1)
                sp.dma_start(outs[e * CAP:(e + 4) * CAP, :].rearrange("(e c) d -> c e d", e=4),
                             eo[0:CAP, e:e + 4, :]).then_inc(s["eo_out"], 16)
            for b in range(B):
                sp.wait_ge(s["res_sb"], b + 1)
                sp.dma_start(out[b], res[:, b, :]).then_inc(s["stored"], 16)
            sp.wait_ge(s["stored"], 16 * B)

        def row(v):
            return v.rearrange("(a n) -> a n", a=1)

        @block.gpsimd
        def _(pool):
            g = nc.gpsimd
            chain = [0]

            def link(ins):
                chain[0] += 1
                ins.then_inc(s["pool_step"], 1)
                pool.wait_ge(s["pool_step"], chain[0])

            g.memset(ident[:], 0.0)
            g.memset(zero[:], 0.0)
            g.memset(mhalf[:], -0.5)
            g.memset(half_pi[:], math.pi / 2)
            g.memset(fb2[:], 0.0)
            link(g.memset(wc[:], 0.0))
            g.affine_select(out=ident[:], in_=ident[:], compare_op=ALU.not_equal, fill=1.0, base=0,
                            pattern=[[-1, 128]], channel_multiplier=1).then_inc(s["c_ident"], 1)
            pool.wait_ge(s["c_ident"], 1)
            pool.dma_start(toks[0:SLOTS, :].rearrange("(c p) d -> p c d", p=128),
                           zero[:].unsqueeze(1).broadcast_to([128, SC, D])).then_inc(s["zrow"], 16)
            pool.dma_start(outs[SLOTS:SLOTS + 1, :], zero[0:1, :]).then_inc(s["zrow"], 16)
            for n in range(NH):
                pool.dma_start(wc[n * HD:(n + 1) * HD, n * NQ:(n + 1) * NQ], Wc[n]).then_inc(s["l_wc"], 16)
            pool.dma_start(fb2[NQ:NQ + 1, :], row(b2)).then_inc(s["l_b2"], 16)
            g.memset(hm[:], 1.0)
            g.memset(evod[:], 1.0)
            g.memset(diag[:], 1.0)
            g.memset(negsel[:], -1.0)
            g.memset(tri[:], 1.0)
            g.memset(onesb[:], 1.0)
            g.memset(qpad, 0.0)
            g.memset(kpad, 0.0).then_inc(s["c_pad"], 1)
            g.memset(va[:], 0.0)
            link(g.memset(qe[:], 0.0))
            for j, wdt in ((0, HD), (1, NQ)):
                link(g.affine_select(out=hm[:, j, :], in_=hm[:, j, :], compare_op=ALU.is_ge, fill=0.0, base=0,
                                     pattern=[[-wdt, NH]], channel_multiplier=1))
                link(g.affine_select(out=hm[:, j, :], in_=hm[:, j, :], compare_op=ALU.is_ge, fill=0.0,
                                     base=wdt - 1, pattern=[[wdt, NH]], channel_multiplier=-1))
            g.memset(va[:, :, :, HD:HD + 1], 1.0).then_inc(s["c_pool"], 1)
            link(g.tensor_tensor(evod[:, 0:1], hm[:, 0, 0:1], hm[:, 0, 2:3], ALU.add))
            link(g.tensor_tensor(evod[:, 0:1], evod[:, 0:1], hm[:, 0, 4:5], ALU.add))
            link(g.tensor_tensor(evod[:, 0:1], evod[:, 0:1], hm[:, 0, 6:7], ALU.add))
            link(g.tensor_scalar(evod[:, 1:2], evod[:, 0:1], -1.0, 1.0, ALU.mult, ALU.add))
            link(g.memset(diag[:], 0.0))
            for b in range(HALF):
                link(g.affine_select(out=diag[:], in_=diag[:], compare_op=ALU.not_equal, fill=1.0, base=-b * NH,
                                     pattern=[[-1, NH]], channel_multiplier=1))
            link(g.affine_select(out=negsel[:], in_=negsel[:], compare_op=ALU.is_ge, fill=0.0, base=0,
                                 pattern=[[-NH, HALF], [0, 128]], channel_multiplier=1))
            link(g.affine_select(out=negsel[:], in_=negsel[:], compare_op=ALU.is_ge, fill=0.0, base=NH - 1,
                                 pattern=[[NH, HALF], [0, 128]], channel_multiplier=-1))
            g.affine_select(out=tri[:], in_=tri[:], compare_op=ALU.is_ge, fill=0.0, base=0,
                            pattern=[[1, 128]], channel_multiplier=-1)
            g.iota(revi[:], [[-1, NE]], base=NE, channel_multiplier=0, allow_small_or_imprecise_dtypes=True)
            g.iota(trash[:], [[S, B]], base=SLOTS, channel_multiplier=1, allow_small_or_imprecise_dtypes=True)
            link(g.affine_select(out=qe[:], in_=qe[:], compare_op=ALU.not_equal, fill=1.0, base=-NQ,
                                 pattern=[[0, HC]], channel_multiplier=1))
            g.memset(kTb[0:1, 0, 0, 0:1], 0.0).then_inc(s["c_mask"], 1)

            def rsqrt(i, h):
                hb = slice(h * HALF, (h + 1) * HALF)
                pool.wait_ge(s["ln_st"], norm_count(i, h))
                link(g.tensor_scalar(ve[:, i, hb], mv[:, i, hb, 1], LN_EPS, 1.0, ALU.add, ALU.mult))
                g.tensor_tensor(rstd[:, i, hb], ve[:, i, hb], mhalf[:, 0:HALF], ALU.pow).then_inc(s["rstd_done"], 1)

            for h in range(NHALF):
                rsqrt(0, h)
            for h in range(NHALF):
                hb = slice(h * HALF, (h + 1) * HALF)
                pool.wait_ge(s["q_sb"], h + 1)
                g.tensor_scalar(qTb[:, hb, :], qT[:, hb, :], 1.0, 1.0, ALU.mult, ALU.mult).then_inc(s["lowp"], 1)
                pool.wait_ge(s["k_sb"], h + 1)
                for j in range(2):
                    g.tensor_scalar(kTb[:, j, hb, :], kT[:, hb, :], evod[:, j:j + 1], 1.0,
                                    ALU.mult, ALU.mult).then_inc(s["lowp"], 1)
            pool.wait_ge(s["hT_sb"], 2 * NHALF)
            for n in range(NH):
                g.tensor_scalar(cosm[1][:, :, n, :], qh[:, HALF:B, :], hm[:, 1, n:n + 1], 1.0,
                                ALU.mult, ALU.mult).then_inc(s["cosm1"], 1)
            pool.wait_ge(s["cos_ps"], GROUPS // NHALF)
            for n in range(NH):
                g.tensor_scalar(dotm[1][:, :, n, :], qT[:, HALF:B, :], hm[:, 0, n:n + 1], 1.0,
                                ALU.mult, ALU.mult).then_inc(s["dotm1"], 1)
            pool.wait_ge(s["l_rows"], 16 * 6)
            pool.wait_ge(s["tT_ps"], 2)
            pool.wait_ge(s["ln_st"], 2)
            for b in range(B):
                g.tensor_tensor(xs[:, b, :], xs[:, b, :], be2r[:], ALU.add)
                last = g.tensor_tensor(xn[:, b, :], xn[:, b, :], bor[:], ALU.add)
            last.then_inc(s["xb_done"], 1)
            for i, h in NORMS[NHALF:]:
                rsqrt(i, h)
            pool.wait_ge(s["zrow"], 32)
            pool.wait_ge(s["si_sb"], 1)
            for b in range(B):
                g.indirect_dma_start(toks, bass.IndirectOffsetOnAxis(ap=si[:, 0, b:b + 1], axis=0),
                                     xn[:, b, :], None).then_inc(s["sent"], 16)
            pool.wait_ge(s["sent"], 16 * B)
            pool.dma_start(xd, toks[0:SLOTS, :].rearrange("(c p) d -> p c d", p=128)).then_inc(s["back"], 16)
            pool.wait_ge(s["eo_out"], 16 * NE // 4)
            for b in range(B):
                g.indirect_dma_start(got[:, b, :], None, outs,
                                     bass.IndirectOffsetOnAxis(ap=si[:, 1, b:b + 1], axis=0)).then_inc(s["got_in"], 16)

        def out_evac(act, a, b):
            act.wait_ge(s["o_ps"], b + 1)
            if b >= 2:
                act.wait_ge(s["oT_ps"], b - 1)
            a.activation(ob[:, b % 2].rearrange("p g s -> p (g s)"), ps[2 + b % 2][:, 0:256], ACT.Copy).then_inc(s["o_sb"], 1)

        def att_evac(act, a, b):
            act.wait_ge(s["atT_ps"], b + 1)
            if b >= 2:
                act.wait_ge(s["y_ps"], b - 1)
            a.activation(atT[:, b % 2, :], ps[4 + b % 2][:, 256:384], ACT.Copy).then_inc(s["atT_sb"], 1)

        @block.scalar
        def _(act):
            a = nc.scalar
            act.dma_start(bcols[:, 0:1], bq.rearrange("n d -> (n d)").rearrange("(p a) -> p a", a=1)).then_inc(s["l_bias"], 16)
            act.dma_start(bcols[:, 1:2], bk.rearrange("n d -> (n d)").rearrange("(p a) -> p a", a=1)).then_inc(s["l_bias"], 16)
            act.dma_start(bcr, row(bc.rearrange("n q -> (n q)")).broadcast_to([128, 64])).then_inc(s["l_bias"], 16)
            for dst, src in ((bvr, bv.rearrange("n d -> (n d)")), (bor, bo), (g1r, g1), (be1r, beta1), (g2r, g2), (be2r, beta2)):
                act.dma_start(dst[:], row(src).broadcast_to([128, 128])).then_inc(s["l_rows"], 16)
            act.dma_start(fw1, W1).then_inc(s["l_ffw"], 16)
            act.dma_start(fwm[:], Wm.rearrange("(p c) q -> p c q", c=4)).then_inc(s["l_ffw"], 16)
            act.dma_start(fb1[:], b1.rearrange("(p c) -> p c", c=4)).then_inc(s["l_ffw"], 16)
            act.dma_start(fbm[:, 0:1], bm.rearrange("(p a) -> p a", a=1)).then_inc(s["l_ffw"], 16)
            act.dma_start(fwqo, Wqo).then_inc(s["l_ffw"], 16)
            act.dma_start(fwqoT[:, NQ, :], bqo.rearrange("(p c) -> p c", c=4)).then_inc(s["l_ffw"], 16)
            act.dma_start(fw2, W2.rearrange("(p c) d -> p c d", c=4)).then_inc(s["l_ffw"], 16)
            act.dma_start(gw, gate_w).then_inc(s["l_gate"], 16)

            chain = [0]

            def link(ins):
                chain[0] += 1
                ins.then_inc(s["ach"], 1)
                act.wait_ge(s["ach"], chain[0])

            act.wait_ge(s["wT_ps"], 1)
            a.activation(wqT.rearrange("p a b -> p (a b)"), ps[4][:, 0:256], ACT.Copy).then_inc(s["wT_sb"], 1)
            act.wait_ge(s["wc_ps"], 1)
            a.activation(wqk, ps[5][:, 0:128], ACT.Copy).then_inc(s["wc_sb"], 1)
            act.wait_ge(s["l_bias"], 48)
            link(a.activation(bcols[:, 2:3], bcols[:, 0:1], ACT.Copy, scale=0.125))
            for h in range(NHALF):
                hb = slice(h * HALF, (h + 1) * HALF)
                act.wait_ge(s["tT_ps"], h + 1)
                a.activation(tT[:, hb, :], quads(2 + h), ACT.Copy).then_inc(s["tT_sb"], 1)
                act.wait_ge(s["proj_ps"], 2 * h + 1)
                a.activation(qT[:, hb, :], quads(6), ACT.Identity, bias=bcols[:, 2:3], scale=0.125).then_inc(s["q_sb"], 1)
                act.wait_ge(s["proj_ps"], 2 * h + 2)
                a.activation(kT[:, hb, :], quads(7), ACT.Identity, bias=bcols[:, 1:2]).then_inc(s["k_sb"], 1)
            def unit_evac(h):
                for j, dst in enumerate((qh, kh)):
                    act.wait_ge(s["hT_ps"], 2 * h + j + 1)
                    a.activation(dst[:, h * HALF:(h + 1) * HALF, :], quads(6 * h + j), ACT.Copy).then_inc(s["hT_sb"], 1)

            unit_evac(0)
            a.preload_act_table(ACT.Sin)
            for k in range(GROUPS):
                act.wait_ge(s["cos_ps"], k + 1)
                if k == 12:
                    act.wait_ge(s["fu_ps"], 2)
                a.activation(group(k), ps[k % 2][:], ACT.Sin, scale=PI_IN).then_inc(s["sin_sb"], 1)
                if k == 1:
                    unit_evac(1)
                if k % 2 == 1:
                    n = k // 2
                    a.activation(dotm[0][:, :, n, :], qT[:, 0:HALF, :], ACT.Copy,
                                 scale=hm[:, 0, n:n + 1]).then_inc(s["dotm0"], 1)
                if k == 4:
                    act.wait_ge(s["fw_ps"], 1)
                    a.activation(fw1T.rearrange("p a b -> p (a b)"), ps[6][:], ACT.Copy).then_inc(s["fw_sb"], 1)
                if k == 6:
                    act.wait_ge(s["fw_ps"], 2)
                    a.activation(fwqoT[:, 0:NQ, :], ps[7][:, 0:32].rearrange("p (c q) -> p q c", c=4), ACT.Copy).then_inc(s["fw_sb"], 1)
                    a.activation(gwT[:], ps[7][:, 64:64 + NE], ACT.Copy).then_inc(s["fw_sb"], 1)
                if k == 8:
                    act.wait_ge(s["fu_ps"], 1)
                    a.activation(w1m[:], ps[6][:, 0:NQ], ACT.Copy).then_inc(s["fu_sb"], 1)
                    a.activation(fbm[:, 1:2], ps[6][0:NQ, 16:17], ACT.Identity, bias=fbm[:, 0:1]).then_inc(s["fu_sb"], 1)

            def step(j, h):
                hb = slice(h * HALF, (h + 1) * HALF)
                if j == 1:
                    act.wait_ge(s["x1T_ps"], h + 1)
                    a.activation(tT[:, hb, :], quads(BK[h][0]), ACT.Copy).then_inc(s["x1T_sb"], 1)
                if j == 2:
                    act.wait_ge(s["qm_ps"], h + 1)
                    if h:
                        act.wait_ge(s["qe_sb"], h)
                    a.activation(ffs[:, 0, :], ps[BK[h][1]][0:NQ, :], ACT.Tanh, bias=fbm[:, 1:2]).then_inc(s["th_sb"], 1)
                    act.wait_ge(s["ra_sb"], h + 1)
                    a.activation(ffs[:, 4, :], ffs[:, 3, :], ACT.Sin, bias=half_pi[0:NQ, :],
                                 scale=-math.pi / 4).then_inc(s["cos_sb"], 1)
                    a.preload_act_table(ACT.Exp)
                if j == 6:
                    act.wait_ge(s["x3T_ps"], h + 1)
                    a.activation(tT[:, hb, :], quads(BK[h][1]), ACT.Copy).then_inc(s["x3T_sb"], 1)
                if j == 7:
                    act.wait_ge(s["lg_sb"], h + 1)
                    for b in range(h * HALF, (h + 1) * HALF):
                        a.activation(lg_[:, b, :], lg_[:, b, :], ACT.Exp, bias=ngm[:, b:b + 1],
                                     accum_out=sume[:, b:b + 1]).then_inc(s["ex_sb"], 1)
                    act.wait_ge(s["pT_ps"], h + 1)
                    a.activation(pT[:, hb, :], quads(BK[h][1]), ACT.Copy).then_inc(s["pT_sb"], 1)
                if j == 9:
                    act.wait_ge(s["x4T_ps"], h + 1)
                    a.activation(tT[:, hb, :], quads(BK[h][1]), ACT.Copy).then_inc(s["x4T_sb"], 1)

            act.wait_ge(s["small_known"], 1)
            with a.If(a.value_load(small[0:1, 0:1]) > 0):
                for k in range(GROUPS):
                    act.wait_ge(s["small_f"], k + 1)
                    if k == 0:
                        act.wait_ge(s["cos_g"], GROUPS)
                    a.activation(group(k), fval, ACT.Sin, scale=PI_IN).then_inc(s["small_sin"], 1)
            a.preload_act_table(ACT.Exp)
            for k in range(GROUPS):
                if k in (2, 4):
                    h = k // 2 - 1
                    act.wait_ge(s["ctxT_ps"], h + 1)
                    a.activation(cxT[:, h * HALF:(h + 1) * HALF, :], quads(6 + h), ACT.Copy).then_inc(s["ctxT_sb"], 1)
                act.wait_ge(s["arg_sb"], k + 1)
                a.activation(group(k), group(k), ACT.Exp).then_inc(s["exp_sb"], 1)
                if k >= 3 and k % 2 == 1:
                    out_evac(act, a, (k - 3) // 2)
                if k >= 5 and k % 2 == 1:
                    att_evac(act, a, (k - 5) // 2)
                for j in WITHIN.get(k, ()):
                    step(j, 0)
            out_evac(act, a, B - 1)
            att_evac(act, a, B - 2)
            att_evac(act, a, B - 1)
            for j, h in TAIL:
                step(j, h)
            act.wait_ge(s["rx_sb"], 1)
            a.activation(rt[:, 1], rt[:, 0], ACT.Exp).then_inc(s["re_sb"], 1)
            a.preload_act_table(ACT.Gelu_apprx_tanh)
            for c in range(3):
                act.wait_ge(s["xdT_ps"], c + 1)
                w = min(512, SLOTS - 512 * c)
                a.activation(xdT[:, 512 * c:512 * c + w], ps[2 + c][:, 0:w], ACT.Copy).then_inc(s["xdT_sb"], 1)
            for e in range(NE):
                act.wait_ge(s["hid_ps"], e + 1)
                if e >= 3:
                    act.wait_ge(s["eo_ps"], e - 2)
                a.activation(hT[:, e % 3], ps[5 + e % 3][:, 0:4 * CW].rearrange("p (c k) -> p c k", c=4)[:, :, 0:CAP],
                             ACT.Gelu_apprx_tanh).then_inc(s["hid_sb"], 1)

        @block.vector
        def _(dve):
            v = nc.vector
            chain = [0]

            def link(ins):
                chain[0] += 1
                ins.then_inc(s["dch"], 1)
                dve.wait_ge(s["dch"], chain[0])

            def stats(i, src, h):
                for b in range(h * HALF, (h + 1) * HALF):
                    last = v.bn_stats(bns[:, b, :], src[:, b, :])
                link(last)
                for b in range(h * HALF, (h + 1) * HALF):
                    last = v.bn_aggr(mv[:, i, b, :], bns[:, b, :])
                last.then_inc(s["ln_st"], 1)

            def rstd_wait(i, h):
                dve.wait_ge(s["rstd_done"], norm_count(i, h))

            for h in range(NHALF):
                dve.wait_ge(s["l_x"], 32)
                stats(0, xs, h)
            dve.wait_ge(s["wc_ps"], 2)
            dve.wait_ge(s["l_bias"], 48)
            bps = ps[5][:, 128:256].rearrange("p (a q) -> p a q", a=2)
            v.tensor_tensor(bqkr.rearrange("p (a q) -> p a q", a=2), bps,
                            bcr.unsqueeze(1).broadcast_to([128, 2, 64]), ALU.add).then_inc(s["wc_sb"], 1)
            for h in range(NHALF):
                rstd_wait(0, h)
                for b in range(h * HALF, (h + 1) * HALF):
                    v.tensor_scalar(xn[:, b, :], xs[:, b, :], mv[:, 0, b, 0:1], rstd[:, 0, b:b + 1],
                                    ALU.subtract, ALU.mult).then_inc(s["xn_done"], 1)

            def norms(h):
                hb = slice(h * HALF, (h + 1) * HALF)
                dve.wait_ge(s["qk_ps"], h + 1)
                if h == 0:
                    dve.wait_ge(s["c_pad"], 1)
                link(v.tensor_tensor(qk[:, hb, :], quads(4 + h), bqkr.unsqueeze(1).broadcast_to([128, HALF, 128]), ALU.add))
                link(v.tensor_tensor(sq[:, hb, :], qk[:, hb, :], qk[:, hb, :], ALU.mult))
                ss, half_i, y, t0, t1, y2 = (nr[:, i] for i in range(6))
                link(v.tensor_reduce(t0, sq[:, hb, :].rearrange("p b (n q) -> p b n q", q=NQ), X, ALU.add))
                link(v.tensor_scalar(ss, t0, 1e-30, None, ALU.max))
                link(v.tensor_scalar(half_i.bitcast(I32), ss.bitcast(I32), 1, None, ALU.logical_shift_right))
                link(v.tensor_scalar(y.bitcast(I32), half_i.bitcast(I32), -1.0, 1597463007.0, ALU.mult, ALU.add))
                for _ in range(3):
                    link(v.scalar_tensor_tensor(t0, y, -0.5, y, ALU.mult, ALU.mult))
                    link(v.tensor_tensor(t1, t0, ss, ALU.mult))
                    link(v.scalar_tensor_tensor(y, t1, 1.5, y, ALU.add, ALU.mult))
                v.tensor_tensor(nrm[:, hb, :], ss, y, ALU.mult)
                for j, dst in enumerate((qpad, kpad)):
                    v.tensor_tensor(dst[:, hb, 0:64].rearrange("p b (n q) -> p b n q", q=NQ),
                                    qk[:, hb, 64 * j:64 * j + 64].rearrange("p b (n q) -> p b n q", q=NQ),
                                    y[:, :, 8 * j:8 * j + 8].unsqueeze(3).broadcast_to([128, HALF, NH, NQ]),
                                    ALU.mult).then_inc(s["pad_done"], 1)

            norms(0)
            dve.wait_ge(s["c_pool"], 1)
            dve.wait_ge(s["l_rows"], 16 * 6)
            for h in range(NHALF):
                hb = slice(h * HALF, (h + 1) * HALF)
                dve.wait_ge(s["v_ps"], h + 1)
                for b in range(h * HALF, (h + 1) * HALF):
                    last = v.tensor_tensor(va[:, b, :, 0:HD],
                                           ps[2 + h][:, (b % 4) * 128:(b % 4) * 128 + 128].rearrange("p (n d) -> p n d", d=HD),
                                           bvr.rearrange("p (n d) -> p n d", d=HD), ALU.add)
                last.then_inc(s["v_sb"], 1)
                if h == 0:
                    dve.wait_ge(s["c_mask"], 1)
                    dve.wait_ge(s["hT_sb"], 1)
                    for n in range(NH):
                        v.tensor_scalar(cosm[0][:, :, n, :], qh[:, 0:HALF, :], hm[:, 1, n:n + 1], None,
                                        ALU.mult).then_inc(s["cosm0"], 1)
                    norms(1)

            for k in range(GROUPS):
                dve.wait_ge(s["sin_sb"], k + 1)
                v.scalar_tensor_tensor(group(k), group(k), 10.0, ps[k % 2][:],
                                       ALU.add, ALU.mult).then_inc(s["cos_g"], 1)
                pr, i = divmod(k, 4)
                dve.wait_ge(s["max_ps"], k + 1)
                v.tensor_reduce(mx[:, 2 * pr:2 * pr + 2, 2 * i:2 * i + 2],
                                ps[2 + i][:].rearrange("p (b n t) -> p b n t", b=2, n=2), X, ALU.max).then_inc(s["max_sb"], 1)
                if k == 3:
                    for j in range(2):
                        last = v.tensor_reduce(least[:, j:j + 1], nrm[:, :, 8 * j:8 * j + 8], XY, ALU.min)
                    last.then_inc(s["least_sb"], 1)
                if k == 7:
                    dve.wait_ge(s["least_ps"], 1)
                    dve.wait_ge(s["fw_sb"], 3)
                    link(v.tensor_reduce(least2[:, 0:2], ps[7][0:1, 256:512].rearrange("p (a t) -> p a t", a=2), X, ALU.min))
                    link(v.tensor_tensor(least2[:, 2:3], least2[:, 0:1], least2[:, 1:2], ALU.mult))
                    v.tensor_scalar(small[:], least2[:, 2:3], COS_EPS, None, ALU.is_lt).then_inc(s["small_known"], 1)
                if k == 10:
                    dve.wait_ge(s["fu_ps"], 2)
                    dve.wait_ge(s["l_b2"], 16)
                    dve.wait_ge(s["zrow"], 32)
                    v.tensor_tensor(w2f[0:NQ + 1, :], ps[7][0:NQ + 1, 128:256], fb2[0:NQ + 1, :], ALU.add).then_inc(s["fu_sb"], 1)
                if k == 3:
                    dve.wait_ge(s["l_mask"], 16)
                    link(v.tensor_scalar(mlow[:], mk[:], -1.0, None, ALU.is_lt))

            def guarded(k):
                b, gi = divmod(k, 2)
                hs = slice(HG * gi, HG * gi + HG)
                if k:
                    dve.wait_ge(s["small_ps"], 2 * k)
                for i in range(HG):
                    v.tensor_scalar(masked[:, i * 128:(i + 1) * 128], qh[:, b, :], hm[:, 1, HG * gi + i:HG * gi + i + 1], None,
                                    ALU.mult)
                dve.wait_ge(s["small_ps"], 2 * k + 1)
                v.tensor_copy(kn, ps[6][0:NH, 128:256])
                v.tensor_tensor(an.rearrange("p (n s) -> p n s", n=HG),
                                ps[6][0:NH, 0:128].unsqueeze(1).broadcast_to([NH, HG, S]),
                                diag[0:NH, hs].unsqueeze(2).broadcast_to([NH, HG, S]), ALU.mult).then_inc(s["small_ops"], 1)
                dve.wait_ge(s["small_ps"], 2 * k + 2)
                g_count[0] += 1
                v.tensor_scalar(scaled, ps[1][:], 1.0 / COS_EPS, 1.0, ALU.mult, ALU.min).then_inc(s["small_g"], 1)
                dve.wait_ge(s["small_g"], g_count[0])
                v.tensor_tensor(fval, ps[0][:], scaled, ALU.mult).then_inc(s["small_f"], 1)
                dve.wait_ge(s["small_sin"], k + 1)
                g_count[0] += 1
                v.scalar_tensor_tensor(group(k), group(k), 10.0, fval, ALU.add, ALU.mult).then_inc(s["small_g"], 1)
                dve.wait_ge(s["small_g"], g_count[0])

            g_count = [0]
            with v.If(v.value_load(small[0:1, 0:1]) > 0):
                for k in range(GROUPS):
                    guarded(k)
            for h in range(NHALF):
                dve.wait_ge(s["mT_ps"], h + 1)
                v.tensor_tensor(bd[:, h], ps[6 + h][0:32, 0:128].unsqueeze(1).broadcast_to([32, NH, S]),
                                diag[:].unsqueeze(2).broadcast_to([32, NH, S]), ALU.mult).then_inc(s["bd_sb"], 1)

            def arg(k):
                dve.wait_ge(s["dot_ps"], k + 1)
                if k == 0:
                    dve.wait_ge(s["cos_g"], GROUPS)
                v.scalar_tensor_tensor(group(k), group(k), 0.05, ps[k % 2][:], ALU.mult, ALU.add).then_inc(s["arg_sb"], 1)

            def divide(b):
                dve.wait_ge(s["oT_ps"], b + 1)
                o = ps[4 + b % 2][:, 0:256].rearrange("p (n c) -> p n c", c=32)
                link(v.reciprocal(rec[:, b % 2, :], o[:, :, HD]))
                v.tensor_tensor(at[:, b % 2, :].rearrange("p (n d) -> p n d", d=HD), o[:, :, 0:HD],
                                rec[:, b % 2, :].unsqueeze(2).broadcast_to([128, NH, HD]), ALU.mult).then_inc(s["at_sb"], 1)

            def resid(b):
                dve.wait_ge(s["y_ps"], b + 1)
                if b == 0:
                    dve.wait_ge(s["xb_done"], 1)
                v.tensor_tensor(y1[:, b, :], ps[4 + b % 2][:, 384:512], xn[:, b, :], ALU.add).then_inc(s["y_sb"], 1)

            def step(j, h):
                hb = slice(h * HALF, (h + 1) * HALF)
                bs = range(h * HALF, (h + 1) * HALF)
                if j == 0:
                    dve.wait_ge(s["y_sb"], HALF * (h + 1))
                    stats(1, y1, h)
                if j == 1:
                    rstd_wait(1, h)
                    for b in bs:
                        last = v.scalar_tensor_tensor(y1[:, b, :], y1[:, b, :], mv[:, 1, b, 0:1], g1r[:], ALU.subtract, ALU.mult)
                    link(last)
                    for b in bs:
                        last = v.scalar_tensor_tensor(x1[:, b, :], y1[:, b, :], rstd[:, 1, b:b + 1], be1r[:], ALU.mult, ALU.add)
                    last.then_inc(s["x1_sb"], 1)
                if j == 2:
                    dve.wait_ge(s["th_sb"], h + 1)
                    qm, u, r = ffs[:, 1, :], ffs[:, 2, :], ffs[:, 3, :]
                    dve.wait_ge(s["fu_sb"], 3)
                    link(v.tensor_scalar(qm, ps[BK[h][1]][0:NQ, :], fbm[:, 1:2], None, ALU.add))
                    link(v.tensor_scalar(u, qm, 0.125, ROUND, ALU.mult, ALU.add))
                    link(v.tensor_scalar(u, u, ROUND, 8.0, ALU.subtract, ALU.mult))
                    link(v.tensor_tensor(r, qm, u, ALU.subtract))
                    link(v.tensor_scalar(u, r, -1.0, 4.0, ALU.mult, ALU.min))
                    link(v.tensor_tensor(r, r, u, ALU.max))
                    v.tensor_scalar(r, r, 4.0, None, ALU.min).then_inc(s["ra_sb"], 1)
                if j == 3:
                    dve.wait_ge(s["cos_sb"], h + 1)
                    if h:
                        dve.wait_ge(s["ff_ps"], h)
                    else:
                        dve.wait_ge(s["c_mask"], 1)
                    v.tensor_tensor(qe[0:NQ, :], ffs[:, 0, :], ffs[:, 4, :], ALU.mult).then_inc(s["qe_sb"], 1)
                if j == 4:
                    dve.wait_ge(s["ff_ps"], h + 1)
                    link(v.tensor_tensor(y1[:, hb, :], quads(BK[h][0]), x1[:, hb, :], ALU.add))
                    stats(2, y1, h)
                if j == 5:
                    rstd_wait(2, h)
                    for b in bs:
                        last = v.scalar_tensor_tensor(y1[:, b, :], y1[:, b, :], mv[:, 2, b, 0:1], g2r[:], ALU.subtract, ALU.mult)
                    link(last)
                    for b in bs:
                        last = v.scalar_tensor_tensor(xs[:, b, :], y1[:, b, :], rstd[:, 2, b:b + 1], xs[:, b, :], ALU.mult, ALU.add)
                    link(last)
                    stats(3, xs, h)
                if j == 6:
                    rstd_wait(3, h)
                    for b in bs:
                        last = v.tensor_scalar(x1[:, b, :], xs[:, b, :], mv[:, 3, b, 0:1], rstd[:, 3, b:b + 1],
                                               ALU.subtract, ALU.mult)
                    last.then_inc(s["xn3_sb"], 1)
                if j == 7:
                    dve.wait_ge(s["lg_ps"], h + 1)
                    link(v.tensor_scalar(lg_[:, hb, :], quads(BK[h][0]), 1.0 / math.sqrt(D), None, ALU.mult))
                    link(v.copy_predicated(lg_[:, hb, :], mlow[:, hb, :], mk[:, hb, :]))
                    v.tensor_reduce(ngm[:, hb], lg_[:, hb, :], X, ALU.max, negate=True).then_inc(s["lg_sb"], 1)
                    dve.wait_ge(s["ex_sb"], HALF * (h + 1))
                    v.reciprocal(rsum[:, hb], sume[:, hb])
                    link(v.tensor_tensor(okr[:, hb], sume[:, hb], sume[:, hb], ALU.is_equal))
                if j == 8:
                    dve.wait_ge(s["pv_ps"], h + 1)
                    for b in bs:
                        last = v.scalar_tensor_tensor(y1[:, b, :], ps[BK[h][0]][:, (b % 4) * 128:(b % 4) * 128 + 128],
                                                      rsum[:, b:b + 1], xs[:, b, :], ALU.mult, ALU.add)
                    link(last)
                    link(v.copy_predicated(xs[:, hb, :], okr[:, hb].bitcast(I32).unsqueeze(2).broadcast_to([128, HALF, D]), y1[:, hb, :]))
                    stats(4, xs, h)
                if j == 9:
                    rstd_wait(4, h)
                    for b in bs:
                        last = v.tensor_scalar(xn[:, b, :], xs[:, b, :], mv[:, 4, b, 0:1], rstd[:, 4, b:b + 1],
                                               ALU.subtract, ALU.mult)
                    last.then_inc(s["xn4_sb"], 1)
                if j == 10:
                    dve.wait_ge(s["gt_ps"], h + 1)
                    v.tensor_copy(rt[:, 2, hb, :], ps[BK[h][0]][:, 0:HALF * NE].rearrange("p (b e) -> p b e", b=HALF)).then_inc(s["gt_sb"], 1)

            for k in range(GROUPS):
                arg(k)
                if k >= 4 and k % 2 == 0:
                    divide((k - 4) // 2)
                if k >= 6 and k % 2 == 0:
                    resid((k - 6) // 2)
                for j in WITHIN.get(k, ()):
                    step(j, 0)
            divide(B - 2)
            resid(B - 3)
            divide(B - 1)
            resid(B - 2)
            resid(B - 1)
            for j, h in TAIL:
                step(j, h)

            lg = rt[:, 2]
            m8, sum8, p8, vm, rk, keep, sl, wgt = (r1[:, i] for i in range(8))

            def wide(a8):
                return a8.unsqueeze(2).broadcast_to([128, B, NE])
            dve.wait_ge(s["gt_sb"], NHALF)
            link(v.tensor_reduce(m8, lg, X, ALU.max))
            v.tensor_tensor(rt[:, 0], lg, wide(m8), ALU.subtract).then_inc(s["rx_sb"], 1)
            link(v.tensor_tensor(rt[:, 3], lg, wide(m8), ALU.is_ge))
            link(v.tensor_tensor(rt[:, 3], rt[:, 3], revi[:].unsqueeze(1).broadcast_to([128, B, NE]), ALU.mult))
            link(v.tensor_reduce(vm, rt[:, 3], X, ALU.max))
            link(v.tensor_tensor(rt[:, 3], rt[:, 3], wide(vm), ALU.is_equal))
            v.tensor_copy(ohb[:], rt[:, 3]).then_inc(s["oh_sb"], 1)
            dve.wait_ge(s["re_sb"], 1)
            link(v.tensor_reduce(sum8, rt[:, 1], X, ALU.add))
            link(v.reciprocal(p8, sum8))
            dve.wait_ge(s["rk_ps"], 1)
            link(v.tensor_tensor(rt[:, 3], ps[7][:, 0:128].rearrange("p (b e) -> p b e", b=B), rt[:, 3], ALU.mult))
            link(v.tensor_reduce(rk, rt[:, 3], X, ALU.add))
            link(v.tensor_scalar(keep, rk, float(CAP), None, ALU.is_le))
            v.tensor_tensor(wgt, p8, keep, ALU.mult)
            link(v.scalar_tensor_tensor(sl, vm, -float(CAP), rk, ALU.mult, ALU.add))
            link(v.tensor_scalar(sl, sl, float(NE * CAP - 1), None, ALU.add))
            link(v.tensor_tensor(m8, sl, trash[:], ALU.subtract))
            link(v.tensor_tensor(m8, m8, keep, ALU.mult))
            link(v.tensor_tensor(m8, m8, trash[:], ALU.add))
            v.tensor_copy(si[:, 0, :], m8)
            link(v.tensor_scalar(sl, m8, float(SLOTS), None, ALU.min))
            v.tensor_copy(si[:, 1, :], sl).then_inc(s["si_sb"], 1)
            dve.wait_ge(s["o_ps"], B)
            v.memset(xdT[:, SLOTS:SLOTS + CW - CAP], 0.0).then_inc(s["xdT_sb"], 1)
            for q in range(NE // 4):
                dve.wait_ge(s["eo_ps"], 4 * (q + 1))
                v.tensor_copy(eo[0:CAP, 4 * q:4 * q + 4, :],
                              ps[q % 2][0:CAP, :].rearrange("p (e d) -> p e d", e=4)).then_inc(s["eo_sb"], 1)
            dve.wait_ge(s["got_in"], 16 * B)
            for b in range(B):
                v.scalar_tensor_tensor(res[:, b, :], got[:, b, :], wgt[:, b:b + 1], xs[:, b, :],
                                       ALU.mult, ALU.add).then_inc(s["res_sb"], 1)

        @block.tensor
        def _(pe):
            t = nc.tensor

            def turn4(bank, src, h, done):
                for i in range(HALF):
                    last = t.transpose(ps[bank][:, i * 128:(i + 1) * 128], src[:, h * HALF + i, :], ident[:])
                last.then_inc(s[done], 1)

            pe.wait_ge(s["c_ident"], 1)
            pe.wait_ge(s["l_qkv"], 48)
            t.transpose(ps[4][:, 0:128], wq, ident[:])
            t.transpose(ps[4][:, 128:256], wk, ident[:]).then_inc(s["wT_ps"], 1)
            pe.wait_ge(s["wT_sb"], 1)
            pe.wait_ge(s["l_wc"], 16 * NH)
            for j in range(2):
                last = t.matmul(ps[5][:, 64 * j:64 * j + 64], wqT[:, j, :], wc[:], start=True, stop=True)
            last.then_inc(s["wc_ps"], 1)
            pe.wait_ge(s["l_bias"], 48)
            pe.wait_ge(s["wc_sb"], 1)
            for j in range(2):
                last = t.matmul(ps[5][:, 128 + 64 * j:192 + 64 * j], bcols[:, j:j + 1].broadcast_to([128, 128]), wc[:],
                                start=True, stop=True)
            last.then_inc(s["wc_ps"], 1)
            for h in range(NHALF):
                pe.wait_ge(s["xn_done"], HALF * (h + 1))
                turn4(2 + h, xn, h, "tT_ps")
            for h in range(NHALF):
                pe.wait_ge(s["tT_sb"], h + 1)
                pe.wait_ge(s["wc_sb"], 2)
                for i in range(HALF):
                    last = t.matmul(ps[4 + h][:, i * 128:(i + 1) * 128], tT[:, h * HALF + i, :], wqk, start=True, stop=True)
                last.then_inc(s["qk_ps"], 1)
                if h:
                    pe.wait_ge(s["q_sb"], h)
                tcols = tT[:, h * HALF:(h + 1) * HALF, :].rearrange("p b s -> p (b s)")
                t.matmul(ps[6][:], wq, tcols, start=True, stop=True).then_inc(s["proj_ps"], 1)
                if h:
                    pe.wait_ge(s["k_sb"], h)
                t.matmul(ps[7][:], wk, tcols, start=True, stop=True).then_inc(s["proj_ps"], 1)
                for i in range(HALF):
                    last = t.matmul(ps[2 + h][:, i * 128:(i + 1) * 128], tT[:, h * HALF + i, :], wv, start=True, stop=True)
                last.then_inc(s["v_ps"], 1)

            pe.wait_ge(s["pad_done"], 1)
            turn4(0, qpad, 0, "hT_ps")
            pe.wait_ge(s["pad_done"], 2)
            turn4(1, kpad, 0, "hT_ps")

            def max_scores(u):
                pr, i = divmod(u, 4)
                if u >= 4:
                    pe.wait_ge(s["max_sb"], u - 3)
                elif u >= 2:
                    pe.wait_ge(s["pad_done"], 2 * (u - 1))
                else:
                    pe.wait_ge(s["v_sb"], u + 1)
                pe.wait_ge(s["lowp"], 3 * (pr // 2 + 1))
                rows = slice(32 * i, 32 * i + 32)
                for c in range(4):
                    b, par = 2 * pr + c // 2, c % 2
                    last = t.matmul(ps[2 + i][:, c * 128:(c + 1) * 128], qTb[rows, b, :], kTb[rows, par, b, :], start=True, stop=True)
                last.then_inc(s["max_ps"], 1)

            pe.wait_ge(s["hT_sb"], 2)
            for k in range(GROUPS):
                b, gi = divmod(k, 2)
                h, bb = divmod(b, HALF)
                pe.wait_ge(s[f"cosm{h}"], NH)
                if k >= 2:
                    pe.wait_ge(s["cos_g"], k - 1)
                t.matmul(ps[k % 2][:], kh[:, b, :], cosm[h][:, bb, HG * gi:HG * gi + HG, :].rearrange("p n s -> p (n s)"),
                         start=True, stop=True).then_inc(s["cos_ps"], 1)
                max_scores(k)
                if k == 0:
                    pe.wait_ge(s["q_sb"], 2)
                    pe.wait_ge(s["pad_done"], 3)
                    turn4(6, qpad, 1, "hT_ps")
                    pe.wait_ge(s["k_sb"], 2)
                    pe.wait_ge(s["pad_done"], 4)
                    turn4(7, kpad, 1, "hT_ps")
                if k == 3:
                    pe.wait_ge(s["l_ffw"], 16 * 7)
                    pe.wait_ge(s["hT_sb"], 3)
                    for c in range(4):
                        last = t.transpose(ps[6][:, c * 128:(c + 1) * 128], fw1[:, c:FF:4], ident[:])
                    last.then_inc(s["fw_ps"], 1)
                if k == 5:
                    pe.wait_ge(s["hT_sb"], 4)
                    pe.wait_ge(s["l_gate"], 16)
                    for c in range(4):
                        t.transpose(ps[7][:, c * NQ:(c + 1) * NQ], fwqo[:, c:FF:4], ident[0:NQ, 0:NQ])
                    t.transpose(ps[7][:, 64:64 + NE], gw, ident[0:NE, 0:NE]).then_inc(s["fw_ps"], 1)
                    pe.wait_ge(s["least_sb"], 1)
                    for j in range(2):
                        last = t.transpose(ps[7][0:1, 256 + 128 * j:384 + 128 * j], least[:, j:j + 1], ident[:])
                    last.then_inc(s["least_ps"], 1)
                if k == 7:
                    pe.wait_ge(s["fw_sb"], 3)
                    for c in range(4):
                        t.matmul(ps[6][:, 0:NQ], fw1T[:, c, :], fwm[:, c, :], start=(c == 0), stop=(c == 3))
                    for c in range(4):
                        last = t.matmul(ps[6][0:NQ, 16:17], fwm[:, c, :], fb1[:, c:c + 1], start=(c == 0), stop=(c == 3))
                    last.then_inc(s["fu_ps"], 1)
                if k == 8:
                    pe.wait_ge(s["small_known"], 1)
                    pe.wait_ge(s["c_pool"], 1)
                    for c in range(4):
                        last = t.matmul(ps[7][0:NQ + 1, 128:256], fwqoT[:, :, c], fw2[:, c, :], start=(c == 0), stop=(c == 3))
                    last.then_inc(s["fu_ps"], 1)
            pe.wait_ge(s["fu_sb"], 3)
            with t.If(t.value_load(small[0:1, 0:1]) > 0):
                pe.wait_ge(s["cos_g"], GROUPS)
                for k in range(GROUPS):
                    b, gi = divmod(k, 2)
                    if k:
                        pe.wait_ge(s["small_g"], 2 * k)
                    for j in range(2):
                        last = t.transpose(ps[6][0:NH, 128 * j:128 * j + 128], nrm[:, b, 8 * j:8 * j + 8], ident[:])
                    last.then_inc(s["small_ps"], 1)
                    pe.wait_ge(s["small_ops"], k + 1)
                    t.matmul(ps[1][:], kn, an, start=True, stop=True)
                    t.matmul(ps[0][:], kh[:, b, :], masked, start=True, stop=True).then_inc(s["small_ps"], 1)
                pe.wait_ge(s["small_g"], 2 * GROUPS)
            for h in range(NHALF):
                pe.wait_ge(s["max_sb"], 8 * (h + 1))
                t.transpose(ps[6 + h][0:32, 0:128], mx[:, h * HALF:(h + 1) * HALF, :].rearrange("p b n -> p (b n)"),
                            ident[:]).then_inc(s["mT_ps"], 1)

            def dots(k):
                b, gi = divmod(k, 2)
                h, bb = divmod(b, HALF)
                pe.wait_ge(s[f"dotm{h}"], NH)
                pe.wait_ge(s["bd_sb"], h + 1)
                if k >= 2:
                    pe.wait_ge(s["arg_sb"], k - 1)
                else:
                    pe.wait_ge(s["cos_g"], GROUPS - 1 + k)
                t.matmul(ps[k % 2][:], kT[:, b, :], dotm[h][:, bb, HG * gi:HG * gi + HG, :].rearrange("p n s -> p (n s)"),
                         start=True, stop=False)
                t.matmul(ps[k % 2][:], negsel[:, bb, :], bd[:, h, HG * gi:HG * gi + HG, :].rearrange("p n s -> p (n s)"),
                         start=False, stop=True).then_inc(s["dot_ps"], 1)

            def pv(k):
                b, gi = divmod(k, 2)
                pe.wait_ge(s["exp_sb"], k + 1)
                if gi == 0:
                    if b >= 2:
                        pe.wait_ge(s["o_sb"], b - 1)
                    else:
                        pe.wait_ge(s["max_sb"], GROUPS)
                for i in range(HG):
                    n = HG * gi + i
                    last = t.matmul(ps[2 + b % 2][32 * i:32 * i + 32, gi * 128:gi * 128 + 128], va[:, b, n, :], G[:, b, n, :],
                                    start=True, stop=True)
                if gi:
                    last.then_inc(s["o_ps"], 1)

            def turn_out(b):
                pe.wait_ge(s["o_sb"], b + 1)
                if b >= 2:
                    pe.wait_ge(s["y_sb"], b - 1)
                for gi in range(2):
                    last = t.transpose(ps[4 + b % 2][:, gi * 128:gi * 128 + 128], ob[:, b % 2, gi, :], ident[:])
                last.then_inc(s["oT_ps"], 1)

            def turn_att(b):
                pe.wait_ge(s["at_sb"], b + 1)
                t.transpose(ps[4 + b % 2][:, 256:384], at[:, b % 2, :], ident[:]).then_inc(s["atT_ps"], 1)

            def project(b):
                pe.wait_ge(s["atT_sb"], b + 1)
                if b == 0:
                    pe.wait_ge(s["l_wo"], 16)
                t.matmul(ps[4 + b % 2][:, 384:512], atT[:, b % 2, :], wo[:], start=True, stop=True).then_inc(s["y_ps"], 1)

            def step(j, h):
                hb = slice(h * HALF, (h + 1) * HALF)
                if j == 1:
                    pe.wait_ge(s["x1_sb"], h + 1)
                    pe.wait_ge(*((s["o_sb"], B) if h else (s["ctxT_sb"], 2)))
                    turn4(BK[h][0], x1, h, "x1T_ps")
                    pe.wait_ge(s["x1T_sb"], h + 1)
                    pe.wait_ge(s["fu_sb"], 3)
                    t.matmul(ps[BK[h][1]][0:NQ, :], w1m[:], tT[:, hb, :].rearrange("p b s -> p (b s)"),
                             start=True, stop=True).then_inc(s["qm_ps"], 1)
                if j == 3:
                    pe.wait_ge(s["qe_sb"], h + 1)
                    for i in range(HALF):
                        last = t.matmul(ps[BK[h][0]][:, i * 128:(i + 1) * 128], qe[:, i * 128:(i + 1) * 128], w2f[:], start=True, stop=True)
                    last.then_inc(s["ff_ps"], 1)
                if j == 6:
                    pe.wait_ge(s["xn3_sb"], h + 1)
                    turn4(BK[h][1], x1, h, "x3T_ps")
                    pe.wait_ge(s["x3T_sb"], h + 1)
                    for i in range(HALF):
                        b = h * HALF + i
                        last = t.matmul(ps[BK[h][0]][:, i * 128:(i + 1) * 128], tT[:, b, :], cxT[:, b, :], start=True, stop=True)
                    last.then_inc(s["lg_ps"], 1)
                if j == 7:
                    pe.wait_ge(s["ex_sb"], HALF * (h + 1))
                    turn4(BK[h][1], lg_, h, "pT_ps")
                    pe.wait_ge(s["pT_sb"], h + 1)
                    for i in range(HALF):
                        b = h * HALF + i
                        last = t.matmul(ps[BK[h][0]][:, i * 128:(i + 1) * 128], pT[:, b, :], cx[:, b, :], start=True, stop=True)
                    last.then_inc(s["pv_ps"], 1)
                if j == 9:
                    pe.wait_ge(s["xn4_sb"], h + 1)
                    turn4(BK[h][1], xn, h, "x4T_ps")
                    pe.wait_ge(s["x4T_sb"], h + 1)
                    for i in range(HALF):
                        last = t.matmul(ps[BK[h][0]][:, i * NE:(i + 1) * NE], tT[:, h * HALF + i, :], gwT[:], start=True, stop=True)
                    last.then_inc(s["gt_ps"], 1)

            for k in range(GROUPS):
                dots(k)
                if k >= 1:
                    pv(k - 1)
                if k in (1, 3):
                    pe.wait_ge(s["bd_sb"], 2)
                    pe.wait_ge(s["l_ctx"], 16)
                    turn4(6 + k // 2, cx, k // 2, "ctxT_ps")
                if k >= 4 and k % 2 == 0:
                    turn_out((k - 4) // 2)
                if k >= 5 and k % 2 == 1:
                    turn_att((k - 5) // 2)
                if k >= 6 and k % 2 == 0:
                    project((k - 6) // 2)
                for j in WITHIN.get(k, ()):
                    step(j, 0)
            pv(GROUPS - 1)
            turn_out(B - 2)
            turn_att(B - 2)
            project(B - 3)
            turn_out(B - 1)
            turn_att(B - 1)
            project(B - 2)
            project(B - 1)
            for j, h in TAIL:
                step(j, h)

            pe.wait_ge(s["oh_sb"], 1)
            pe.wait_ge(s["x4T_sb"], 2)
            rank = ps[7][:, 0:128].rearrange("p (b e) -> p b e", b=B)
            t.matmul(rank, tri[:], ohb[:], start=True, stop=False, skip_group_check=True)
            for b in range(B - 1):
                last = t.matmul(rank[:, b + 1:B, :], onesb[:], ohb[:, b:b + 1, :].broadcast_to([128, B - 1 - b, NE]),
                                start=False, stop=(b == B - 2), skip_group_check=True)
            last.then_inc(s["rk_ps"], 1)
            pe.wait_ge(s["back"], 16)
            for c in range(SC):
                bank, i = divmod(c, 4)
                last = t.transpose(ps[2 + bank][:, i * 128:(i + 1) * 128], xd[:, c, :], ident[:])
                if i == 3 or c == SC - 1:
                    last.then_inc(s["xdT_ps"], 1)

            def hidden(e):
                if e == 0:
                    pe.wait_ge(s["xdT_sb"], 4)
                    pe.wait_ge(s["si_sb"], 1)
                if e % 4 == 0:
                    pe.wait_ge(s["l_w1"], 16 * 4)
                if e >= 3:
                    pe.wait_ge(s["hid_sb"], e - 2)
                for c in range(4):
                    last = t.matmul(ps[5 + e % 3][:, c * CW:(c + 1) * CW], w1s[:, e, c * 128:(c + 1) * 128],
                                    xdT[:, e * CAP:e * CAP + CW], start=True, stop=True)
                last.then_inc(s["hid_ps"], 1)

            def expert_out(e):
                q, i = divmod(e, 4)
                pe.wait_ge(s["hid_sb"], e + 1)
                if e == 0:
                    pe.wait_ge(s["l_w2"], 16 * 4)
                if i == 0 and q >= 2:
                    pe.wait_ge(s["eo_sb"], q - 1)
                for c in range(4):
                    last = t.matmul(ps[q % 2][0:CAP, i * 128:(i + 1) * 128], hT[:, e % 3, c, :], w2s[:, e, c, :],
                                    start=(c == 0), stop=(c == 3))
                last.then_inc(s["eo_ps"], 1)

            for e in range(NE + 1):
                if e < NE:
                    hidden(e)
                if e:
                    expert_out(e - 1)


_INS = ['x', 'ctx_1024', 'mask_BxSxS2_fk0'] + ['L0_attn_' + n for n in (
    'Wq', 'bq', 'Wk', 'bk', 'Wv', 'bv', 'Wc2q', 'bc2q', 'Wo', 'bo', 'g1', 'beta1', 'g2', 'beta2', 'W1', 'b1',
    'Wm', 'bm', 'Wqo', 'bqo', 'W2', 'b2')] + ['L0_ffn_gate_w', 'L0_ffn_w1', 'L0_ffn_w2']


def kernel(**inputs):
    import concourse.bacc as _bacc
    from concourse.bass_utils import run_bass_kernel_spmd as _run

    nc = _bacc.Bacc("TRN2", target_bir_lowering=False, num_devices=1)
    arrays, args = {}, []
    for name in _INS:
        a = np.ascontiguousarray(inputs[name])
        arrays[f"in_{name}"] = a
        args.append(nc.dram_tensor(f"in_{name}", a.shape, mybir.dt.from_np(a.dtype), kind="ExternalInput").ap())
    out = nc.dram_tensor("out_0", (B, S, D), F32, kind="ExternalOutput").ap()
    decoder_block(nc, *args, out)
    r = _run(nc, [arrays], core_ids=[0])
    return r.results[0]["out_0"]
```

```python
import math
from contextlib import ExitStack

import numpy as np

import concourse.bass as bass
from concourse import mybir

F32 = mybir.dt.float32
BF16 = mybir.dt.bfloat16
I32 = mybir.dt.int32
U8 = mybir.dt.uint8
U32 = mybir.dt.uint32
ALU = mybir.AluOpType
ACT = mybir.ActivationFunctionType
X = mybir.AxisListType.X
XY = mybir.AxisListType.XY

B, S, D = 8, 128, 128
NH, HD, NQ = 8, 16, 8
FF = 512
NE, DFF = 16, 512
TOK = B * S
CAP = math.floor(1.25 * TOK / NE)
CAP = max(CAP + CAP % 2, 4)
SLOTS = NE * CAP
SC = SLOTS // 128
CW = 96
HALF = 4
HC = HALF * S
NHALF = B // HALF
HG = 4
GROUPS = B * NH // HG
LN_EPS = 1e-05
COS_EPS = 1e-08
PI_IN = float(np.float32(math.pi * (1 - 2.0 ** -21)))
PAIR = 2
NPAIR = B // PAIR
ROW = D + 2
NOWHERE = 4 * TOK
COS = [0.999999999885, -4.93480218577, 4.05871181578, -1.3352602774, 0.23532080051, -0.0257857720901, 0.00190430229777, -8.86833217906e-05]
ROUND = 12582912.0


def decoder_block(nc, x, ctx_in, mask, Wq, bq, Wk, bk, Wv, bv, Wc, bc, Wo, bo, g1, beta1, g2, beta2,
                  W1, b1, Wm, bm, Wqo, bqo, W2, b2, gate_w, w1, w2, out):
    st = ExitStack()
    with st:
        def sb(name, shape, dt=F32):
            return st.enter_context(nc.sbuf_tensor(name, shape, dt))

        def sem(name):
            return st.enter_context(nc.semaphore(name))

        xs = sb("xs", [128, B, D])
        cx = sb("cx", [128, B, D])
        mk = sb("mk", [128, B, S])
        mlow = sb("mlow", [128, B, S], U8)
        xn = sb("xn", [128, B, D])
        tT = sb("tT", [128, B, S])
        qT = sb("qT", [128, B, S])
        kT = sb("kT", [128, B, S])
        qTb = sb("qTb", [128, B, S], BF16)
        kTb = sb("kTb", [128, 2, B, S], BF16)
        qh = sb("qh", [128, B, S])
        kh = sb("kh", [128, B, S])
        cxT = kh
        va = sb("va", [128, B, NH, 32])
        md = sb("md", [128, 3 * HALF * NH * S])
        G = sb("G", [128, B, NH, S])
        w1s = sb("w1s", [128, NE, DFF])
        w2s = sb("w2s", [128, NE, DFF // 128, D])

        def group(k):
            return G[:, k // 2, HG * (k % 2):HG * (k % 2) + HG, :].rearrange("p n s -> p (n s)")

        def slot(i):
            return md[:, i * HALF * NH * S:(i + 1) * HALF * NH * S]

        def heads(i):
            return slot(i).rearrange("p (b n s) -> p b n s", b=HALF, n=NH)
        cosm = [heads(0), heads(1)]
        dotm = [heads(2), heads(0)]
        early = slot(2).rearrange("p (a b c) -> p a b c", a=4, b=B)
        qk, sq, qpad, kpad = (early[:, i] for i in range(4))
        late = slot(1).rearrange("p (a b c) -> p a b c", a=4, b=B)
        y1, x1, lg_, pT = (late[:, i] for i in range(4))

        wq, wk, wv, wqk, bqkr, bvr = (G[:, B - 3, i, :] for i in range(6))
        wqT = G[:, B - 3, 6:8, :]
        gw = G[0:NE, B - 4, 0, :]
        wc = sb("wc", [128, 64])
        wcs = sb("wcs", [128, NQ])
        bcr = G[:, 3, 6, 0:64]
        bcols = sb("bcols", [128, 4])
        bor = sb("bor", [128, 128])
        g1r = sb("g1r", [128, 128]); be1r = sb("be1r", [128, 128])
        g2r = sb("g2r", [128, 128]); be2r = sb("be2r", [128, 128])
        wo = sb("wo", [128, 128])
        fw1, fwqo = G[:, B - 2, 0:4, :].rearrange("p n s -> p (n s)"), G[0:NQ, B - 1, 0:4, :].rearrange("p n s -> p (n s)")
        fw1T, fw2 = G[:, B - 2, 4:8, :], G[:, B - 1, 4:8, :]
        fwm = sb("fwm", [128, 4, NQ]); fb1 = sb("fb1", [128, 4]); fbm = sb("fbm", [128, 2, NQ])
        fwqoT = sb("fwqoT", [128, NQ + 1, 4])
        w1m = sb("w1m", [128, NQ])
        w2f = sb("w2f", [128, 128])
        fb2 = sb("fb2", [NQ + 1, 128])
        gwT = sb("gwT", [128, NE])
        ident = sb("ident", [128, 128])
        tri = sb("tri", [128, 128], BF16); onesb = sb("onesb", [128, 128], BF16)
        hm = sb("hm", [128, 2, NH])
        evod = sb("evod", [128, 2])
        diag = sb("diag", [32, NH])
        negsel = sb("negsel", [32, HALF, 128], BF16)
        revi = sb("revi", [128, NE])
        blank = sb("blank", [128, ROW])
        prev = sb("prev", [128, 2, NE], BF16)
        mhalf = sb("mhalf", [128, 8])

        bns = sb("bns", [128, B, 6]); mv = sb("mv", [128, 5, B, 2])
        ve = sb("ve", [128, 5, B]); rstd = sb("rstd", [128, 5, B])
        nr = G[:, 3, 0:6, :].rearrange("p a s -> p (a s)").rearrange("p (i b c) -> p i b c", i=6, b=B)
        nrm = sb("nrm", [128, B, 16])
        mx = sb("mx", [128, B, NH])
        bd = tT[0:32].rearrange("p b s -> p (b s)").bitcast(BF16).rearrange("p (h n s) -> p h n s", h=NHALF, n=NH)
        ob = qh[:, 0:4, :].rearrange("p (r g) s -> p r g s", r=2)
        at, atT = qh[:, 4:6, :], qh[:, 6:8, :]
        rec = sb("rec", [128, 2, NH])
        qeT = sb("qeT", [128, 2, PAIR * S])
        pay = slot(2)[:, 0:B * ROW].rearrange("p (b r) -> p b r", b=B)
        rt = slot(2)[:, 1040:1040 + 4 * B * NE].rearrange("p (i b e) -> p i b e", i=4, b=B)
        ffs = slot(2)[:, 1552:1552 + 10 * B * NQ].rearrange("p (i b q) -> p i b q", i=10, b=B)
        ngm = sb("ngm", [128, B]); sume = sb("sume", [128, B]); rsum = sb("rsum", [128, B])
        okr = sb("okr", [128, B])
        ohb = sb("ohb", [128, B, NE], BF16)
        r1 = sb("r1", [128, 8, B]); si = sb("si", [128, B], U32)

        least = sb("least", [128, 2]); least2 = sb("least2", [1, 4]); small = sb("small", [1, 1], I32)
        redo = slot(1).rearrange("p (i c) -> p i c", i=8)
        masked, scaled, fval = redo[:, 0], redo[:, 1], redo[:, 2]
        kn, an = redo[0:NH, 3, 0:128], redo[0:NH, 4]

        Gf = G[:].rearrange("p b n s -> p (b n s)")
        xd = Gf[0:CAP, 0:NE * ROW].rearrange("p (e r) -> p e r", e=NE)
        xdT = Gf[:, 2080:2080 + SLOTS + CW - CAP]
        hT = Gf[:, 3376:3376 + 3 * 4 * CAP].rearrange("p (r c k) -> p r c k", r=3, c=4)
        eo = Gf[0:CAP, 4336:4336 + NE * 128].rearrange("p (e d) -> p e d", e=NE)

        ps = [st.enter_context(nc.psum_tensor(f"bank{i}", [128, 512], F32)) for i in range(8)]

        def quads(i):
            return ps[i][:].rearrange("p (b s) -> p b s", b=4)

        toks = nc.dram_tensor("slot_tokens", [SLOTS, ROW], F32, kind="Internal").ap()

        names = """l_x0 l_x1 l_qk l_v l_wc wc_diag l_bias l_rows l_wo l_ffw l_ctx l_mask l_gate l_w1 l_w2 l_b2 zrow
            c_ident c_zero c_half c_rest c_pay rstd_done pool_step
            xn_done tT_ps tT_sb wT_ps wT_sb wc_ps wc_sb qk_ps proj_ps q_sb k_sb v_ps v_sb lowp pad_done hT_ps hT_sb
            cosm0 cosm1 dotm0 dotm1 cos_ps sin_sb cos_g max_ps max_sb mT_ps bd_sb
            dot_ps arg_sb exp_sb o_ps o_sb oT_ps at_sb atT_ps atT_sb y_ps y_sb xb_done
            ln_st y1_sb y1T_ps y1T_sb qm_ps qm_sb th_sb qe_sb qeT_ps qeT_sb ff_ps xn3_sb x3T_ps x3T_sb
            lg_ps lg_sb ex_sb pT_ps pT_sb pv_ps x3_sb xn4_sb x4T_ps x4T_sb gt_ps oh_sb rx_sb re_sb rk_ps si_sb
            fw_ps fw_sb fu_ps fu_sb ctxT_ps ctxT_sb
            sent back0 back1 back2 back3 xdT_ps xdT_sb xd_pad hid_ps hid_sb eo_ps eo_sb added stored dch ach
            least_sb least_ps small_known small_ops small_ps small_f small_sin small_g""".split()
        s = {n: sem(n) for n in names}

        block = st.enter_context(nc.Block())

        STAGES = 13
        NSLOTS = 35
        AT = {k: [] for k in range(NSLOTS)}
        for pair, when in enumerate([[8, 12, 13, 15, 16, 17, 18, 19, 20, 21, 22, 23, 24], [14, 15, 16, 17, 18, 19, 20, 23, 25, 26, 27, 28, 29], [16, 17, 18, 21, 22, 23, 24, 25, 26, 27, 29, 30, 31], [20, 21, 22, 23, 24, 25, 26, 27, 28, 29, 32, 33, 34]]):
            when = when + [when[-1] + 1 + i for i in range(STAGES - len(when))]
            for stage, k in enumerate(when):
                AT[k].append((stage, pair))
        NORM_OF_STAGE = {0: 1, 4: 2, 5: 3, 9: 4}
        NORMS = [(0, h) for h in range(NHALF)] + [(NORM_OF_STAGE[j], p) for k in range(NSLOTS) for j, p in AT[k]
                                                  if j in NORM_OF_STAGE]

        def norm_count(i, u):
            return NORMS.index((i, u)) + 1

        def norm_batches(i, u):
            return slice(u * HALF, (u + 1) * HALF) if i == 0 else slice(u * PAIR, (u + 1) * PAIR)

        EO_BANK = [0, 1, 4]
        PAIR_BANK = [6, 7, 0, 1]

        def turned(p):
            return ps[PAIR_BANK[p]][:, 0:PAIR * 128].rearrange("p (b s) -> p b s", b=PAIR)

        def product(p):
            return ps[PAIR_BANK[p]][:, PAIR * 128:2 * PAIR * 128].rearrange("p (b s) -> p b s", b=PAIR)

        def batches(p):
            return slice(p * PAIR, (p + 1) * PAIR)

        def row(v):
            return v.rearrange("(a n) -> a n", a=1)

        @block.sync
        def _(sp):
            def load_x(h):
                hb = slice(h * HALF, (h + 1) * HALF)
                sp.dma_start(xs[:, hb, :], x[hb].rearrange("b s d -> s b d")).then_inc(s[f"l_x{h}"], 16)

            def load_projection(dst, src, done):
                sp.dma_start(dst[:].rearrange("p (n d) -> p n d", n=NH),
                             src.rearrange("n h d -> h n d")).then_inc(s[done], 16)

            load_x(0)
            load_projection(wq, Wq, "l_qk")
            load_projection(wk, Wk, "l_qk")
            load_x(1)
            load_projection(wv, Wv, "l_v")
            for dst, src in ((bvr, bv.rearrange("n d -> (n d)")), (bor, bo), (g1r, g1), (be1r, beta1), (g2r, g2), (be2r, beta2)):
                sp.dma_start(dst[:], row(src).broadcast_to([128, 128])).then_inc(s["l_rows"], 16)
            sp.dma_start(fw1, W1).then_inc(s["l_ffw"], 16)
            sp.dma_start(fwm[:], Wm.rearrange("(p c) q -> p c q", c=4)).then_inc(s["l_ffw"], 16)
            sp.dma_start(fb1[:], b1.rearrange("(p c) -> p c", c=4)).then_inc(s["l_ffw"], 16)
            sp.dma_start(fbm[:, 0, :], row(bm).broadcast_to([128, NQ])).then_inc(s["l_ffw"], 16)
            sp.dma_start(bcols[:, 3:4], beta1.rearrange("(p a) -> p a", a=1)).then_inc(s["l_ffw"], 16)
            sp.dma_start(fwqo, Wqo).then_inc(s["l_ffw"], 16)
            sp.dma_start(fwqoT[:, NQ, :], bqo.rearrange("(p c) -> p c", c=4)).then_inc(s["l_ffw"], 16)
            sp.dma_start(fw2, W2.rearrange("(p c) d -> p c d", c=4)).then_inc(s["l_ffw"], 16)
            sp.dma_start(gw, gate_w).then_inc(s["l_gate"], 16)
            sp.dma_start(wo[:], Wo).then_inc(s["l_wo"], 16)
            sp.wait_ge(s["c_zero"], 2)
            sp.dma_start(toks.rearrange("(c p) r -> p c r", p=128),
                         blank[:].unsqueeze(1).broadcast_to([128, SC, ROW])).then_inc(s["zrow"], 16)
            sp.dma_start(fb2[NQ:NQ + 1, :], row(b2)).then_inc(s["l_b2"], 16)
            sp.wait_ge(s["l_rows"], 16 * 6)
            sp.wait_ge(s["l_ffw"], 16 * 8)
            sp.dma_start(cx[:], ctx_in.rearrange("b t d -> t b d")).then_inc(s["l_ctx"], 16)
            sp.dma_start(mk[:], mask.rearrange("b s t -> s b t")).then_inc(s["l_mask"], 16)
            for e in range(0, NE, 4):
                sp.dma_start(w1s[:, e:e + 4, :], w1[e:e + 4].rearrange("e d f -> d e f")).then_inc(s["l_w1"], 16)
                sp.dma_start(w2s[:, e:e + 4], w2[e:e + 4].rearrange("e (c p) d -> p e c d", p=128)).then_inc(s["l_w2"], 16)
            for p in range(NPAIR):
                sp.wait_ge(s["x3_sb"], p + 1)
                sp.dma_start(out[batches(p)].rearrange("b s d -> s b d"), xs[:, batches(p), :]).then_inc(s["stored"], 16)
            sp.wait_ge(s["sent"], 16 * B)
            sp.wait_ge(s["o_ps"], B)
            for e in range(0, NE, 4):
                sp.dma_start(xd[:, e:e + 4, :], toks[e * CAP:(e + 4) * CAP, :].rearrange("(e c) r -> c e r", e=4)).then_inc(s[f"back{e // 4}"], 16)

        @block.gpsimd
        def _(pool):
            g = nc.gpsimd
            chain = [0]

            def link(ins):
                chain[0] += 1
                ins.then_inc(s["pool_step"], 1)
                pool.wait_ge(s["pool_step"], chain[0])

            g.memset(mhalf[:], -0.5)
            g.memset(hm[:], 1.0)
            link(g.memset(ident[:], 0.0))
            g.affine_select(out=ident[:], in_=ident[:], compare_op=ALU.not_equal, fill=1.0, base=0,
                            pattern=[[-1, 128]], channel_multiplier=1).then_inc(s["c_ident"], 1)
            for j, wdt in ((0, HD), (1, NQ)):
                link(g.affine_select(out=hm[:, j, :], in_=hm[:, j, :], compare_op=ALU.is_ge, fill=0.0, base=0,
                                     pattern=[[-wdt, NH]], channel_multiplier=1))
                link(g.affine_select(out=hm[:, j, :], in_=hm[:, j, :], compare_op=ALU.is_ge, fill=0.0,
                                     base=wdt - 1, pattern=[[wdt, NH]], channel_multiplier=-1))
            link(g.tensor_tensor(evod[:, 0:1], hm[:, 0, 0:1], hm[:, 0, 2:3], ALU.add))
            link(g.tensor_tensor(evod[:, 0:1], evod[:, 0:1], hm[:, 0, 4:5], ALU.add))
            link(g.tensor_tensor(evod[:, 0:1], evod[:, 0:1], hm[:, 0, 6:7], ALU.add))
            g.tensor_scalar(evod[:, 1:2], evod[:, 0:1], -1.0, 1.0, ALU.mult, ALU.add).then_inc(s["c_half"], 1)

            def rest_of_constants():
                g.memset(diag[:], 0.0)
                g.memset(negsel[:], -1.0)
                g.memset(tri[:], 1.0)
                g.memset(onesb[:], 1.0)
                g.memset(va[:], 0.0)
                g.memset(prev[:], 0.0)
                link(g.memset(qeT[:], 0.0))
                g.memset(va[:, :, :, HD:HD + 1], 1.0)
                for b in range(HALF):
                    link(g.affine_select(out=diag[:], in_=diag[:], compare_op=ALU.not_equal, fill=1.0, base=-b * NH,
                                         pattern=[[-1, NH]], channel_multiplier=1))
                link(g.affine_select(out=negsel[:], in_=negsel[:], compare_op=ALU.is_ge, fill=0.0, base=0,
                                     pattern=[[-NH, HALF], [0, 128]], channel_multiplier=1))
                link(g.affine_select(out=negsel[:], in_=negsel[:], compare_op=ALU.is_ge, fill=0.0, base=NH - 1,
                                     pattern=[[NH, HALF], [0, 128]], channel_multiplier=-1))
                g.affine_select(out=tri[:], in_=tri[:], compare_op=ALU.is_ge, fill=0.0, base=0,
                                pattern=[[1, 128]], channel_multiplier=-1)
                g.iota(revi[:], [[-1, NE]], base=NE, channel_multiplier=0, allow_small_or_imprecise_dtypes=True)
                g.affine_select(out=qeT[:], in_=qeT[:], compare_op=ALU.not_equal, fill=1.0, base=-NQ,
                                pattern=[[0, 2], [0, PAIR * S]], channel_multiplier=1).then_inc(s["c_rest"], 1)

            def rsqrt(i, h):
                hb = norm_batches(i, h)
                pool.wait_ge(s["ln_st"], norm_count(i, h))
                link(g.tensor_scalar(ve[:, i, hb], mv[:, i, hb, 1], LN_EPS, 1.0, ALU.add, ALU.mult))
                g.tensor_tensor(rstd[:, i, hb], ve[:, i, hb], mhalf[:, 0:hb.stop - hb.start], ALU.pow).then_inc(s["rstd_done"], 1)

            def cosine_of(p):
                qm, th, u, z, z2, qe, even, odd, low, high = (ffs[:, i, batches(p), :] for i in range(10))
                pool.wait_ge(s["qm_sb"], p + 1)
                link(g.tensor_scalar(u, qm, 0.125, ROUND, ALU.mult, ALU.add))
                link(g.tensor_scalar(u, u, ROUND, 8.0, ALU.subtract, ALU.mult))
                link(g.tensor_tensor(u, qm, u, ALU.subtract))
                link(g.tensor_tensor(z, u, u, ALU.mult))
                link(g.tensor_scalar(z, z, 1.0 / 16, 1.0, ALU.mult, ALU.min))
                g.tensor_tensor(z2, z, z, ALU.mult)
                g.tensor_scalar(odd, z, COS[7], COS[6], ALU.mult, ALU.add)
                g.tensor_scalar(even, z, COS[3], COS[2], ALU.mult, ALU.add)
                g.tensor_scalar(high, z, COS[5], COS[4], ALU.mult, ALU.add)
                link(g.tensor_scalar(low, z, COS[1], COS[0], ALU.mult, ALU.add))
                g.tensor_tensor(odd, odd, z2, ALU.mult)
                g.tensor_tensor(even, even, z2, ALU.mult)
                link(g.tensor_tensor(z2, z2, z2, ALU.mult))
                g.tensor_tensor(high, high, odd, ALU.add)
                link(g.tensor_tensor(low, low, even, ALU.add))
                link(g.tensor_tensor(high, high, z2, ALU.mult))
                link(g.tensor_tensor(low, low, high, ALU.add))
                pool.wait_ge(s["th_sb"], p + 1)
                g.tensor_tensor(qe, low, th, ALU.mult).then_inc(s["qe_sb"], 1)

            for h in range(NHALF):
                rsqrt(0, h)
            rest_of_constants()
            for h in range(NHALF):
                hb = slice(h * HALF, (h + 1) * HALF)
                pool.wait_ge(s["q_sb"], h + 1)
                g.tensor_scalar(qTb[:, hb, :], qT[:, hb, :], 1.0, 1.0, ALU.mult, ALU.mult).then_inc(s["lowp"], 1)
                pool.wait_ge(s["k_sb"], h + 1)
                for j in range(2):
                    g.tensor_scalar(kTb[:, j, hb, :], kT[:, hb, :], evod[:, j:j + 1], 1.0,
                                    ALU.mult, ALU.mult).then_inc(s["lowp"], 1)
            pool.wait_ge(s["hT_sb"], 2 * NHALF)
            for n in range(NH):
                g.tensor_scalar(cosm[1][:, :, n, :], qh[:, HALF:B, :], hm[:, 1, n:n + 1], 1.0,
                                ALU.mult, ALU.mult).then_inc(s["cosm1"], 1)
            pool.wait_ge(s["cos_ps"], GROUPS // NHALF)
            for n in range(NH):
                g.tensor_scalar(dotm[1][:, :, n, :], qT[:, HALF:B, :], hm[:, 0, n:n + 1], 1.0,
                                ALU.mult, ALU.mult).then_inc(s["dotm1"], 1)
            pool.wait_ge(s["l_rows"], 16 * 6)
            pool.wait_ge(s["tT_ps"], 2)
            pool.wait_ge(s["ln_st"], 2)
            for b in range(B):
                g.tensor_tensor(xs[:, b, :], xs[:, b, :], be2r[:], ALU.add)
                last = g.tensor_tensor(xn[:, b, :], xn[:, b, :], bor[:], ALU.add)
            last.then_inc(s["xb_done"], 1)
            pool.wait_ge(s["arg_sb"], GROUPS // NHALF)
            g.iota(pay[:, :, D + 1].bitcast(I32), [[S, B]], base=0, channel_multiplier=1).then_inc(s["c_pay"], 1)
            for k in range(NSLOTS):
                for j, p in AT[k]:
                    if j in NORM_OF_STAGE:
                        rsqrt(NORM_OF_STAGE[j], p)
                    if j == 2:
                        cosine_of(p)
                    if j == 12:
                        pool.wait_ge(s["si_sb"], p + 1)
                        if p == 0:
                            pool.wait_ge(s["zrow"], 16)
                        for b in range(p * PAIR, (p + 1) * PAIR):
                            g.indirect_dma_start(toks, bass.IndirectOffsetOnAxis(ap=si[:, b:b + 1], axis=0),
                                                 pay[:, b, :], None, bounds_check=SLOTS - 1,
                                                 oob_is_err=False).then_inc(s["sent"], 16)
            pool.wait_ge(s["stored"], 16 * NPAIR)
            rows = out.rearrange("b s d -> (b s) d")
            for e in range(NE):
                if e % 4 == 0:
                    pool.wait_ge(s[f"back{e // 4}"], 16)
                pool.wait_ge(s["eo_sb"], e + 1)
                g.indirect_dma_start(rows, bass.IndirectOffsetOnAxis(ap=xd[:, e, D + 1:D + 2].bitcast(U32), axis=0),
                                     eo[:, e, :], None, bounds_check=TOK - 1, oob_is_err=False,
                                     compute_op=ALU.add).then_inc(s["added"], 16)
            pool.wait_ge(s["added"], 16 * NE)

        def out_evac(act, a, b):
            act.wait_ge(s["o_ps"], b + 1)
            if b >= 2:
                act.wait_ge(s["oT_ps"], b - 1)
            a.activation(ob[:, b % 2].rearrange("p g s -> p (g s)"), ps[2 + b % 2][:, 0:256], ACT.Copy).then_inc(s["o_sb"], 1)

        def att_evac(act, a, b):
            act.wait_ge(s["atT_ps"], b + 1)
            if b >= 2:
                act.wait_ge(s["y_ps"], b - 1)
            a.activation(atT[:, b % 2, :], ps[4 + b % 2][:, 256:384], ACT.Copy).then_inc(s["atT_sb"], 1)

        @block.scalar
        def _(act):
            a = nc.scalar
            act.dma_start(wcs[:], Wc.rearrange("n d q -> (n d) q")).then_inc(s["l_wc"], 16)
            act.dma_start(bcols[:, 0:1], bq.rearrange("n d -> (n d)").rearrange("(p a) -> p a", a=1)).then_inc(s["l_bias"], 16)
            act.dma_start(bcols[:, 1:2], bk.rearrange("n d -> (n d)").rearrange("(p a) -> p a", a=1)).then_inc(s["l_bias"], 16)
            act.dma_start(bcr, row(bc.rearrange("n q -> (n q)")).broadcast_to([128, 64])).then_inc(s["l_bias"], 16)
            chain = [0]

            def link(ins):
                chain[0] += 1
                ins.then_inc(s["ach"], 1)
                act.wait_ge(s["ach"], chain[0])

            a.preload_act_table(ACT.Exp)
            act.wait_ge(s["wT_ps"], 1)
            a.activation(wqT.rearrange("p a b -> p (a b)"), ps[4][:, 0:256], ACT.Copy).then_inc(s["wT_sb"], 1)
            act.wait_ge(s["wc_ps"], 1)
            a.activation(wqk, ps[5][:, 0:128], ACT.Copy).then_inc(s["wc_sb"], 1)
            act.wait_ge(s["l_bias"], 48)
            link(a.activation(bcols[:, 2:3], bcols[:, 0:1], ACT.Copy, scale=0.125))
            for h in range(NHALF):
                hb = slice(h * HALF, (h + 1) * HALF)
                act.wait_ge(s["tT_ps"], h + 1)
                a.activation(tT[:, hb, :], quads(2 + h), ACT.Copy).then_inc(s["tT_sb"], 1)
            for h in range(NHALF):
                hb = slice(h * HALF, (h + 1) * HALF)
                act.wait_ge(s["proj_ps"], 2 * h + 1)
                a.activation(qT[:, hb, :], quads(6), ACT.Identity, bias=bcols[:, 2:3], scale=0.125).then_inc(s["q_sb"], 1)
                act.wait_ge(s["proj_ps"], 2 * h + 2)
                a.activation(kT[:, hb, :], quads(7), ACT.Identity, bias=bcols[:, 1:2]).then_inc(s["k_sb"], 1)

            def spread_maxima(h, n):
                act.wait_ge(s["mT_ps"], h + 1)
                a.activation(bd[:, h, n, :], ps[6 + h][0:32, 0:128], ACT.Copy, scale=diag[:, n:n + 1]).then_inc(s["bd_sb"], 1)

            def unit_evac(h):
                for j, dst in enumerate((qh, kh)):
                    act.wait_ge(s["hT_ps"], 2 * h + j + 1)
                    a.activation(dst[:, h * HALF:(h + 1) * HALF, :], quads(6 * h + j), ACT.Copy).then_inc(s["hT_sb"], 1)

            unit_evac(0)
            unit_evac(1)
            a.preload_act_table(ACT.Sin)
            for k in range(GROUPS):
                act.wait_ge(s["cos_ps"], k + 1)
                if k == 12:
                    act.wait_ge(s["fu_ps"], 2)
                a.activation(group(k), ps[k % 2][:], ACT.Sin, scale=PI_IN).then_inc(s["sin_sb"], 1)
                if k % 2 == 1:
                    n = k // 2
                    a.activation(dotm[0][:, :, n, :], qT[:, 0:HALF, :], ACT.Copy,
                                 scale=hm[:, 0, n:n + 1]).then_inc(s["dotm0"], 1)
                if k == 4:
                    act.wait_ge(s["fw_ps"], 1)
                    a.activation(fw1T.rearrange("p a b -> p (a b)"), ps[6][:], ACT.Copy).then_inc(s["fw_sb"], 1)
                if k == 6:
                    act.wait_ge(s["fw_ps"], 2)
                    a.activation(fwqoT[:, 0:NQ, :], ps[7][:, 0:32].rearrange("p (c q) -> p q c", c=4), ACT.Copy).then_inc(s["fw_sb"], 1)
                    a.activation(gwT[:], ps[7][:, 64:64 + NE], ACT.Copy).then_inc(s["fw_sb"], 1)
                if k >= 14:
                    for n in range(HG * (k - 14), HG * (k - 13)):
                        spread_maxima(0, n)
                if k == 8:
                    act.wait_ge(s["fu_ps"], 1)
                    a.activation(w1m[:], ps[6][:, 0:NQ], ACT.Copy).then_inc(s["fu_sb"], 1)

            def stage(j, p):
                pb = batches(p)
                if j == 1:
                    act.wait_ge(s["y1T_ps"], p + 1)
                    a.activation(tT[:, pb, :], turned(p), ACT.Copy).then_inc(s["y1T_sb"], 1)
                if j == 2:
                    act.wait_ge(s["qm_sb"], p + 1)
                    a.activation(ffs[:, 1, pb, :], ffs[:, 0, pb, :], ACT.Tanh).then_inc(s["th_sb"], 1)
                if j == 3:
                    act.wait_ge(s["qeT_ps"], p + 1)
                    if p >= 2:
                        act.wait_ge(s["ff_ps"], p - 1)
                    else:
                        act.wait_ge(s["c_rest"], 1)
                    a.activation(qeT[0:NQ, p % 2, :], ps[PAIR_BANK[p]][0:NQ, 0:PAIR * 128], ACT.Copy).then_inc(s["qeT_sb"], 1)
                if j == 6:
                    act.wait_ge(s["x3T_ps"], p + 1)
                    a.activation(tT[:, pb, :], turned(p), ACT.Copy).then_inc(s["x3T_sb"], 1)
                if j == 7:
                    act.wait_ge(s["lg_sb"], p + 1)
                    for b in range(p * PAIR, (p + 1) * PAIR):
                        a.activation(lg_[:, b, :], lg_[:, b, :], ACT.Exp, bias=ngm[:, b:b + 1],
                                     accum_out=sume[:, b:b + 1]).then_inc(s["ex_sb"], 1)
                if j == 8:
                    act.wait_ge(s["pT_ps"], p + 1)
                    a.activation(pT[:, pb, :], turned(p), ACT.Copy).then_inc(s["pT_sb"], 1)
                if j == 10:
                    act.wait_ge(s["x4T_ps"], p + 1)
                    a.activation(tT[:, pb, :], turned(p), ACT.Copy).then_inc(s["x4T_sb"], 1)
                if j == 11:
                    act.wait_ge(s["rx_sb"], p + 1)
                    a.activation(rt[:, 1, pb, :], rt[:, 0, pb, :], ACT.Exp).then_inc(s["re_sb"], 1)

            act.wait_ge(s["small_known"], 1)
            with a.If(a.value_load(small[0:1, 0:1]) > 0):
                for k in range(GROUPS):
                    act.wait_ge(s["small_f"], k + 1)
                    if k == 0:
                        act.wait_ge(s["cos_g"], GROUPS)
                    a.activation(group(k), fval, ACT.Sin, scale=PI_IN).then_inc(s["small_sin"], 1)
            a.preload_act_table(ACT.Exp)
            for k in range(NSLOTS):
                if 1 <= k <= 4:
                    spread_maxima(1, 2 * k - 2)
                    spread_maxima(1, 2 * k - 1)
                if k in (2, 10):
                    h = k // 10
                    act.wait_ge(s["ctxT_ps"], h + 1)
                    a.activation(cxT[:, h * HALF:(h + 1) * HALF, :], quads(6 + h), ACT.Copy).then_inc(s["ctxT_sb"], 1)
                if k < GROUPS:
                    act.wait_ge(s["arg_sb"], k + 1)
                    a.activation(group(k), group(k), ACT.Exp).then_inc(s["exp_sb"], 1)
                if k % 2 == 1 and 0 <= (k - 3) // 2 < B:
                    out_evac(act, a, (k - 3) // 2)
                if k % 2 == 1 and 0 <= (k - 5) // 2 < B:
                    att_evac(act, a, (k - 5) // 2)
                for j, p in AT[k]:
                    stage(j, p)
            a.preload_act_table(ACT.Gelu_apprx_tanh)
            for q in range(4):
                act.wait_ge(s["xdT_ps"], q + 1)
                a.activation(xdT[:, 4 * CAP * q:4 * CAP * (q + 1)], ps[2 + q % 2][:, 0:4 * CAP], ACT.Copy).then_inc(s["xdT_sb"], 1)
            for e in range(NE):
                act.wait_ge(s["hid_ps"], e + 1)
                if e >= 3:
                    act.wait_ge(s["eo_ps"], e - 2)
                a.activation(hT[:, e % 3], ps[5 + e % 3][:, 0:4 * CW].rearrange("p (c k) -> p c k", c=4)[:, :, 0:CAP],
                             ACT.Gelu_apprx_tanh).then_inc(s["hid_sb"], 1)

        @block.vector
        def _(dve):
            v = nc.vector
            chain = [0]

            def link(ins):
                chain[0] += 1
                ins.then_inc(s["dch"], 1)
                dve.wait_ge(s["dch"], chain[0])

            def stats(i, src, u):
                bs = range(norm_batches(i, u).start, norm_batches(i, u).stop)
                for b in bs:
                    last = v.bn_stats(bns[:, b, :], src[:, b, :])
                link(last)
                for b in bs:
                    last = v.bn_aggr(mv[:, i, b, :], bns[:, b, :])
                last.then_inc(s["ln_st"], 1)

            def means_wait(i, h):
                dve.wait_ge(s["ln_st"], norm_count(i, h))

            def rstd_wait(i, h):
                dve.wait_ge(s["rstd_done"], norm_count(i, h))

            for h in range(NHALF):
                dve.wait_ge(s[f"l_x{h}"], 16)
                stats(0, xs, h)
                if h == 0:
                    dve.wait_ge(s["l_wc"], 16)
                    dve.wait_ge(s["c_half"], 1)
                    v.tensor_tensor(wc[:].rearrange("p (n q) -> p n q", n=NH), wcs[:].unsqueeze(1).broadcast_to([128, NH, NQ]),
                                    hm[:, 0, :].unsqueeze(2).broadcast_to([128, NH, NQ]), ALU.mult).then_inc(s["wc_diag"], 1)
            for h in range(NHALF):
                rstd_wait(0, h)
                for b in range(h * HALF, (h + 1) * HALF):
                    v.tensor_scalar(xn[:, b, :], xs[:, b, :], mv[:, 0, b, 0:1], rstd[:, 0, b:b + 1],
                                    ALU.subtract, ALU.mult).then_inc(s["xn_done"], 1)
            dve.wait_ge(s["wc_ps"], 2)
            dve.wait_ge(s["l_bias"], 48)
            bps = ps[5][:, 128:256].rearrange("p (a q) -> p a q", a=2)
            v.tensor_tensor(bqkr.rearrange("p (a q) -> p a q", a=2), bps,
                            bcr.unsqueeze(1).broadcast_to([128, 2, 64]), ALU.add).then_inc(s["wc_sb"], 1)
            v.memset(fb2[:], 0.0)
            v.memset(w2f[:], 0.0)
            link(v.memset(blank[:, 0:D + 1], 0.0))
            v.memset(blank[:, D + 1:D + 2].bitcast(I32), NOWHERE).then_inc(s["c_zero"], 1)
            v.memset(qpad, 0.0)
            v.memset(kpad, 0.0).then_inc(s["c_zero"], 1)
            for h in range(NHALF):
                hb = slice(h * HALF, (h + 1) * HALF)
                dve.wait_ge(s["qk_ps"], h + 1)
                link(v.tensor_tensor(qk[:, hb, :], quads(4 + h), bqkr.unsqueeze(1).broadcast_to([128, HALF, 128]), ALU.add))
                last = v.tensor_tensor(sq[:, hb, :], qk[:, hb, :], qk[:, hb, :], ALU.mult)
            link(last)
            ss, half_i, y, t0, t1, y2 = (nr[:, i] for i in range(6))
            link(v.tensor_reduce(t0, sq.rearrange("p b (n q) -> p b n q", q=NQ), X, ALU.add))
            link(v.tensor_scalar(ss, t0, 1e-30, None, ALU.max))
            link(v.tensor_scalar(half_i.bitcast(I32), ss.bitcast(I32), 1, None, ALU.logical_shift_right))
            link(v.tensor_scalar(y.bitcast(I32), half_i.bitcast(I32), -1.0, 1597463007.0, ALU.mult, ALU.add))
            for _ in range(3):
                link(v.scalar_tensor_tensor(t0, y, -0.5, y, ALU.mult, ALU.mult))
                link(v.tensor_tensor(t1, t0, ss, ALU.mult))
                link(v.scalar_tensor_tensor(y, t1, 1.5, y, ALU.add, ALU.mult))
            for h in range(NHALF):
                hb = slice(h * HALF, (h + 1) * HALF)
                for j, dst in enumerate((qpad, kpad)):
                    v.tensor_tensor(dst[:, hb, 0:64].rearrange("p b (n q) -> p b n q", q=NQ),
                                    qk[:, hb, 64 * j:64 * j + 64].rearrange("p b (n q) -> p b n q", q=NQ),
                                    y[:, hb, 8 * j:8 * j + 8].unsqueeze(3).broadcast_to([128, HALF, NH, NQ]),
                                    ALU.mult).then_inc(s["pad_done"], 1)
            v.tensor_tensor(nrm[:], ss, y, ALU.mult)
            dve.wait_ge(s["c_rest"], 1)
            dve.wait_ge(s["l_rows"], 16 * 6)
            for h in range(NHALF):
                dve.wait_ge(s["v_ps"], h + 1)
                for b in range(h * HALF, (h + 1) * HALF):
                    last = v.tensor_tensor(va[:, b, :, 0:HD],
                                           ps[2 + h][:, (b % 4) * 128:(b % 4) * 128 + 128].rearrange("p (n d) -> p n d", d=HD),
                                           bvr.rearrange("p (n d) -> p n d", d=HD), ALU.add)
                last.then_inc(s["v_sb"], 1)
            dve.wait_ge(s["hT_sb"], 1)
            for n in range(NH):
                v.tensor_scalar(cosm[0][:, :, n, :], qh[:, 0:HALF, :], hm[:, 1, n:n + 1], None,
                                ALU.mult).then_inc(s["cosm0"], 1)

            for k in range(GROUPS):
                dve.wait_ge(s["sin_sb"], k + 1)
                v.scalar_tensor_tensor(group(k), group(k), 10.0, ps[k % 2][:],
                                       ALU.add, ALU.mult).then_inc(s["cos_g"], 1)
                pr, i = divmod(k, 4)
                dve.wait_ge(s["max_ps"], k + 1)
                v.tensor_reduce(mx[:, 2 * pr:2 * pr + 2, 2 * i:2 * i + 2],
                                ps[2 + i][:].rearrange("p (b n t) -> p b n t", b=2, n=2), X, ALU.max).then_inc(s["max_sb"], 1)
                if k == 3:
                    for j in range(2):
                        last = v.tensor_reduce(least[:, j:j + 1], nrm[:, :, 8 * j:8 * j + 8], XY, ALU.min)
                    last.then_inc(s["least_sb"], 1)
                if k == 7:
                    dve.wait_ge(s["least_ps"], 1)
                    dve.wait_ge(s["fw_sb"], 3)
                    link(v.tensor_reduce(least2[:, 0:2], ps[7][0:1, 256:512].rearrange("p (a t) -> p a t", a=2), X, ALU.min))
                    link(v.tensor_tensor(least2[:, 2:3], least2[:, 0:1], least2[:, 1:2], ALU.mult))
                    v.tensor_scalar(small[:], least2[:, 2:3], COS_EPS, None, ALU.is_lt).then_inc(s["small_known"], 1)
                if k == 10:
                    dve.wait_ge(s["fu_ps"], 3)
                    dve.wait_ge(s["l_b2"], 16)
                    v.tensor_tensor(fbm[:, 1, :], ps[6][:, 16:16 + NQ], fbm[:, 0, :], ALU.add).then_inc(s["fu_sb"], 1)
                    v.tensor_tensor(w2f[0:NQ + 1, :], ps[7][0:NQ + 1, 128:256], fb2[0:NQ + 1, :], ALU.add).then_inc(s["fu_sb"], 1)
                if k == 12:
                    dve.wait_ge(s["l_mask"], 16)
                    link(v.tensor_scalar(mlow[:], mk[:], -1.0, None, ALU.is_lt))

            def guarded(k):
                b, gi = divmod(k, 2)
                hs = slice(HG * gi, HG * gi + HG)
                if k:
                    dve.wait_ge(s["small_ps"], 2 * k)
                for i in range(HG):
                    v.tensor_scalar(masked[:, i * 128:(i + 1) * 128], qh[:, b, :], hm[:, 1, HG * gi + i:HG * gi + i + 1], None,
                                    ALU.mult)
                dve.wait_ge(s["small_ps"], 2 * k + 1)
                v.tensor_copy(kn, ps[6][0:NH, 128:256])
                v.tensor_tensor(an.rearrange("p (n s) -> p n s", n=HG),
                                ps[6][0:NH, 0:128].unsqueeze(1).broadcast_to([NH, HG, S]),
                                diag[0:NH, hs].unsqueeze(2).broadcast_to([NH, HG, S]), ALU.mult).then_inc(s["small_ops"], 1)
                dve.wait_ge(s["small_ps"], 2 * k + 2)
                g_count[0] += 1
                v.tensor_scalar(scaled, ps[1][:], 1.0 / COS_EPS, 1.0, ALU.mult, ALU.min).then_inc(s["small_g"], 1)
                dve.wait_ge(s["small_g"], g_count[0])
                v.tensor_tensor(fval, ps[0][:], scaled, ALU.mult).then_inc(s["small_f"], 1)
                dve.wait_ge(s["small_sin"], k + 1)
                g_count[0] += 1
                v.scalar_tensor_tensor(group(k), group(k), 10.0, fval, ALU.add, ALU.mult).then_inc(s["small_g"], 1)
                dve.wait_ge(s["small_g"], g_count[0])

            g_count = [0]
            with v.If(v.value_load(small[0:1, 0:1]) > 0):
                for k in range(GROUPS):
                    guarded(k)

            def arg(k):
                dve.wait_ge(s["dot_ps"], k + 1)
                if k == 0:
                    dve.wait_ge(s["cos_g"], GROUPS)
                v.scalar_tensor_tensor(group(k), group(k), 0.05, ps[k % 2][:], ALU.mult, ALU.add).then_inc(s["arg_sb"], 1)

            def divide(b):
                dve.wait_ge(s["oT_ps"], b + 1)
                o = ps[4 + b % 2][:, 0:256].rearrange("p (n c) -> p n c", c=32)
                link(v.reciprocal(rec[:, b % 2, :], o[:, :, HD]))
                v.tensor_tensor(at[:, b % 2, :].rearrange("p (n d) -> p n d", d=HD), o[:, :, 0:HD],
                                rec[:, b % 2, :].unsqueeze(2).broadcast_to([128, NH, HD]), ALU.mult).then_inc(s["at_sb"], 1)

            def resid(b):
                dve.wait_ge(s["y_ps"], b + 1)
                if b == 0:
                    dve.wait_ge(s["xb_done"], 1)
                v.tensor_tensor(y1[:, b, :], ps[4 + b % 2][:, 384:512], xn[:, b, :], ALU.add).then_inc(s["y_sb"], 1)

            def by_query(a8):
                return a8.unsqueeze(2).broadcast_to([128, PAIR, NE])

            def stage(j, p):
                pb = batches(p)
                bs = range(pb.start, pb.stop)
                if j == 0:
                    dve.wait_ge(s["y_sb"], PAIR * (p + 1))
                    stats(1, y1, p)
                    means_wait(1, p)
                    for b in bs:
                        last = v.scalar_tensor_tensor(y1[:, b, :], y1[:, b, :], mv[:, 1, b, 0:1], g1r[:], ALU.subtract, ALU.mult)
                    last.then_inc(s["y1_sb"], 1)
                if j == 1:
                    rstd_wait(1, p)
                    dve.wait_ge(s["y1_sb"], p + 1)
                    for b in bs:
                        last = v.scalar_tensor_tensor(x1[:, b, :], y1[:, b, :], rstd[:, 1, b:b + 1], be1r[:], ALU.mult, ALU.add)
                    link(last)
                if j == 2:
                    dve.wait_ge(s["qm_ps"], p + 1)
                    if p == 0:
                        dve.wait_ge(s["fu_sb"], 3)
                    for b in bs:
                        last = v.scalar_tensor_tensor(ffs[:, 0, b, :], product(p)[:, 0, (b % PAIR) * NQ:(b % PAIR + 1) * NQ],
                                                      rstd[:, 1, b:b + 1], fbm[:, 1, :], ALU.mult, ALU.add)
                    last.then_inc(s["qm_sb"], 1)
                if j == 4:
                    dve.wait_ge(s["ff_ps"], p + 1)
                    link(v.tensor_tensor(y1[:, pb, :], product(p), x1[:, pb, :], ALU.add))
                    stats(2, y1, p)
                if j == 5:
                    rstd_wait(2, p)
                    for b in bs:
                        last = v.scalar_tensor_tensor(y1[:, b, :], y1[:, b, :], mv[:, 2, b, 0:1], g2r[:], ALU.subtract, ALU.mult)
                    link(last)
                    for b in bs:
                        last = v.scalar_tensor_tensor(xs[:, b, :], y1[:, b, :], rstd[:, 2, b:b + 1], xs[:, b, :], ALU.mult, ALU.add)
                    link(last)
                    stats(3, xs, p)
                    means_wait(3, p)
                    for b in bs:
                        last = v.tensor_scalar(x1[:, b, :], xs[:, b, :], mv[:, 3, b, 0:1], None, ALU.subtract)
                    last.then_inc(s["xn3_sb"], 1)
                if j == 7:
                    dve.wait_ge(s["lg_ps"], p + 1)
                    rstd_wait(3, p)
                    for b in bs:
                        last = v.tensor_scalar(lg_[:, b, :], product(p)[:, b % PAIR, :], rstd[:, 3, b:b + 1], 1.0 / math.sqrt(D),
                                               ALU.mult, ALU.mult)
                    link(last)
                    link(v.copy_predicated(lg_[:, pb, :], mlow[:, pb, :], mk[:, pb, :]))
                    v.tensor_reduce(ngm[:, pb], lg_[:, pb, :], X, ALU.max, negate=True).then_inc(s["lg_sb"], 1)
                if j == 8:
                    dve.wait_ge(s["ex_sb"], PAIR * (p + 1))
                    v.reciprocal(rsum[:, pb], sume[:, pb])
                    link(v.tensor_tensor(okr[:, pb], sume[:, pb], sume[:, pb], ALU.is_equal))
                if j == 9:
                    dve.wait_ge(s["pv_ps"], p + 1)
                    for b in bs:
                        last = v.scalar_tensor_tensor(y1[:, b, :], product(p)[:, b % PAIR, :],
                                                      rsum[:, b:b + 1], xs[:, b, :], ALU.mult, ALU.add)
                    link(last)
                    v.copy_predicated(xs[:, pb, :], okr[:, pb].bitcast(I32).unsqueeze(2).broadcast_to([128, PAIR, D]),
                                      y1[:, pb, :]).then_inc(s["x3_sb"], 1)
                    dve.wait_ge(s["x3_sb"], p + 1)
                    stats(4, xs, p)
                    means_wait(4, p)
                    for b in bs:
                        last = v.tensor_scalar(x1[:, b, :], xs[:, b, :], mv[:, 4, b, 0:1], None, ALU.subtract)
                    last.then_inc(s["xn4_sb"], 1)
                if j == 10:
                    rstd_wait(4, p)
                    dve.wait_ge(s["xn4_sb"], p + 1)
                    if p == 0:
                        dve.wait_ge(s["c_pay"], 1)
                    for b in bs:
                        last = v.tensor_scalar(pay[:, b, 0:D], x1[:, b, :], rstd[:, 4, b:b + 1], None, ALU.mult)
                    link(last)
                lg, t3 = rt[:, 2, pb, :], rt[:, 3, pb, :]
                m8, sum8, vm, rk, over, sl = (r1[:, i, pb] for i in range(6))
                if j == 11:
                    dve.wait_ge(s["gt_ps"], p + 1)
                    for b in bs:
                        last = v.tensor_scalar(rt[:, 2, b, :], product(p)[:, 0, (b % PAIR) * NE:(b % PAIR + 1) * NE],
                                               rstd[:, 4, b:b + 1], None, ALU.mult)
                    link(last)
                    link(v.tensor_reduce(m8, lg, X, ALU.max))
                    v.tensor_tensor(rt[:, 0, pb, :], lg, by_query(m8), ALU.subtract).then_inc(s["rx_sb"], 1)
                    link(v.tensor_tensor(t3, lg, by_query(m8), ALU.is_ge))
                    link(v.tensor_tensor(t3, t3, revi[:].unsqueeze(1).broadcast_to([128, PAIR, NE]), ALU.mult))
                    link(v.tensor_reduce(vm, t3, X, ALU.max))
                    v.tensor_tensor(ohb[:, pb, :], t3, by_query(vm), ALU.is_equal).then_inc(s["oh_sb"], 1)
                if j == 12:
                    dve.wait_ge(s["oh_sb"], p + 1)
                    if p < NPAIR - 1:
                        link(v.tensor_tensor(prev[:, (p + 1) % 2, :], ohb[:, pb.start, :], ohb[:, pb.start + 1, :], ALU.add))
                        link(v.tensor_tensor(prev[:, (p + 1) % 2, :], prev[:, (p + 1) % 2, :], prev[:, p % 2, :], ALU.add))
                    dve.wait_ge(s["re_sb"], p + 1)
                    link(v.tensor_reduce(sum8, rt[:, 1, pb, :], X, ALU.add))
                    link(v.reciprocal(pay[:, pb, D], sum8))
                    dve.wait_ge(s["rk_ps"], p + 1)
                    link(v.tensor_tensor(t3, product(p)[:, 1, 0:PAIR * NE].rearrange("p (b e) -> p b e", b=PAIR),
                                         ohb[:, pb, :], ALU.mult))
                    link(v.tensor_reduce(rk, t3, X, ALU.add))
                    v.tensor_scalar(over, rk, float(CAP), float(NOWHERE), ALU.is_gt, ALU.mult)
                    link(v.scalar_tensor_tensor(sl, vm, -float(CAP), rk, ALU.mult, ALU.add))
                    v.scalar_tensor_tensor(si[:, pb], sl, float(NE * CAP - 1), over, ALU.add, ALU.add).then_inc(s["si_sb"], 1)

            for k in range(NSLOTS):
                if k < GROUPS:
                    arg(k)
                if k % 2 == 0 and 0 <= (k - 4) // 2 < B:
                    divide((k - 4) // 2)
                if k % 2 == 0 and 0 <= (k - 6) // 2 < B:
                    resid((k - 6) // 2)
                for j, p in AT[k]:
                    stage(j, p)

            dve.wait_ge(s["o_ps"], B)
            v.memset(xdT[:, SLOTS:SLOTS + CW - CAP], 0.0).then_inc(s["xd_pad"], 1)
            for e in range(NE):
                if e % 4 == 0:
                    dve.wait_ge(s[f"back{e // 4}"], 16)
                dve.wait_ge(s["eo_ps"], e + 1)
                v.tensor_scalar(eo[:, e, :], ps[EO_BANK[e % 3]][0:CAP, 0:128], xd[:, e, D:D + 1], None,
                                ALU.mult).then_inc(s["eo_sb"], 1)

        @block.tensor
        def _(pe):
            t = nc.tensor

            def turn4(bank, src, h, done):
                for i in range(HALF):
                    last = t.transpose(ps[bank][:, i * 128:(i + 1) * 128], src[:, h * HALF + i, :], ident[:])
                last.then_inc(s[done], 1)

            pe.wait_ge(s["c_ident"], 1)
            pe.wait_ge(s["l_qk"], 32)
            t.transpose(ps[4][:, 0:128], wq, ident[:])
            t.transpose(ps[4][:, 128:256], wk, ident[:]).then_inc(s["wT_ps"], 1)
            pe.wait_ge(s["wT_sb"], 1)
            pe.wait_ge(s["wc_diag"], 1)
            for j in range(2):
                last = t.matmul(ps[5][:, 64 * j:64 * j + 64], wqT[:, j, :], wc[:], start=True, stop=True)
            last.then_inc(s["wc_ps"], 1)
            pe.wait_ge(s["l_bias"], 48)
            pe.wait_ge(s["wc_sb"], 1)
            for j in range(2):
                last = t.matmul(ps[5][:, 128 + 64 * j:192 + 64 * j], bcols[:, j:j + 1].broadcast_to([128, 128]), wc[:],
                                start=True, stop=True)
            last.then_inc(s["wc_ps"], 1)
            for h in range(NHALF):
                pe.wait_ge(s["xn_done"], HALF * (h + 1))
                turn4(2 + h, xn, h, "tT_ps")
            for h in range(NHALF):
                pe.wait_ge(s["tT_sb"], h + 1)
                pe.wait_ge(s["wc_sb"], h + 1)
                for i in range(HALF):
                    last = t.matmul(ps[4 + h][:, i * 128:(i + 1) * 128], tT[:, h * HALF + i, :], wqk, start=True, stop=True)
                last.then_inc(s["qk_ps"], 1)
            for h in range(NHALF):
                if h:
                    pe.wait_ge(s["q_sb"], h)
                tcols = tT[:, h * HALF:(h + 1) * HALF, :].rearrange("p b s -> p (b s)")
                t.matmul(ps[6][:], wq, tcols, start=True, stop=True).then_inc(s["proj_ps"], 1)
                if h:
                    pe.wait_ge(s["k_sb"], h)
                t.matmul(ps[7][:], wk, tcols, start=True, stop=True).then_inc(s["proj_ps"], 1)
                pe.wait_ge(s["l_v"], 16)
                for i in range(HALF):
                    last = t.matmul(ps[2 + h][:, i * 128:(i + 1) * 128], tT[:, h * HALF + i, :], wv, start=True, stop=True)
                last.then_inc(s["v_ps"], 1)

            pe.wait_ge(s["pad_done"], 1)
            turn4(0, qpad, 0, "hT_ps")
            pe.wait_ge(s["pad_done"], 2)
            turn4(1, kpad, 0, "hT_ps")
            pe.wait_ge(s["q_sb"], 2)
            pe.wait_ge(s["pad_done"], 3)
            turn4(6, qpad, 1, "hT_ps")
            pe.wait_ge(s["k_sb"], 2)
            pe.wait_ge(s["pad_done"], 4)
            turn4(7, kpad, 1, "hT_ps")

            def max_scores(u):
                pr, i = divmod(u, 4)
                if u >= 4:
                    pe.wait_ge(s["max_sb"], u - 3)
                elif u >= 2:
                    pe.wait_ge(s["pad_done"], 2 * (u - 1))
                else:
                    pe.wait_ge(s["v_sb"], u + 1)
                pe.wait_ge(s["lowp"], 3 * (pr // 2 + 1))
                rows = slice(32 * i, 32 * i + 32)
                for c in range(4):
                    b, par = 2 * pr + c // 2, c % 2
                    last = t.matmul(ps[2 + i][:, c * 128:(c + 1) * 128], qTb[rows, b, :], kTb[rows, par, b, :], start=True, stop=True)
                last.then_inc(s["max_ps"], 1)

            def turn_maxima(h):
                pe.wait_ge(s["max_sb"], 8 * (h + 1))
                pe.wait_ge(s["fu_sb"], 3)
                t.transpose(ps[6 + h][0:32, 0:128], mx[:, h * HALF:(h + 1) * HALF, :].rearrange("p b n -> p (b n)"),
                            ident[:]).then_inc(s["mT_ps"], 1)

            pe.wait_ge(s["hT_sb"], 2)
            for k in range(GROUPS):
                b, gi = divmod(k, 2)
                h, bb = divmod(b, HALF)
                pe.wait_ge(s[f"cosm{h}"], HG * (gi + 1))
                if k >= 2:
                    pe.wait_ge(s["cos_g"], k - 1)
                t.matmul(ps[k % 2][:], kh[:, b, :], cosm[h][:, bb, HG * gi:HG * gi + HG, :].rearrange("p n s -> p (n s)"),
                         start=True, stop=True).then_inc(s["cos_ps"], 1)
                max_scores(k)
                if k == 3:
                    pe.wait_ge(s["l_ffw"], 16 * 8)
                    pe.wait_ge(s["hT_sb"], 3)
                    for c in range(4):
                        last = t.transpose(ps[6][:, c * 128:(c + 1) * 128], fw1[:, c:FF:4], ident[:])
                    last.then_inc(s["fw_ps"], 1)
                if k == 5:
                    pe.wait_ge(s["hT_sb"], 4)
                    pe.wait_ge(s["l_gate"], 16)
                    for c in range(4):
                        t.transpose(ps[7][:, c * NQ:(c + 1) * NQ], fwqo[:, c:FF:4], ident[0:NQ, 0:NQ])
                    t.transpose(ps[7][:, 64:64 + NE], gw, ident[0:NE, 0:NE]).then_inc(s["fw_ps"], 1)
                    pe.wait_ge(s["least_sb"], 1)
                    for j in range(2):
                        last = t.transpose(ps[7][0:1, 256 + 128 * j:384 + 128 * j], least[:, j:j + 1], ident[:])
                    last.then_inc(s["least_ps"], 1)
                if k == 7:
                    pe.wait_ge(s["fw_sb"], 3)
                    for c in range(4):
                        last = t.matmul(ps[6][:, 0:NQ], fw1T[:, c, :], fwm[:, c, :], start=(c == 0), stop=(c == 3))
                    last.then_inc(s["fu_ps"], 1)
                if k == 13:
                    turn_maxima(0)
                if k == 9:
                    pe.wait_ge(s["fu_sb"], 1)
                    for c in range(4):
                        t.matmul(ps[6][:, 16:16 + NQ], fb1[:, c:c + 1].broadcast_to([128, 128]), fwm[:, c, :],
                                 start=(c == 0), stop=False)
                    t.matmul(ps[6][:, 16:16 + NQ], bcols[:, 3:4].broadcast_to([128, 128]), w1m[:],
                             start=False, stop=True).then_inc(s["fu_ps"], 1)
                if k == 8:
                    pe.wait_ge(s["small_known"], 1)
                    pe.wait_ge(s["fw_sb"], 3)
                    for c in range(4):
                        last = t.matmul(ps[7][0:NQ + 1, 128:256], fwqoT[:, :, c], fw2[:, c, :], start=(c == 0), stop=(c == 3))
                    last.then_inc(s["fu_ps"], 1)
            pe.wait_ge(s["fu_sb"], 3)
            with t.If(t.value_load(small[0:1, 0:1]) > 0):
                pe.wait_ge(s["cos_g"], GROUPS)
                for k in range(GROUPS):
                    b, gi = divmod(k, 2)
                    if k:
                        pe.wait_ge(s["small_g"], 2 * k)
                    for j in range(2):
                        last = t.transpose(ps[6][0:NH, 128 * j:128 * j + 128], nrm[:, b, 8 * j:8 * j + 8], ident[:])
                    last.then_inc(s["small_ps"], 1)
                    pe.wait_ge(s["small_ops"], k + 1)
                    t.matmul(ps[1][:], kn, an, start=True, stop=True)
                    t.matmul(ps[0][:], kh[:, b, :], masked, start=True, stop=True).then_inc(s["small_ps"], 1)
                pe.wait_ge(s["small_g"], 2 * GROUPS)
            turn_maxima(1)

            def dots(k):
                b, gi = divmod(k, 2)
                h, bb = divmod(b, HALF)
                pe.wait_ge(s[f"dotm{h}"], NH)
                pe.wait_ge(s["bd_sb"], NH * h + HG * (gi + 1))
                if k >= 2:
                    pe.wait_ge(s["arg_sb"], k - 1)
                else:
                    pe.wait_ge(s["cos_g"], GROUPS - 1 + k)
                t.matmul(ps[k % 2][:], kT[:, b, :], dotm[h][:, bb, HG * gi:HG * gi + HG, :].rearrange("p n s -> p (n s)"),
                         start=True, stop=False)
                t.matmul(ps[k % 2][:], negsel[:, bb, :], bd[:, h, HG * gi:HG * gi + HG, :].rearrange("p n s -> p (n s)"),
                         start=False, stop=True).then_inc(s["dot_ps"], 1)

            def pv(k):
                b, gi = divmod(k, 2)
                pe.wait_ge(s["exp_sb"], k + 1)
                if gi == 0:
                    if b >= 2:
                        pe.wait_ge(s["o_sb"], b - 1)
                    else:
                        pe.wait_ge(s["max_sb"], GROUPS)
                for i in range(HG):
                    n = HG * gi + i
                    last = t.matmul(ps[2 + b % 2][32 * i:32 * i + 32, gi * 128:gi * 128 + 128], va[:, b, n, :], G[:, b, n, :],
                                    start=True, stop=True)
                if gi:
                    last.then_inc(s["o_ps"], 1)

            def turn_out(b):
                pe.wait_ge(s["o_sb"], b + 1)
                if b >= 2:
                    pe.wait_ge(s["y_sb"], b - 1)
                for gi in range(2):
                    last = t.transpose(ps[4 + b % 2][:, gi * 128:gi * 128 + 128], ob[:, b % 2, gi, :], ident[:])
                last.then_inc(s["oT_ps"], 1)

            def turn_att(b):
                pe.wait_ge(s["at_sb"], b + 1)
                t.transpose(ps[4 + b % 2][:, 256:384], at[:, b % 2, :], ident[:]).then_inc(s["atT_ps"], 1)

            def project(b):
                pe.wait_ge(s["atT_sb"], b + 1)
                if b == 0:
                    pe.wait_ge(s["l_wo"], 16)
                t.matmul(ps[4 + b % 2][:, 384:512], atT[:, b % 2, :], wo[:], start=True, stop=True).then_inc(s["y_ps"], 1)

            def turn2(p, src, done):
                for i in range(PAIR):
                    last = t.transpose(turned(p)[:, i, :], src[:, p * PAIR + i, 0:128], ident[:])
                last.then_inc(s[done], 1)

            def stage(j, p):
                bs = range(p * PAIR, (p + 1) * PAIR)
                if j == 1:
                    pe.wait_ge(s["y1_sb"], p + 1)
                    pe.wait_ge(*((s["ctxT_sb"], 2) if p < 2 else (s["arg_sb"], GROUPS)))
                    turn2(p, y1, "y1T_ps")
                if j == 2:
                    pe.wait_ge(s["y1T_sb"], p + 1)
                    pe.wait_ge(s["fu_sb"], 3)
                    for b in bs:
                        last = t.matmul(product(p)[:, 0, (b % PAIR) * NQ:(b % PAIR + 1) * NQ], tT[:, b, :], w1m[:], start=True, stop=True)
                    last.then_inc(s["qm_ps"], 1)
                if j == 3:
                    pe.wait_ge(s["qe_sb"], p + 1)
                    for b in bs:
                        last = t.transpose(turned(p)[0:NQ, b % PAIR, :], ffs[:, 5, b, :], ident[:])
                    last.then_inc(s["qeT_ps"], 1)
                if j == 4:
                    pe.wait_ge(s["qeT_sb"], p + 1)
                    for b in bs:
                        last = t.matmul(product(p)[:, b % PAIR, :], qeT[:, p % 2, (b % PAIR) * 128:(b % PAIR + 1) * 128], w2f[:],
                                        start=True, stop=True)
                    last.then_inc(s["ff_ps"], 1)
                if j == 6:
                    pe.wait_ge(s["xn3_sb"], p + 1)
                    turn2(p, x1, "x3T_ps")
                if j == 7:
                    pe.wait_ge(s["x3T_sb"], p + 1)
                    for b in bs:
                        last = t.matmul(product(p)[:, b % PAIR, :], tT[:, b, :], cxT[:, b, :], start=True, stop=True)
                    last.then_inc(s["lg_ps"], 1)
                if j == 8:
                    pe.wait_ge(s["ex_sb"], PAIR * (p + 1))
                    turn2(p, lg_, "pT_ps")
                if j == 9:
                    pe.wait_ge(s["pT_sb"], p + 1)
                    for b in bs:
                        last = t.matmul(product(p)[:, b % PAIR, :], pT[:, b, :], cx[:, b, :], start=True, stop=True)
                    last.then_inc(s["pv_ps"], 1)
                if j == 10:
                    pe.wait_ge(s["xn4_sb"], p + 1)
                    turn2(p, x1, "x4T_ps")
                if j == 11:
                    pe.wait_ge(s["x4T_sb"], p + 1)
                    for b in bs:
                        last = t.matmul(product(p)[:, 0, (b % PAIR) * NE:(b % PAIR + 1) * NE], tT[:, b, :], gwT[:], start=True, stop=True)
                    last.then_inc(s["gt_ps"], 1)
                if j == 12:
                    pe.wait_ge(s["oh_sb"], p + 1)
                    rank = product(p)[:, 1, 0:PAIR * NE].rearrange("p (b e) -> p b e", b=PAIR)
                    t.matmul(rank, tri[:], ohb[:, batches(p), :], start=True, stop=False, skip_group_check=True)
                    t.matmul(rank[:, 1, :], onesb[:], ohb[:, p * PAIR, :], start=False, stop=False, skip_group_check=True)
                    if p:
                        pe.wait_ge(s["si_sb"], p)
                    last = t.matmul(rank, onesb[:], prev[:, p % 2, :].unsqueeze(1).broadcast_to([128, PAIR, NE]),
                                    start=False, stop=True, skip_group_check=True)
                    last.then_inc(s["rk_ps"], 1)

            for k in range(NSLOTS):
                if k < GROUPS:
                    dots(k)
                if 1 <= k <= GROUPS:
                    pv(k - 1)
                if k in (1, 9):
                    pe.wait_ge(s["l_ctx"], 16)
                    turn4(6 + k // 9, cx, k // 9, "ctxT_ps")
                if k % 2 == 0 and 0 <= (k - 4) // 2 < B:
                    turn_out((k - 4) // 2)
                if k % 2 == 1 and 0 <= (k - 5) // 2 < B:
                    turn_att((k - 5) // 2)
                if k % 2 == 0 and 0 <= (k - 6) // 2 < B:
                    project((k - 6) // 2)
                for j, p in AT[k]:
                    stage(j, p)

            for q in range(4):
                pe.wait_ge(s[f"back{q}"], 16)
                if q >= 2:
                    pe.wait_ge(s["xdT_sb"], q)
                for i in range(4):
                    last = t.transpose(ps[2 + q % 2][:, i * CAP:(i + 1) * CAP], xd[:, 4 * q + i, 0:D], ident[0:CAP, 0:CAP])
                last.then_inc(s["xdT_ps"], 1)

            def hidden(e):
                if e == 0:
                    pe.wait_ge(s["xdT_sb"], 4)
                    pe.wait_ge(s["xd_pad"], 1)
                if e % 4 == 0:
                    pe.wait_ge(s["l_w1"], 16 * 4)
                if e >= 3:
                    pe.wait_ge(s["hid_sb"], e - 2)
                for c in range(4):
                    last = t.matmul(ps[5 + e % 3][:, c * CW:(c + 1) * CW], w1s[:, e, c * 128:(c + 1) * 128],
                                    xdT[:, e * CAP:e * CAP + CW], start=True, stop=True)
                last.then_inc(s["hid_ps"], 1)

            def expert_out(e):
                pe.wait_ge(s["hid_sb"], e + 1)
                if e == 0:
                    pe.wait_ge(s["l_w2"], 16 * 4)
                if e >= 3:
                    pe.wait_ge(s["eo_sb"], e - 2)
                for c in range(4):
                    last = t.matmul(ps[EO_BANK[e % 3]][0:CAP, 0:128], hT[:, e % 3, c, :], w2s[:, e, c, :],
                                    start=(c == 0), stop=(c == 3))
                last.then_inc(s["eo_ps"], 1)

            for e in range(NE + 1):
                if e < NE:
                    hidden(e)
                if e:
                    expert_out(e - 1)


_INS = ['x', 'ctx_1024', 'mask_BxSxS2_fk0'] + ['L0_attn_' + n for n in (
    'Wq', 'bq', 'Wk', 'bk', 'Wv', 'bv', 'Wc2q', 'bc2q', 'Wo', 'bo', 'g1', 'beta1', 'g2', 'beta2', 'W1', 'b1',
    'Wm', 'bm', 'Wqo', 'bqo', 'W2', 'b2')] + ['L0_ffn_gate_w', 'L0_ffn_w1', 'L0_ffn_w2']


def kernel(**inputs):
    import concourse.bacc as _bacc
    from concourse.bass_utils import run_bass_kernel_spmd as _run

    nc = _bacc.Bacc("TRN2", target_bir_lowering=False, num_devices=1)
    arrays, args = {}, []
    for name in _INS:
        a = np.ascontiguousarray(inputs[name])
        arrays[f"in_{name}"] = a
        args.append(nc.dram_tensor(f"in_{name}", a.shape, mybir.dt.from_np(a.dtype), kind="ExternalInput").ap())
    out = nc.dram_tensor("out_0", (B, S, D), F32, kind="ExternalOutput").ap()
    decoder_block(nc, *args, out)
    r = _run(nc, [arrays], core_ids=[0])
    return r.results[0]["out_0"]
```

```python
import math
from contextlib import ExitStack

import numpy as np

import concourse.bass as bass
from concourse import mybir

F32 = mybir.dt.float32
BF16 = mybir.dt.bfloat16
I32 = mybir.dt.int32
U8 = mybir.dt.uint8
U32 = mybir.dt.uint32
ALU = mybir.AluOpType
ACT = mybir.ActivationFunctionType
X = mybir.AxisListType.X
XY = mybir.AxisListType.XY

B, S, D = 8, 128, 128
NH, HD, NQ = 8, 16, 8
FF = 512
NE, DFF = 16, 512
TOK = B * S
CAP = math.floor(1.25 * TOK / NE)
CAP = max(CAP + CAP % 2, 4)
SLOTS = NE * CAP
SC = SLOTS // 128
CW = 96
HALF = 4
NHALF = B // HALF
HG = 4
GROUPS = B * NH // HG
LN_EPS = 1e-05
COS_EPS = 1e-08
PI_IN = float(np.float32(math.pi * (1 - 2.0 ** -21)))
PAIR = 2
NPAIR = B // PAIR
ROW = 2 * D + 2
NOWHERE = 4 * TOK
COS = [0.999999999885, -4.93480218577, 4.05871181578, -1.3352602774, 0.23532080051, -0.0257857720901, 0.00190430229777, -8.86833217906e-05]
ROUND = 12582912.0


def decoder_block(nc, x, ctx_in, mask, Wq, bq, Wk, bk, Wv, bv, Wc, bc, Wo, bo, g1, beta1, g2, beta2,
                  W1, b1, Wm, bm, Wqo, bqo, W2, b2, gate_w, w1, w2, out):
    st = ExitStack()
    with st:
        def sb(name, shape, dt=F32):
            return st.enter_context(nc.sbuf_tensor(name, shape, dt))

        def sem(name):
            return st.enter_context(nc.semaphore(name))

        xs = sb("xs", [128, B, D])
        cx = sb("cx", [128, B, D])
        mk = sb("mk", [128, B, S])
        mlow = sb("mlow", [128, B, S], U8)
        xn = sb("xn", [128, B, D])
        tT = sb("tT", [128, B, S])
        qT = sb("qT", [128, B, S])
        kT = sb("kT", [128, B, S])
        qTb = sb("qTb", [128, B, S], BF16)
        kTb = sb("kTb", [128, 2, B, S], BF16)
        qh = sb("qh", [128, B, S])
        kh = sb("kh", [128, B, S])
        cxT = kh
        va = sb("va", [128, B, NH, HD + 1])
        md = sb("md", [128, 3 * HALF * NH * S])
        G = sb("G", [128, B, NH, S])
        w1s = sb("w1s", [128, NE, DFF])
        w2s = sb("w2s", [128, NE, DFF // 128, D])

        def group(k):
            return G[:, k // 2, HG * (k % 2):HG * (k % 2) + HG, :].rearrange("p n s -> p (n s)")

        def slot(i):
            return md[:, i * HALF * NH * S:(i + 1) * HALF * NH * S]

        def heads(i):
            return slot(i).rearrange("p (b n s) -> p b n s", b=HALF, n=NH)
        cosm = [heads(0), heads(1)]
        dotm = [heads(2), heads(0)]
        early = slot(2).rearrange("p (a b c) -> p a b c", a=4, b=B)
        qk, sq, qpad, kpad = (early[:, i] for i in range(4))
        late = slot(1).rearrange("p (a b c) -> p a b c", a=4, b=B)
        y1, x1, lg_, pT = (late[:, i] for i in range(4))

        wq, wk, wv, wqk, bqkr, bvr = (G[:, B - 3, i, :] for i in range(6))
        wqT = G[:, B - 3, 6:8, :]
        gw = G[0:NE, B - 4, 0, :]
        wc = sb("wc", [128, 64])
        wcs = sb("wcs", [128, NQ])
        bcr = G[:, 3, 6, 0:64]
        bcols = sb("bcols", [128, 4])
        bor = sb("bor", [128, 128])
        g1r = sb("g1r", [128, 128])
        g2r = sb("g2r", [128, 128]); be2r = sb("be2r", [128, 128])
        wo = sb("wo", [128, 128])
        fw1, fwqo = G[:, B - 2, 0:4, :].rearrange("p n s -> p (n s)"), G[0:NQ, B - 1, 0:4, :].rearrange("p n s -> p (n s)")
        fw1T, fw2 = G[:, B - 2, 4:8, :], G[:, B - 1, 4:8, :]
        fwm = sb("fwm", [128, 4, NQ]); fb1 = sb("fb1", [128, 4]); fbm = sb("fbm", [128, 2, NQ])
        fwqoT = sb("fwqoT", [128, NQ + 1, 4])
        w1m = sb("w1m", [128, NQ])
        w2f = sb("w2f", [128, 128])
        fb2 = sb("fb2", [NQ + 1, 2, 128])
        gwT = sb("gwT", [128, NE])
        ident = sb("ident", [128, 128])
        tri = sb("tri", [128, 128], BF16); onesb = sb("onesb", [128, 128], BF16)
        hm = sb("hm", [128, 2, NH])
        evod = sb("evod", [128, 2])
        diag = sb("diag", [32, NH])
        negsel = sb("negsel", [32, HALF, 128], BF16)
        revi = sb("revi", [128, NE])
        blank = sb("blank", [128, ROW])
        prev = sb("prev", [128, 2, NE], BF16)
        mhalf = sb("mhalf", [128, 8])

        bns = sb("bns", [128, B, 6]); mv = sb("mv", [128, 5, B, 2])
        ve = sb("ve", [128, 5, B]); rstd = sb("rstd", [128, 5, B])
        nr = G[:, 3, 0:5, :].rearrange("p a s -> p (a s)").rearrange("p (i b c) -> p i b c", i=5, b=B)
        nrm = sb("nrm", [128, B, 16])
        mx = sb("mx", [128, B, NH])
        bd = tT[0:32].rearrange("p b s -> p (b s)").bitcast(BF16).rearrange("p (h n s) -> p h n s", h=NHALF, n=NH)
        at, atT = qh[:, 4:6, :], qh[:, 6:8, :]
        rec = sb("rec", [128, 2, NH])
        qeT = sb("qeT", [128, 2, PAIR * S])
        pay = slot(2)[:, 0:B * ROW].rearrange("p (b r) -> p b r", b=B)
        rt = slot(2)[:, B * ROW:B * ROW + 4 * B * NE].rearrange("p (i b e) -> p i b e", i=4, b=B)
        ffs = slot(2)[:, 3000:3000 + 10 * B * NQ].rearrange("p (i b q) -> p i b q", i=10, b=B)
        ngm = sb("ngm", [128, B]); sume = sb("sume", [128, B]); rsum = sb("rsum", [128, B])
        okr = sb("okr", [128, B])
        ohb = sb("ohb", [128, B, NE], BF16)
        r1 = sb("r1", [128, 8, B]); si = sb("si", [128, B], U32)

        least = sb("least", [128, 2]); least2 = sb("least2", [1, 4]); small = sb("small", [1, 1], I32)
        redo = slot(1).rearrange("p (i c) -> p i c", i=8)
        masked, scaled, fval = redo[:, 0], redo[:, 1], redo[:, 2]
        kn, an = redo[0:NH, 3, 0:128], redo[0:NH, 4]

        Gf = G[:].rearrange("p b n s -> p (b n s)")
        xd = Gf[0:CAP, 0:NE * ROW].rearrange("p (e r) -> p e r", e=NE)
        xdT = Gf[:, 4608:4608 + SLOTS + CW - CAP]
        hT = Gf[:, 6144:6144 + 3 * 4 * CAP].rearrange("p (r c k) -> p r c k", r=3, c=4)
        eo = slot(0)[0:CAP, 0:NE * 128].rearrange("p (e d) -> p e d", e=NE)

        ps = [st.enter_context(nc.psum_tensor(f"bank{i}", [128, 512], F32)) for i in range(8)]

        def quads(i):
            return ps[i][:].rearrange("p (b s) -> p b s", b=4)

        toks = nc.dram_tensor("slot_tokens", [SLOTS, ROW], F32, kind="Internal").ap()

        names = """l_x0 l_x1 l_qk l_v l_wc wc_diag l_bias l_rows l_wo l_ffw l_ctx l_mask l_gate l_w1 l_w2 l_b2 zrow
            c_ident c_zero c_half c_rest c_pay rstd_done pool_step
            xn_done tT_ps tT_sb wT_ps wT_sb wc_ps wc_sb qk_ps proj_ps q_sb k_sb v_ps v_sb lowp pad_done hT_ps hT_sb
            cosm0 cosm1 dotm0 dotm1 cos_ps sin_sb cos_g max_ps max_sb mT_ps bd_sb
            dot_ps arg_sb exp_sb o_ps at_sb atT_ps atT_sb y_ps y_sb xb_done mlow_done
            ln_st y1_sb y1T_ps y1T_sb qm_ps qm_sb th_sb qe_sb qeT_ps qeT_sb ff_ps xn3_sb x3T_ps x3T_sb
            lg_ps lg_raw lg_sb ex_sb pT_ps pT_sb pv_ps xn4_sb x4T_ps x4T_sb gt_ps oh_sb rx_sb re_sb rk_ps si_sb
            fw_ps fw_sb fu_ps fu_sb ctxT_ps ctxT_sb
            sent back0 back1 back2 back3 back_res0 back_res1 pay_res xdT_ps xdT_sb xd_pad hid_ps hid_sb eo_ps eo_sb routed stored dch ach
            least_sb least_ps small_known small_ops small_ps small_f small_sin small_g""".split()
        s = {n: sem(n) for n in names}

        block = st.enter_context(nc.Block())

        STAGE_SLOTS = [[8, 10, 11, 13, 14, 15, 17, 18, 19, 20, 21, 22, 23],
                       [12, 13, 13, 15, 16, 17, 18, 19, 21, 22, 23, 24, 25],
                       [14, 15, 16, 19, 20, 21, 22, 23, 24, 25, 27, 28, 29],
                       [18, 19, 20, 22, 23, 24, 25, 26, 27, 28, 29, 30, 31]]
        NSLOTS = max(GROUPS + 4, 1 + max(when[-1] for when in STAGE_SLOTS))
        AT = [[(stage, pair) for pair in range(NPAIR) for stage, at_slot in enumerate(STAGE_SLOTS[pair]) if at_slot == k]
              for k in range(NSLOTS)]
        NORM_OF_STAGE = {0: 1, 4: 2, 5: 3, 9: 4}
        NORMS = [(0, h) for h in range(NHALF)] + [(NORM_OF_STAGE[j], p) for k in range(NSLOTS) for j, p in AT[k]
                                                  if j in NORM_OF_STAGE]

        def norm_count(i, u):
            return NORMS.index((i, u)) + 1

        def norm_batches(i, u):
            return slice(u * HALF, (u + 1) * HALF) if i == 0 else slice(u * PAIR, (u + 1) * PAIR)

        COS_BANK = [0, 1, 4, 5]
        XD_BANK = [2, 3, 0, 1]
        EO_BANK = [0, 1, 4]
        PAIR_BANK = [6, 7, 0, 1]

        def turned(p):
            return ps[PAIR_BANK[p]][:, 0:PAIR * 128].rearrange("p (b s) -> p b s", b=PAIR)

        def product(p):
            return ps[PAIR_BANK[p]][:, PAIR * 128:2 * PAIR * 128].rearrange("p (b s) -> p b s", b=PAIR)

        def batches(p):
            return slice(p * PAIR, (p + 1) * PAIR)

        def row(v):
            return v.rearrange("(a n) -> a n", a=1)

        @block.sync
        def _(sp):
            def load_x(h):
                hb = slice(h * HALF, (h + 1) * HALF)
                sp.dma_start(xs[:, hb, :], x[hb].rearrange("b s d -> s b d")).then_inc(s[f"l_x{h}"], 16)

            def load_projection(dst, src, done):
                sp.dma_start(dst[:].rearrange("p (n d) -> p n d", n=NH),
                             src.rearrange("n h d -> h n d")).then_inc(s[done], 16)

            load_x(0)
            load_projection(wq, Wq, "l_qk")
            load_projection(wk, Wk, "l_qk")
            load_x(1)
            load_projection(wv, Wv, "l_v")
            for dst, src in ((bvr, bv.rearrange("n d -> (n d)")), (bor, bo), (g1r, g1), (g2r, g2), (be2r, beta2)):
                sp.dma_start(dst[:], row(src).broadcast_to([128, 128])).then_inc(s["l_rows"], 16)
            sp.dma_start(fw1, W1).then_inc(s["l_ffw"], 16)
            sp.dma_start(fwm[:], Wm.rearrange("(p c) q -> p c q", c=4)).then_inc(s["l_ffw"], 16)
            sp.dma_start(fb1[:], b1.rearrange("(p c) -> p c", c=4)).then_inc(s["l_ffw"], 16)
            sp.dma_start(fbm[:, 0, :], row(bm).broadcast_to([128, NQ])).then_inc(s["l_ffw"], 16)
            sp.dma_start(bcols[:, 3:4], beta1.rearrange("(p a) -> p a", a=1)).then_inc(s["l_ffw"], 16)
            sp.dma_start(fwqo, Wqo).then_inc(s["l_ffw"], 16)
            sp.dma_start(fwqoT[:, NQ, :], bqo.rearrange("(p c) -> p c", c=4)).then_inc(s["l_ffw"], 16)
            sp.dma_start(fw2, W2.rearrange("(p c) d -> p c d", c=4)).then_inc(s["l_ffw"], 16)
            sp.dma_start(gw, gate_w).then_inc(s["l_gate"], 16)
            sp.dma_start(wo[:], Wo).then_inc(s["l_wo"], 16)
            sp.wait_ge(s["c_zero"], 2)
            sp.dma_start(fb2[NQ:NQ + 1, 0, :], row(b2)).then_inc(s["l_b2"], 16)
            sp.dma_start(fb2[NQ:NQ + 1, 1, :], row(beta1)).then_inc(s["l_b2"], 16)
            sp.wait_ge(s["l_rows"], 16 * 5)
            sp.wait_ge(s["l_ffw"], 16 * 8)
            sp.dma_start(cx[:], ctx_in.rearrange("b t d -> t b d")).then_inc(s["l_ctx"], 16)
            sp.dma_start(mk[:], mask.rearrange("b s t -> s b t")).then_inc(s["l_mask"], 16)
            for e in range(0, NE, 4):
                sp.dma_start(w1s[:, e:e + 4, :], w1[e:e + 4].rearrange("e d f -> d e f")).then_inc(s["l_w1"], 16)
                sp.dma_start(w2s[:, e:e + 4], w2[e:e + 4].rearrange("e (c p) d -> p e c d", p=128)).then_inc(s["l_w2"], 16)
            sp.dma_start(toks.rearrange("(c p) r -> p c r", p=128),
                         blank[:].unsqueeze(1).broadcast_to([128, SC, ROW])).then_inc(s["zrow"], 16)
            for p in range(NPAIR):
                sp.wait_ge(s["xn4_sb"], p + 1)
                sp.dma_start(out[batches(p)].rearrange("b s d -> s b d"), xs[:, batches(p), :]).then_inc(s["stored"], 16)
            sp.wait_ge(s["sent"], 16 * B)
            sp.wait_ge(s["o_ps"], B)
            for e in range(0, NE, 4):
                sp.dma_start(xd[:, e:e + 4, 0:D + 2],
                             toks[e * CAP:(e + 4) * CAP, 0:D + 2].rearrange("(e c) r -> c e r", e=4)).then_inc(s[f"back{e // 4}"], 16)
            for h, back in enumerate(("back_res0", "back_res1")):
                es = slice(h * NE // 2, (h + 1) * NE // 2)
                sp.dma_start(xd[:, es, D + 2:ROW],
                             toks[es.start * CAP:es.stop * CAP, D + 2:ROW].rearrange("(e c) r -> c e r", c=CAP)).then_inc(s[back], 16)

        @block.gpsimd
        def _(pool):
            g = nc.gpsimd
            chain = [0]

            def link(ins):
                chain[0] += 1
                ins.then_inc(s["pool_step"], 1)
                pool.wait_ge(s["pool_step"], chain[0])

            g.memset(mhalf[:], -0.5)
            g.memset(hm[:], 1.0)
            link(g.memset(ident[:], 0.0))
            g.affine_select(out=ident[:], in_=ident[:], compare_op=ALU.not_equal, fill=1.0, base=0,
                            pattern=[[-1, 128]], channel_multiplier=1).then_inc(s["c_ident"], 1)
            for j, wdt in ((0, HD), (1, NQ)):
                link(g.affine_select(out=hm[:, j, :], in_=hm[:, j, :], compare_op=ALU.is_ge, fill=0.0, base=0,
                                     pattern=[[-wdt, NH]], channel_multiplier=1))
                link(g.affine_select(out=hm[:, j, :], in_=hm[:, j, :], compare_op=ALU.is_ge, fill=0.0,
                                     base=wdt - 1, pattern=[[wdt, NH]], channel_multiplier=-1))
            link(g.tensor_tensor(evod[:, 0:1], hm[:, 0, 0:1], hm[:, 0, 2:3], ALU.add))
            link(g.tensor_tensor(evod[:, 0:1], evod[:, 0:1], hm[:, 0, 4:5], ALU.add))
            link(g.tensor_tensor(evod[:, 0:1], evod[:, 0:1], hm[:, 0, 6:7], ALU.add))
            g.tensor_scalar(evod[:, 1:2], evod[:, 0:1], -1.0, 1.0, ALU.mult, ALU.add).then_inc(s["c_half"], 1)

            def rest_of_constants():
                g.memset(diag[:], 0.0)
                g.memset(negsel[:], -1.0)
                g.memset(tri[:], 1.0)
                g.memset(onesb[:], 1.0)
                g.memset(prev[:], 0.0)
                link(g.memset(qeT[:], 0.0))
                g.memset(va[:, :, :, HD:HD + 1], 1.0)
                for b in range(HALF):
                    link(g.affine_select(out=diag[:], in_=diag[:], compare_op=ALU.not_equal, fill=1.0, base=-b * NH,
                                         pattern=[[-1, NH]], channel_multiplier=1))
                link(g.affine_select(out=negsel[:], in_=negsel[:], compare_op=ALU.is_ge, fill=0.0, base=0,
                                     pattern=[[-NH, HALF], [0, 128]], channel_multiplier=1))
                link(g.affine_select(out=negsel[:], in_=negsel[:], compare_op=ALU.is_ge, fill=0.0, base=NH - 1,
                                     pattern=[[NH, HALF], [0, 128]], channel_multiplier=-1))
                g.affine_select(out=tri[:], in_=tri[:], compare_op=ALU.is_ge, fill=0.0, base=0,
                                pattern=[[1, 128]], channel_multiplier=-1)
                g.iota(revi[:], [[-1, NE]], base=NE, channel_multiplier=0, allow_small_or_imprecise_dtypes=True)
                g.affine_select(out=qeT[:], in_=qeT[:], compare_op=ALU.not_equal, fill=1.0, base=-NQ,
                                pattern=[[0, 2], [0, PAIR * S]], channel_multiplier=1).then_inc(s["c_rest"], 1)

            def rsqrt(i, h):
                hb = norm_batches(i, h)
                pool.wait_ge(s["ln_st"], norm_count(i, h))
                link(g.tensor_scalar(ve[:, i, hb], mv[:, i, hb, 1], LN_EPS, float(D) if i == 3 else 1.0, ALU.add, ALU.mult))
                g.tensor_tensor(rstd[:, i, hb], ve[:, i, hb], mhalf[:, 0:hb.stop - hb.start], ALU.pow).then_inc(s["rstd_done"], 1)

            def cosine_of(p):
                qm, th, u, z, z2, qe, even, odd, low, high = (ffs[:, i, batches(p), :] for i in range(10))
                pool.wait_ge(s["qm_sb"], p + 1)
                link(g.tensor_scalar(u, qm, 0.125, ROUND, ALU.mult, ALU.add))
                link(g.tensor_scalar(u, u, ROUND, 8.0, ALU.subtract, ALU.mult))
                link(g.tensor_tensor(u, qm, u, ALU.subtract))
                link(g.tensor_tensor(z, u, u, ALU.mult))
                link(g.tensor_scalar(z, z, 1.0 / 16, 1.0, ALU.mult, ALU.min))
                g.tensor_tensor(z2, z, z, ALU.mult)
                g.tensor_scalar(odd, z, COS[7], COS[6], ALU.mult, ALU.add)
                g.tensor_scalar(even, z, COS[3], COS[2], ALU.mult, ALU.add)
                g.tensor_scalar(high, z, COS[5], COS[4], ALU.mult, ALU.add)
                link(g.tensor_scalar(low, z, COS[1], COS[0], ALU.mult, ALU.add))
                g.tensor_tensor(odd, odd, z2, ALU.mult)
                g.tensor_tensor(even, even, z2, ALU.mult)
                link(g.tensor_tensor(z2, z2, z2, ALU.mult))
                g.tensor_tensor(high, high, odd, ALU.add)
                link(g.tensor_tensor(low, low, even, ALU.add))
                link(g.tensor_tensor(high, high, z2, ALU.mult))
                link(g.tensor_tensor(low, low, high, ALU.add))
                pool.wait_ge(s["th_sb"], p + 1)
                g.tensor_tensor(qe, low, th, ALU.mult).then_inc(s["qe_sb"], 1)

            for h in range(NHALF):
                rsqrt(0, h)
            rest_of_constants()
            for h in range(NHALF):
                hb = slice(h * HALF, (h + 1) * HALF)
                pool.wait_ge(s["q_sb"], h + 1)
                g.tensor_scalar(qTb[:, hb, :], qT[:, hb, :], 1.0, 1.0, ALU.mult, ALU.mult).then_inc(s["lowp"], 1)
                pool.wait_ge(s["k_sb"], h + 1)
                for j in range(2):
                    g.tensor_scalar(kTb[:, j, hb, :], kT[:, hb, :], evod[:, j:j + 1], 1.0,
                                    ALU.mult, ALU.mult).then_inc(s["lowp"], 1)
            pool.wait_ge(s["hT_sb"], 2 * NHALF)
            for n in range(NH):
                g.tensor_scalar(cosm[1][:, :, n, :], qh[:, HALF:B, :], hm[:, 1, n:n + 1], 1.0,
                                ALU.mult, ALU.mult).then_inc(s["cosm1"], 1)
            pool.wait_ge(s["cos_ps"], GROUPS // NHALF)
            for n in range(NH):
                g.tensor_scalar(dotm[1][:, :, n, :], qT[:, HALF:B, :], hm[:, 0, n:n + 1], 1.0,
                                ALU.mult, ALU.mult).then_inc(s["dotm1"], 1)
            pool.wait_ge(s["l_rows"], 16 * 5)
            pool.wait_ge(s["tT_ps"], 2)
            pool.wait_ge(s["ln_st"], 2)
            for b in range(B):
                g.tensor_tensor(xs[:, b, :], xs[:, b, :], be2r[:], ALU.add)
                last = g.tensor_tensor(xn[:, b, :], xn[:, b, :], bor[:], ALU.add)
            last.then_inc(s["xb_done"], 1)
            pool.wait_ge(s["l_mask"], 16)
            g.tensor_scalar(mlow[:], mk[:], -1.0, 1.0, ALU.is_lt, ALU.mult).then_inc(s["mlow_done"], 1)
            pool.wait_ge(s["arg_sb"], GROUPS // NHALF)
            g.iota(pay[:, :, D + 1].bitcast(I32), [[S, B]], base=0, channel_multiplier=1).then_inc(s["c_pay"], 1)
            for k in range(NSLOTS):
                for j, p in AT[k]:
                    if j in NORM_OF_STAGE:
                        rsqrt(NORM_OF_STAGE[j], p)
                for j, p in AT[k]:
                    if j == 2:
                        cosine_of(p)
                for j, p in AT[k]:
                    if j == 12:
                        pool.wait_ge(s["si_sb"], p + 1)
                        pool.wait_ge(s["pay_res"], p + 1)
                        if p == 0:
                            pool.wait_ge(s["zrow"], 16)
                        for b in range(p * PAIR, (p + 1) * PAIR):
                            g.indirect_dma_start(toks, bass.IndirectOffsetOnAxis(ap=si[:, b:b + 1], axis=0),
                                                 pay[:, b, :], None, bounds_check=SLOTS - 1,
                                                 oob_is_err=False).then_inc(s["sent"], 16)
            pool.wait_ge(s["stored"], 16 * NPAIR)
            rows = out.rearrange("b s d -> (b s) d")
            for e in range(NE):
                if e % 4 == 0:
                    pool.wait_ge(s[f"back{e // 4}"], 16)
                pool.wait_ge(s["eo_sb"], e + 1)
                g.indirect_dma_start(rows, bass.IndirectOffsetOnAxis(ap=xd[:, e, D + 1:D + 2].bitcast(U32), axis=0),
                                     eo[:, e, :], None, bounds_check=TOK - 1, oob_is_err=False).then_inc(s["routed"], 16)
            pool.wait_ge(s["routed"], 16 * NE)

        def att_evac(act, a, b):
            act.wait_ge(s["atT_ps"], b + 1)
            if b >= 2:
                act.wait_ge(s["y_ps"], b - 1)
            a.activation(atT[:, b % 2, :], ps[4 + b % 2][:, 256:384], ACT.Copy).then_inc(s["atT_sb"], 1)

        @block.scalar
        def _(act):
            a = nc.scalar
            act.dma_start(wcs[:], Wc.rearrange("n d q -> (n d) q")).then_inc(s["l_wc"], 16)
            act.dma_start(bcols[:, 0:1], bq.rearrange("n d -> (n d)").rearrange("(p a) -> p a", a=1)).then_inc(s["l_bias"], 16)
            act.dma_start(bcols[:, 1:2], bk.rearrange("n d -> (n d)").rearrange("(p a) -> p a", a=1)).then_inc(s["l_bias"], 16)
            act.dma_start(bcr, row(bc.rearrange("n q -> (n q)")).broadcast_to([128, 64])).then_inc(s["l_bias"], 16)
            chain = [0]

            def link(ins):
                chain[0] += 1
                ins.then_inc(s["ach"], 1)
                act.wait_ge(s["ach"], chain[0])

            a.preload_act_table(ACT.Exp)
            act.wait_ge(s["wT_ps"], 1)
            a.activation(wqT.rearrange("p a b -> p (a b)"), ps[4][:, 0:256], ACT.Copy).then_inc(s["wT_sb"], 1)
            act.wait_ge(s["wc_ps"], 1)
            a.activation(wqk, ps[5][:, 0:128], ACT.Copy).then_inc(s["wc_sb"], 1)
            act.wait_ge(s["l_bias"], 48)
            link(a.activation(bcols[:, 2:3], bcols[:, 0:1], ACT.Copy, scale=0.125))
            for h in range(NHALF):
                hb = slice(h * HALF, (h + 1) * HALF)
                act.wait_ge(s["tT_ps"], h + 1)
                a.activation(tT[:, hb, :], quads(2 + h), ACT.Copy).then_inc(s["tT_sb"], 1)
            for h in range(NHALF):
                hb = slice(h * HALF, (h + 1) * HALF)
                act.wait_ge(s["proj_ps"], 2 * h + 1)
                a.activation(qT[:, hb, :], quads(6), ACT.Identity, bias=bcols[:, 2:3], scale=0.125).then_inc(s["q_sb"], 1)
                act.wait_ge(s["proj_ps"], 2 * h + 2)
                a.activation(kT[:, hb, :], quads(7), ACT.Identity, bias=bcols[:, 1:2]).then_inc(s["k_sb"], 1)

            def spread_maxima(h, n):
                act.wait_ge(s["mT_ps"], h + 1)
                a.activation(bd[:, h, n, :], ps[6 + h][0:32, 0:128], ACT.Copy, scale=diag[:, n:n + 1]).then_inc(s["bd_sb"], 1)

            def unit_evac(h):
                for j, dst in enumerate((qh, kh)):
                    act.wait_ge(s["hT_ps"], 2 * h + j + 1)
                    a.activation(dst[:, h * HALF:(h + 1) * HALF, :], quads(6 * h + j), ACT.Copy).then_inc(s["hT_sb"], 1)

            unit_evac(0)
            unit_evac(1)
            a.preload_act_table(ACT.Sin)
            for k in range(GROUPS):
                act.wait_ge(s["cos_ps"], k + 1)
                if k == 12:
                    act.wait_ge(s["fu_ps"], 2)
                a.activation(group(k), ps[COS_BANK[k % 4]][:], ACT.Sin, scale=PI_IN).then_inc(s["sin_sb"], 1)
                if 2 <= k < 2 + NH:
                    n = k - 2
                    a.activation(dotm[0][:, :, n, :], qT[:, 0:HALF, :], ACT.Copy,
                                 scale=hm[:, 0, n:n + 1]).then_inc(s["dotm0"], 1)
                if k == 4:
                    act.wait_ge(s["fw_ps"], 1)
                    a.activation(fw1T.rearrange("p a b -> p (a b)"), ps[6][:], ACT.Copy).then_inc(s["fw_sb"], 1)
                if k == 6:
                    act.wait_ge(s["fw_ps"], 2)
                    a.activation(fwqoT[:, 0:NQ, :], ps[7][:, 0:32].rearrange("p (c q) -> p q c", c=4), ACT.Copy).then_inc(s["fw_sb"], 1)
                    a.activation(gwT[:], ps[7][:, 64:64 + NE], ACT.Copy).then_inc(s["fw_sb"], 1)
                if k >= 13:
                    for n in range(3 * (k - 13), min(3 * (k - 12), NH)):
                        spread_maxima(0, n)
                if k == 9:
                    act.wait_ge(s["fu_ps"], 1)
                    a.activation(w1m[:], ps[6][:, 0:NQ], ACT.Copy).then_inc(s["fu_sb"], 1)

            def stage(j, p):
                pb = batches(p)
                if j == 1:
                    act.wait_ge(s["y1T_ps"], p + 1)
                    a.activation(tT[:, pb, :], turned(p), ACT.Copy).then_inc(s["y1T_sb"], 1)
                if j == 2:
                    act.wait_ge(s["qm_sb"], p + 1)
                    a.activation(ffs[:, 1, pb, :], ffs[:, 0, pb, :], ACT.Tanh).then_inc(s["th_sb"], 1)
                if j == 3:
                    act.wait_ge(s["qeT_ps"], p + 1)
                    if p >= 2:
                        act.wait_ge(s["ff_ps"], p - 1)
                    else:
                        act.wait_ge(s["c_rest"], 1)
                    a.activation(qeT[0:NQ, p % 2, :], ps[PAIR_BANK[p]][0:NQ, 0:PAIR * 128], ACT.Copy).then_inc(s["qeT_sb"], 1)
                if j == 6:
                    act.wait_ge(s["x3T_ps"], p + 1)
                    a.activation(tT[:, pb, :], turned(p), ACT.Copy).then_inc(s["x3T_sb"], 1)
                if j == 7:
                    act.wait_ge(s["lg_ps"], p + 1)
                    act.wait_ge(s["rstd_done"], norm_count(3, p))
                    for b in range(p * PAIR, (p + 1) * PAIR):
                        last = a.activation(lg_[:, b, :], product(p)[:, b % PAIR, :], ACT.Copy, scale=rstd[:, 3, b:b + 1])
                    last.then_inc(s["lg_raw"], 1)
                    act.wait_ge(s["lg_sb"], p + 1)
                    for b in range(p * PAIR, (p + 1) * PAIR):
                        a.activation(lg_[:, b, :], lg_[:, b, :], ACT.Exp, bias=ngm[:, b:b + 1],
                                     accum_out=sume[:, b:b + 1]).then_inc(s["ex_sb"], 1)
                if j == 8:
                    act.wait_ge(s["pT_ps"], p + 1)
                    a.activation(pT[:, pb, :], turned(p), ACT.Copy).then_inc(s["pT_sb"], 1)
                if j == 10:
                    act.wait_ge(s["x4T_ps"], p + 1)
                    a.activation(tT[:, pb, :], turned(p), ACT.Copy).then_inc(s["x4T_sb"], 1)
                    act.wait_ge(s["xn4_sb"], p + 1)
                    if p == 0:
                        act.wait_ge(s["c_pay"], 1)
                    a.activation(pay[:, pb, D + 2:ROW], xs[:, pb, :], ACT.Copy).then_inc(s["pay_res"], 1)
                if j == 11:
                    act.wait_ge(s["rx_sb"], p + 1)
                    for b in range(p * PAIR, (p + 1) * PAIR):
                        last = a.activation(rt[:, 1, b, :], rt[:, 2, b, :], ACT.Exp, bias=r1[:, 5, b:b + 1], accum_out=r1[:, 1, b:b + 1])
                    last.then_inc(s["re_sb"], 1)

            act.wait_ge(s["small_known"], 1)
            with a.If(a.value_load(small[0:1, 0:1]) > 0):
                for k in range(GROUPS):
                    act.wait_ge(s["small_f"], k + 1)
                    if k == 0:
                        act.wait_ge(s["cos_g"], GROUPS)
                    a.activation(group(k), fval, ACT.Sin, scale=PI_IN).then_inc(s["small_sin"], 1)
            a.preload_act_table(ACT.Exp)
            for k in range(NSLOTS):
                if 1 <= k <= 4:
                    spread_maxima(1, 2 * k - 2)
                    spread_maxima(1, 2 * k - 1)
                if k in (2, 10):
                    h = k // 10
                    act.wait_ge(s["ctxT_ps"], h + 1)
                    a.activation(cxT[:, h * HALF:(h + 1) * HALF, :], quads(6 + h), ACT.Copy).then_inc(s["ctxT_sb"], 1)
                if k < GROUPS:
                    act.wait_ge(s["arg_sb"], k + 1)
                    a.activation(group(k), group(k), ACT.Exp).then_inc(s["exp_sb"], 1)
                if k % 2 == 1 and 0 <= (k - 3) // 2 < B:
                    att_evac(act, a, (k - 3) // 2)
                for j, p in AT[k]:
                    stage(j, p)
            a.preload_act_table(ACT.Gelu_apprx_tanh)
            for q in range(4):
                act.wait_ge(s["xdT_ps"], q + 1)
                a.activation(xdT[:, 4 * CAP * q:4 * CAP * (q + 1)], ps[XD_BANK[q]][:, 0:4 * CAP], ACT.Copy).then_inc(s["xdT_sb"], 1)
            for e in range(NE):
                act.wait_ge(s["hid_ps"], e + 1)
                if e >= 3:
                    act.wait_ge(s["eo_ps"], e - 2)
                a.activation(hT[:, e % 3], ps[5 + e % 3][:, 0:4 * CW].rearrange("p (c k) -> p c k", c=4)[:, :, 0:CAP],
                             ACT.Gelu_apprx_tanh).then_inc(s["hid_sb"], 1)

        @block.vector
        def _(dve):
            v = nc.vector
            chain = [0]

            def mark(ins):
                chain[0] += 1
                ins.then_inc(s["dch"], 1)
                return chain[0]

            def after(count):
                dve.wait_ge(s["dch"], count)

            def link(ins):
                after(mark(ins))

            def stats(i, src, u, written=None):
                bs = range(norm_batches(i, u).start, norm_batches(i, u).stop)
                sums = []
                for n, b in enumerate(bs):
                    if written:
                        after(written[n])
                    sums.append(mark(v.bn_stats(bns[:, b, :], src[:, b, :])))
                means = []
                for n, b in enumerate(bs):
                    after(sums[n])
                    ins = v.bn_aggr(mv[:, i, b, :], bns[:, b, :])
                    if b < bs[-1]:
                        means.append(mark(ins))
                    else:
                        ins.then_inc(s["ln_st"], 1)
                return means

            def after_mean(i, u, means, n):
                if n < len(means):
                    after(means[n])
                else:
                    dve.wait_ge(s["ln_st"], norm_count(i, u))

            def rstd_wait(i, h):
                dve.wait_ge(s["rstd_done"], norm_count(i, h))

            for h in range(NHALF):
                dve.wait_ge(s[f"l_x{h}"], 16)
                stats(0, xs, h)
                if h == 0:
                    dve.wait_ge(s["l_wc"], 16)
                    dve.wait_ge(s["c_half"], 1)
                    v.tensor_tensor(wc[:].rearrange("p (n q) -> p n q", n=NH), wcs[:].unsqueeze(1).broadcast_to([128, NH, NQ]),
                                    hm[:, 0, :].unsqueeze(2).broadcast_to([128, NH, NQ]), ALU.mult).then_inc(s["wc_diag"], 1)
            for h in range(NHALF):
                rstd_wait(0, h)
                for b in range(h * HALF, (h + 1) * HALF):
                    v.tensor_scalar(xn[:, b, :], xs[:, b, :], mv[:, 0, b, 0:1], rstd[:, 0, b:b + 1],
                                    ALU.subtract, ALU.mult).then_inc(s["xn_done"], 1)
            dve.wait_ge(s["wc_ps"], 2)
            dve.wait_ge(s["l_bias"], 48)
            bps = ps[5][:, 128:256].rearrange("p (a q) -> p a q", a=2)
            v.tensor_tensor(bqkr.rearrange("p (a q) -> p a q", a=2), bps,
                            bcr.unsqueeze(1).broadcast_to([128, 2, 64]), ALU.add).then_inc(s["wc_sb"], 1)
            v.memset(fb2[:], 0.0)
            v.memset(w2f[:], 0.0)
            link(v.memset(blank[:], 0.0))
            v.memset(blank[:, D + 1:D + 2].bitcast(I32), NOWHERE).then_inc(s["c_zero"], 1)
            v.memset(qpad, 0.0)
            v.memset(kpad, 0.0).then_inc(s["c_zero"], 1)
            for h in range(NHALF):
                hb = slice(h * HALF, (h + 1) * HALF)
                dve.wait_ge(s["qk_ps"], h + 1)
                link(v.tensor_tensor(qk[:, hb, :], quads(4 + h), bqkr.unsqueeze(1).broadcast_to([128, HALF, 128]), ALU.add))
                last = v.tensor_tensor(sq[:, hb, :], qk[:, hb, :], qk[:, hb, :], ALU.mult)
            link(last)
            ss, half_i, y, t0, t1 = (nr[:, i] for i in range(5))
            link(v.tensor_reduce(t0, sq.rearrange("p b (n q) -> p b n q", q=NQ), X, ALU.add))
            link(v.tensor_scalar(ss, t0, 1e-30, None, ALU.max))
            link(v.tensor_scalar(half_i.bitcast(I32), ss.bitcast(I32), 1, None, ALU.logical_shift_right))
            link(v.tensor_scalar(y.bitcast(I32), half_i.bitcast(I32), -1.0, 1597463007.0, ALU.mult, ALU.add))
            for _ in range(3):
                link(v.scalar_tensor_tensor(t0, y, -0.5, y, ALU.mult, ALU.mult))
                link(v.tensor_tensor(t1, t0, ss, ALU.mult))
                link(v.scalar_tensor_tensor(y, t1, 1.5, y, ALU.add, ALU.mult))
            for h in range(NHALF):
                hb = slice(h * HALF, (h + 1) * HALF)
                for j, dst in enumerate((qpad, kpad)):
                    v.tensor_tensor(dst[:, hb, 0:64].rearrange("p b (n q) -> p b n q", q=NQ),
                                    qk[:, hb, 64 * j:64 * j + 64].rearrange("p b (n q) -> p b n q", q=NQ),
                                    y[:, hb, 8 * j:8 * j + 8].unsqueeze(3).broadcast_to([128, HALF, NH, NQ]),
                                    ALU.mult).then_inc(s["pad_done"], 1)
            v.tensor_tensor(nrm[:], ss, y, ALU.mult)
            dve.wait_ge(s["c_rest"], 1)
            dve.wait_ge(s["l_rows"], 16 * 5)
            for h in range(NHALF):
                dve.wait_ge(s["v_ps"], h + 1)
                for b in range(h * HALF, (h + 1) * HALF):
                    last = v.tensor_tensor(va[:, b, :, 0:HD],
                                           ps[2 + h][:, (b % 4) * 128:(b % 4) * 128 + 128].rearrange("p (n d) -> p n d", d=HD),
                                           bvr.rearrange("p (n d) -> p n d", d=HD), ALU.add)
                last.then_inc(s["v_sb"], 1)
            dve.wait_ge(s["hT_sb"], 1)
            for n in range(NH):
                v.tensor_scalar(cosm[0][:, :, n, :], qh[:, 0:HALF, :], hm[:, 1, n:n + 1], None,
                                ALU.mult).then_inc(s["cosm0"], 1)

            for k in range(GROUPS):
                dve.wait_ge(s["sin_sb"], k + 1)
                v.scalar_tensor_tensor(group(k), group(k), 10.0, ps[COS_BANK[k % 4]][:],
                                       ALU.add, ALU.mult).then_inc(s["cos_g"], 1)
                pr, i = divmod(k, 4)
                dve.wait_ge(s["max_ps"], k + 1)
                v.tensor_reduce(mx[:, 2 * pr:2 * pr + 2, 2 * i:2 * i + 2],
                                ps[2 + k % 2][:].rearrange("p (b n t) -> p b n t", b=2, n=2), X, ALU.max).then_inc(s["max_sb"], 1)
                if k == 3:
                    for j in range(2):
                        last = v.tensor_reduce(least[:, j:j + 1], nrm[:, :, 8 * j:8 * j + 8], XY, ALU.min)
                    last.then_inc(s["least_sb"], 1)
                if k == 7:
                    dve.wait_ge(s["least_ps"], 1)
                    dve.wait_ge(s["fw_sb"], 3)
                    link(v.tensor_reduce(least2[:, 0:2], ps[7][0:1, 256:512].rearrange("p (a t) -> p a t", a=2), X, ALU.min))
                    link(v.tensor_tensor(least2[:, 2:3], least2[:, 0:1], least2[:, 1:2], ALU.mult))
                    v.tensor_scalar(small[:], least2[:, 2:3], COS_EPS, None, ALU.is_lt).then_inc(s["small_known"], 1)
                if k == 11:
                    dve.wait_ge(s["fu_ps"], 3)
                    dve.wait_ge(s["l_b2"], 32)
                    v.tensor_tensor(fbm[:, 1, :], ps[6][:, 16:16 + NQ], fbm[:, 0, :], ALU.add).then_inc(s["fu_sb"], 1)
                    link(v.tensor_tensor(w2f[0:NQ + 1, :], ps[7][0:NQ + 1, 128:256], fb2[:, 0, :], ALU.add))
                    v.tensor_tensor(w2f[0:NQ + 1, :], w2f[0:NQ + 1, :], fb2[:, 1, :], ALU.add).then_inc(s["fu_sb"], 1)

            def guarded(k):
                b, gi = divmod(k, 2)
                hs = slice(HG * gi, HG * gi + HG)
                if k:
                    dve.wait_ge(s["small_ps"], 2 * k)
                for i in range(HG):
                    v.tensor_scalar(masked[:, i * 128:(i + 1) * 128], qh[:, b, :], hm[:, 1, HG * gi + i:HG * gi + i + 1], None,
                                    ALU.mult)
                dve.wait_ge(s["small_ps"], 2 * k + 1)
                v.tensor_copy(kn, ps[6][0:NH, 128:256])
                v.tensor_tensor(an.rearrange("p (n s) -> p n s", n=HG),
                                ps[6][0:NH, 0:128].unsqueeze(1).broadcast_to([NH, HG, S]),
                                diag[0:NH, hs].unsqueeze(2).broadcast_to([NH, HG, S]), ALU.mult).then_inc(s["small_ops"], 1)
                dve.wait_ge(s["small_ps"], 2 * k + 2)
                g_count[0] += 1
                v.tensor_scalar(scaled, ps[1][:], 1.0 / COS_EPS, 1.0, ALU.mult, ALU.min).then_inc(s["small_g"], 1)
                dve.wait_ge(s["small_g"], g_count[0])
                v.tensor_tensor(fval, ps[0][:], scaled, ALU.mult).then_inc(s["small_f"], 1)
                dve.wait_ge(s["small_sin"], k + 1)
                g_count[0] += 1
                v.scalar_tensor_tensor(group(k), group(k), 10.0, fval, ALU.add, ALU.mult).then_inc(s["small_g"], 1)
                dve.wait_ge(s["small_g"], g_count[0])

            g_count = [0]
            with v.If(v.value_load(small[0:1, 0:1]) > 0):
                for k in range(GROUPS):
                    guarded(k)

            def arg(k):
                dve.wait_ge(s["dot_ps"], k + 1)
                if k == 0:
                    dve.wait_ge(s["cos_g"], GROUPS)
                v.scalar_tensor_tensor(group(k), group(k), 0.05, ps[k % 2][:], ALU.mult, ALU.add).then_inc(s["arg_sb"], 1)

            def divide(b):
                dve.wait_ge(s["o_ps"], b + 1)
                if b >= 2:
                    dve.wait_ge(s["atT_ps"], b - 1)
                o = ps[2 + b % 2][:, 0:256].rearrange("p (n c) -> p n c", c=32)
                link(v.reciprocal(rec[:, b % 2, :], o[:, :, HD]))
                v.tensor_tensor(at[:, b % 2, :].rearrange("p (n d) -> p n d", d=HD), o[:, :, 0:HD],
                                rec[:, b % 2, :].unsqueeze(2).broadcast_to([128, NH, HD]), ALU.mult).then_inc(s["at_sb"], 1)

            def resid(b):
                dve.wait_ge(s["y_ps"], b + 1)
                if b == 0:
                    dve.wait_ge(s["xb_done"], 1)
                v.tensor_tensor(y1[:, b, :], ps[4 + b % 2][:, 384:512], xn[:, b, :], ALU.add).then_inc(s["y_sb"], 1)

            def by_query(a8):
                return a8.unsqueeze(2).broadcast_to([128, PAIR, NE])

            def stage(j, p):
                pb = batches(p)
                bs = range(pb.start, pb.stop)
                if j == 0:
                    dve.wait_ge(s["y_sb"], PAIR * (p + 1))
                    means = stats(1, y1, p)
                    for n, b in enumerate(bs):
                        after_mean(1, p, means, n)
                        last = v.scalar_tensor_tensor(y1[:, b, :], y1[:, b, :], mv[:, 1, b, 0:1], g1r[:], ALU.subtract, ALU.mult)
                    last.then_inc(s["y1_sb"], 1)
                if j == 2:
                    dve.wait_ge(s["qm_ps"], p + 1)
                    rstd_wait(1, p)
                    if p == 0:
                        dve.wait_ge(s["fu_sb"], 3)
                    for b in bs:
                        last = v.scalar_tensor_tensor(ffs[:, 0, b, :], product(p)[:, 0, (b % PAIR) * NQ:(b % PAIR + 1) * NQ],
                                                      rstd[:, 1, b:b + 1], fbm[:, 1, :], ALU.mult, ALU.add)
                    last.then_inc(s["qm_sb"], 1)
                if j == 4:
                    dve.wait_ge(s["ff_ps"], p + 1)
                    sums = [mark(v.scalar_tensor_tensor(y1[:, b, :], y1[:, b, :], rstd[:, 1, b:b + 1], product(p)[:, b % PAIR, :],
                                                        ALU.mult, ALU.add)) for b in bs]
                    stats(2, y1, p, sums)
                if j == 5:
                    rstd_wait(2, p)
                    scaled = [mark(v.scalar_tensor_tensor(y1[:, b, :], y1[:, b, :], mv[:, 2, b, 0:1], g2r[:],
                                                          ALU.subtract, ALU.mult)) for b in bs]
                    x2 = []
                    for n, b in enumerate(bs):
                        after(scaled[n])
                        x2.append(mark(v.scalar_tensor_tensor(xs[:, b, :], y1[:, b, :], rstd[:, 2, b:b + 1], xs[:, b, :],
                                                              ALU.mult, ALU.add)))
                    means = stats(3, xs, p, x2)
                    for n, b in enumerate(bs):
                        after_mean(3, p, means, n)
                        last = v.tensor_scalar(x1[:, b, :], xs[:, b, :], mv[:, 3, b, 0:1], None, ALU.subtract)
                    last.then_inc(s["xn3_sb"], 1)
                if j == 7:
                    dve.wait_ge(s["lg_raw"], p + 1)
                    if p == 0:
                        dve.wait_ge(s["mlow_done"], 1)
                    link(v.copy_predicated(lg_[:, pb, :], mlow[:, pb, :], mk[:, pb, :]))
                    v.tensor_reduce(ngm[:, pb], lg_[:, pb, :], X, ALU.max, negate=True).then_inc(s["lg_sb"], 1)
                if j == 8:
                    dve.wait_ge(s["ex_sb"], PAIR * (p + 1))
                    v.reciprocal(rsum[:, pb], sume[:, pb])
                    link(v.tensor_tensor(okr[:, pb], sume[:, pb], sume[:, pb], ALU.is_equal))
                if j == 9:
                    dve.wait_ge(s["pv_ps"], p + 1)
                    sums = [mark(v.scalar_tensor_tensor(y1[:, b, :], product(p)[:, b % PAIR, :], rsum[:, b:b + 1], xs[:, b, :],
                                                        ALU.mult, ALU.add)) for b in bs]
                    x3 = []
                    for n, b in enumerate(bs):
                        after(sums[n])
                        x3.append(mark(v.copy_predicated(xs[:, b, :], okr[:, b:b + 1].bitcast(I32).broadcast_to([128, D]),
                                                         y1[:, b, :])))
                    means = stats(4, xs, p, x3)
                    for n, b in enumerate(bs):
                        after_mean(4, p, means, n)
                        last = v.tensor_scalar(x1[:, b, :], xs[:, b, :], mv[:, 4, b, 0:1], None, ALU.subtract)
                    last.then_inc(s["xn4_sb"], 1)
                if j == 10:
                    rstd_wait(4, p)
                    dve.wait_ge(s["xn4_sb"], p + 1)
                    if p == 0:
                        dve.wait_ge(s["c_pay"], 1)
                    for b in bs:
                        last = v.tensor_scalar(pay[:, b, 0:D], x1[:, b, :], rstd[:, 4, b:b + 1], None, ALU.mult)
                    link(last)
                lg, t3 = rt[:, 2, pb, :], rt[:, 3, pb, :]
                m8, sum8, vm, rk, over, negm, sl = (r1[:, i, pb] for i in range(7))
                if j == 11:
                    dve.wait_ge(s["gt_ps"], p + 1)
                    for b in bs:
                        last = v.tensor_scalar(rt[:, 2, b, :], product(p)[:, 0, (b % PAIR) * NE:(b % PAIR + 1) * NE],
                                               rstd[:, 4, b:b + 1], None, ALU.mult)
                    link(last)
                    link(v.tensor_reduce(m8, lg, X, ALU.max))
                    v.tensor_scalar(negm, m8, -1.0, None, ALU.mult).then_inc(s["rx_sb"], 1)
                    for b in bs:
                        last = v.scalar_tensor_tensor(rt[:, 3, b, :], rt[:, 2, b, :], r1[:, 0, b:b + 1], revi[:], ALU.is_ge, ALU.mult)
                    link(last)
                    link(v.tensor_reduce(vm, t3, X, ALU.max))
                    v.tensor_tensor(ohb[:, pb, :], t3, by_query(vm), ALU.is_equal).then_inc(s["oh_sb"], 1)
                if j == 12:
                    dve.wait_ge(s["oh_sb"], p + 1)
                    if p < NPAIR - 1:
                        link(v.tensor_tensor(prev[:, (p + 1) % 2, :], ohb[:, pb.start, :], ohb[:, pb.start + 1, :], ALU.add))
                        link(v.tensor_tensor(prev[:, (p + 1) % 2, :], prev[:, (p + 1) % 2, :], prev[:, p % 2, :], ALU.add))
                    dve.wait_ge(s["re_sb"], p + 1)
                    v.reciprocal(pay[:, pb, D], sum8)
                    dve.wait_ge(s["rk_ps"], p + 1)
                    for b in bs:
                        last = v.scalar_tensor_tensor(rt[:, 3, b, :], product(p)[:, 1, (b % PAIR) * NE:(b % PAIR + 1) * NE], 1.0,
                                                      ohb[:, b, :], ALU.mult, ALU.mult, accum_out=r1[:, 3, b:b + 1])
                    link(last)
                    v.tensor_scalar(over, rk, float(CAP), float(NOWHERE), ALU.is_gt, ALU.mult)
                    link(v.scalar_tensor_tensor(sl, vm, -float(CAP), rk, ALU.mult, ALU.add))
                    v.scalar_tensor_tensor(si[:, pb], sl, float(NE * CAP - 1), over, ALU.add, ALU.add).then_inc(s["si_sb"], 1)

            for k in range(NSLOTS):
                if k < GROUPS:
                    arg(k)
                if k % 2 == 0 and 0 <= (k - 2) // 2 < B:
                    divide((k - 2) // 2)
                if k % 2 == 0 and 0 <= (k - 4) // 2 < B:
                    resid((k - 4) // 2)
                for j, p in AT[k]:
                    stage(j, p)

            dve.wait_ge(s["o_ps"], B)
            v.memset(xdT[:, SLOTS:SLOTS + CW - CAP], 0.0).then_inc(s["xd_pad"], 1)
            for e in range(NE):
                if e % 4 == 0:
                    dve.wait_ge(s[f"back{e // 4}"], 16)
                if e % (NE // 2) == 0:
                    dve.wait_ge(s[f"back_res{e // (NE // 2)}"], 16)
                dve.wait_ge(s["eo_ps"], e + 1)
                v.scalar_tensor_tensor(eo[:, e, :], ps[EO_BANK[e % 3]][0:CAP, 0:128], xd[:, e, D:D + 1], xd[:, e, D + 2:ROW],
                                       ALU.mult, ALU.add).then_inc(s["eo_sb"], 1)

        @block.tensor
        def _(pe):
            t = nc.tensor

            def turn4(bank, src, h, done):
                for i in range(HALF):
                    last = t.transpose(ps[bank][:, i * 128:(i + 1) * 128], src[:, h * HALF + i, :], ident[:])
                last.then_inc(s[done], 1)

            def keep_warm(bank, n):
                for _ in range(n):
                    t.matmul(ps[bank][:, 384:512], ident[:], ident[:], start=True, stop=True)

            pe.wait_ge(s["c_ident"], 1)
            pe.wait_ge(s["l_qk"], 32)
            t.transpose(ps[4][:, 0:128], wq, ident[:])
            t.transpose(ps[4][:, 128:256], wk, ident[:]).then_inc(s["wT_ps"], 1)
            pe.wait_ge(s["wT_sb"], 1)
            pe.wait_ge(s["wc_diag"], 1)
            for j in range(2):
                last = t.matmul(ps[5][:, 64 * j:64 * j + 64], wqT[:, j, :], wc[:], start=True, stop=True)
            last.then_inc(s["wc_ps"], 1)
            pe.wait_ge(s["l_bias"], 48)
            pe.wait_ge(s["wc_sb"], 1)
            for j in range(2):
                last = t.matmul(ps[5][:, 128 + 64 * j:192 + 64 * j], bcols[:, j:j + 1].broadcast_to([128, 128]), wc[:],
                                start=True, stop=True)
            last.then_inc(s["wc_ps"], 1)
            for h in range(NHALF):
                pe.wait_ge(s["xn_done"], HALF * (h + 1))
                turn4(2 + h, xn, h, "tT_ps")
            for h in range(NHALF):
                pe.wait_ge(s["tT_sb"], h + 1)
                pe.wait_ge(s["wc_sb"], h + 1)
                for i in range(HALF):
                    last = t.matmul(ps[4 + h][:, i * 128:(i + 1) * 128], tT[:, h * HALF + i, :], wqk, start=True, stop=True)
                last.then_inc(s["qk_ps"], 1)
            for h in range(NHALF):
                if h:
                    pe.wait_ge(s["q_sb"], h)
                tcols = tT[:, h * HALF:(h + 1) * HALF, :].rearrange("p b s -> p (b s)")
                t.matmul(ps[6][:], wq, tcols, start=True, stop=True).then_inc(s["proj_ps"], 1)
                if h:
                    pe.wait_ge(s["k_sb"], h)
                t.matmul(ps[7][:], wk, tcols, start=True, stop=True).then_inc(s["proj_ps"], 1)
                pe.wait_ge(s["l_v"], 16)
                for i in range(HALF):
                    last = t.matmul(ps[2 + h][:, i * 128:(i + 1) * 128], tT[:, h * HALF + i, :], wv, start=True, stop=True)
                last.then_inc(s["v_ps"], 1)

            pe.wait_ge(s["pad_done"], 1)
            turn4(0, qpad, 0, "hT_ps")
            pe.wait_ge(s["pad_done"], 2)
            turn4(1, kpad, 0, "hT_ps")
            pe.wait_ge(s["q_sb"], 2)
            pe.wait_ge(s["pad_done"], 3)
            turn4(6, qpad, 1, "hT_ps")
            pe.wait_ge(s["k_sb"], 2)
            pe.wait_ge(s["pad_done"], 4)
            turn4(7, kpad, 1, "hT_ps")

            def max_scores(u):
                pr, i = divmod(u, 4)
                if u >= 2:
                    pe.wait_ge(s["max_sb"], u - 1)
                else:
                    pe.wait_ge(s["v_sb"], u + 1)
                pe.wait_ge(s["lowp"], 3 * (pr // 2 + 1))
                rows = slice(32 * i, 32 * i + 32)
                for c in range(4):
                    b, par = 2 * pr + c // 2, c % 2
                    last = t.matmul(ps[2 + u % 2][:, c * 128:(c + 1) * 128], qTb[rows, b, :], kTb[rows, par, b, :], start=True, stop=True)
                last.then_inc(s["max_ps"], 1)

            def turn_maxima(h):
                pe.wait_ge(s["max_sb"], 8 * (h + 1))
                pe.wait_ge(s["fu_sb"], 3)
                t.transpose(ps[6 + h][0:32, 0:128], mx[:, h * HALF:(h + 1) * HALF, :].rearrange("p b n -> p (b n)"),
                            ident[:]).then_inc(s["mT_ps"], 1)

            keep_warm(5, 14)
            pe.wait_ge(s["hT_sb"], 2)
            for k in range(GROUPS):
                b, gi = divmod(k, 2)
                h, bb = divmod(b, HALF)
                pe.wait_ge(s[f"cosm{h}"], HG * (gi + 1))
                if k >= 4:
                    pe.wait_ge(s["cos_g"], k - 3)
                elif k >= 2:
                    pe.wait_ge(s["pad_done"], 4)
                t.matmul(ps[COS_BANK[k % 4]][:], kh[:, b, :], cosm[h][:, bb, HG * gi:HG * gi + HG, :].rearrange("p n s -> p (n s)"),
                         start=True, stop=True).then_inc(s["cos_ps"], 1)
                max_scores(k)
                if k == 3:
                    pe.wait_ge(s["l_ffw"], 16 * 8)
                    pe.wait_ge(s["hT_sb"], 3)
                    for c in range(4):
                        last = t.transpose(ps[6][:, c * 128:(c + 1) * 128], fw1[:, c:FF:4], ident[:])
                    last.then_inc(s["fw_ps"], 1)
                if k == 5:
                    pe.wait_ge(s["hT_sb"], 4)
                    pe.wait_ge(s["l_gate"], 16)
                    for c in range(4):
                        t.transpose(ps[7][:, c * NQ:(c + 1) * NQ], fwqo[:, c:FF:4], ident[0:NQ, 0:NQ])
                    t.transpose(ps[7][:, 64:64 + NE], gw, ident[0:NE, 0:NE]).then_inc(s["fw_ps"], 1)
                    pe.wait_ge(s["least_sb"], 1)
                    for j in range(2):
                        last = t.transpose(ps[7][0:1, 256 + 128 * j:384 + 128 * j], least[:, j:j + 1], ident[:])
                    last.then_inc(s["least_ps"], 1)
                if k == 8:
                    pe.wait_ge(s["fw_sb"], 3)
                    for c in range(4):
                        last = t.matmul(ps[6][:, 0:NQ], fw1T[:, c, :], fwm[:, c, :], start=(c == 0), stop=(c == 3))
                    last.then_inc(s["fu_ps"], 1)
                if k == 9:
                    pe.wait_ge(s["small_known"], 1)
                    pe.wait_ge(s["fw_sb"], 3)
                    for c in range(4):
                        last = t.matmul(ps[7][0:NQ + 1, 128:256], fwqoT[:, :, c], fw2[:, c, :], start=(c == 0), stop=(c == 3))
                    last.then_inc(s["fu_ps"], 1)
                if k == 10:
                    pe.wait_ge(s["fu_sb"], 1)
                    for c in range(4):
                        t.matmul(ps[6][:, 16:16 + NQ], fb1[:, c:c + 1].broadcast_to([128, 128]), fwm[:, c, :],
                                 start=(c == 0), stop=False)
                    t.matmul(ps[6][:, 16:16 + NQ], bcols[:, 3:4].broadcast_to([128, 128]), w1m[:],
                             start=False, stop=True).then_inc(s["fu_ps"], 1)
                if k == 12:
                    turn_maxima(0)
            pe.wait_ge(s["fu_sb"], 3)
            with t.If(t.value_load(small[0:1, 0:1]) > 0):
                pe.wait_ge(s["bd_sb"], NH)
                pe.wait_ge(s["cos_g"], GROUPS)
                for k in range(GROUPS):
                    b, gi = divmod(k, 2)
                    if k:
                        pe.wait_ge(s["small_g"], 2 * k)
                    for j in range(2):
                        last = t.transpose(ps[6][0:NH, 128 * j:128 * j + 128], nrm[:, b, 8 * j:8 * j + 8], ident[:])
                    last.then_inc(s["small_ps"], 1)
                    pe.wait_ge(s["small_ops"], k + 1)
                    t.matmul(ps[1][:], kn, an, start=True, stop=True)
                    t.matmul(ps[0][:], kh[:, b, :], masked, start=True, stop=True).then_inc(s["small_ps"], 1)
                pe.wait_ge(s["small_g"], 2 * GROUPS)
            keep_warm(7, 3)
            turn_maxima(1)

            def dots(k):
                b, gi = divmod(k, 2)
                h, bb = divmod(b, HALF)
                pe.wait_ge(s[f"dotm{h}"], NH)
                pe.wait_ge(s["bd_sb"], NH * h + HG * (gi + 1))
                if k >= 2:
                    pe.wait_ge(s["arg_sb"], k - 1)
                else:
                    pe.wait_ge(s["cos_g"], GROUPS - 3 + k)
                t.matmul(ps[k % 2][:], kT[:, b, :], dotm[h][:, bb, HG * gi:HG * gi + HG, :].rearrange("p n s -> p (n s)"),
                         start=True, stop=False)
                t.matmul(ps[k % 2][:], negsel[:, bb, :], bd[:, h, HG * gi:HG * gi + HG, :].rearrange("p n s -> p (n s)"),
                         start=False, stop=True).then_inc(s["dot_ps"], 1)

            def pv(k):
                b, gi = divmod(k, 2)
                pe.wait_ge(s["exp_sb"], k + 1)
                if gi == 0:
                    if b >= 2:
                        pe.wait_ge(s["at_sb"], b - 1)
                    else:
                        pe.wait_ge(s["max_sb"], GROUPS)
                for i in range(HG):
                    n = HG * gi + i
                    last = t.matmul(ps[2 + b % 2][:, n * 32:n * 32 + HD + 1], G[:, b, n, :], va[:, b, n, :], start=True, stop=True)
                if gi:
                    last.then_inc(s["o_ps"], 1)

            def turn_att(b):
                pe.wait_ge(s["at_sb"], b + 1)
                if b >= 2:
                    pe.wait_ge(s["y_sb"], b - 1)
                t.transpose(ps[4 + b % 2][:, 256:384], at[:, b % 2, :], ident[:]).then_inc(s["atT_ps"], 1)

            def project(b):
                pe.wait_ge(s["atT_sb"], b + 1)
                if b == 0:
                    pe.wait_ge(s["l_wo"], 16)
                t.matmul(ps[4 + b % 2][:, 384:512], atT[:, b % 2, :], wo[:], start=True, stop=True).then_inc(s["y_ps"], 1)

            def turn2(p, src, done):
                for i in range(PAIR):
                    last = t.transpose(turned(p)[:, i, :], src[:, p * PAIR + i, 0:128], ident[:])
                last.then_inc(s[done], 1)

            def stage(j, p):
                bs = range(p * PAIR, (p + 1) * PAIR)
                if j == 1:
                    pe.wait_ge(s["y1_sb"], p + 1)
                    pe.wait_ge(*((s["ctxT_sb"], 2) if p < 2 else (s["arg_sb"], GROUPS)))
                    turn2(p, y1, "y1T_ps")
                if j == 2:
                    pe.wait_ge(s["y1T_sb"], p + 1)
                    pe.wait_ge(s["fu_sb"], 3)
                    for b in bs:
                        last = t.matmul(product(p)[:, 0, (b % PAIR) * NQ:(b % PAIR + 1) * NQ], tT[:, b, :], w1m[:], start=True, stop=True)
                    last.then_inc(s["qm_ps"], 1)
                if j == 3:
                    pe.wait_ge(s["qe_sb"], p + 1)
                    for b in bs:
                        last = t.transpose(turned(p)[0:NQ, b % PAIR, :], ffs[:, 5, b, :], ident[:])
                    last.then_inc(s["qeT_ps"], 1)
                if j == 4:
                    pe.wait_ge(s["qeT_sb"], p + 1)
                    for b in bs:
                        last = t.matmul(product(p)[:, b % PAIR, :], qeT[:, p % 2, (b % PAIR) * 128:(b % PAIR + 1) * 128], w2f[:],
                                        start=True, stop=True)
                    last.then_inc(s["ff_ps"], 1)
                if j == 6:
                    pe.wait_ge(s["xn3_sb"], p + 1)
                    turn2(p, x1, "x3T_ps")
                if j == 7:
                    pe.wait_ge(s["x3T_sb"], p + 1)
                    for b in bs:
                        last = t.matmul(product(p)[:, b % PAIR, :], tT[:, b, :], cxT[:, b, :], start=True, stop=True)
                    last.then_inc(s["lg_ps"], 1)
                if j == 8:
                    pe.wait_ge(s["ex_sb"], PAIR * (p + 1))
                    turn2(p, lg_, "pT_ps")
                if j == 9:
                    pe.wait_ge(s["pT_sb"], p + 1)
                    for b in bs:
                        last = t.matmul(product(p)[:, b % PAIR, :], pT[:, b, :], cx[:, b, :], start=True, stop=True)
                    last.then_inc(s["pv_ps"], 1)
                if j == 10:
                    pe.wait_ge(s["xn4_sb"], p + 1)
                    turn2(p, x1, "x4T_ps")
                if j == 11:
                    pe.wait_ge(s["x4T_sb"], p + 1)
                    for b in bs:
                        last = t.matmul(product(p)[:, 0, (b % PAIR) * NE:(b % PAIR + 1) * NE], tT[:, b, :], gwT[:], start=True, stop=True)
                    last.then_inc(s["gt_ps"], 1)
                if j == 12:
                    pe.wait_ge(s["oh_sb"], p + 1)
                    rank = product(p)[:, 1, 0:PAIR * NE].rearrange("p (b e) -> p b e", b=PAIR)
                    t.matmul(rank, tri[:], ohb[:, batches(p), :], start=True, stop=False, skip_group_check=True)
                    t.matmul(rank[:, 1, :], onesb[:], ohb[:, p * PAIR, :], start=False, stop=False, skip_group_check=True)
                    if p:
                        pe.wait_ge(s["si_sb"], p)
                    last = t.matmul(rank, onesb[:], prev[:, p % 2, :].unsqueeze(1).broadcast_to([128, PAIR, NE]),
                                    start=False, stop=True, skip_group_check=True)
                    last.then_inc(s["rk_ps"], 1)

            for k in range(NSLOTS):
                if k < GROUPS:
                    dots(k)
                if 1 <= k <= GROUPS:
                    pv(k - 1)
                if k in (1, 9):
                    pe.wait_ge(s["l_ctx"], 16)
                    turn4(6 + k // 9, cx, k // 9, "ctxT_ps")
                if k % 2 == 1 and 0 <= (k - 3) // 2 < B:
                    turn_att((k - 3) // 2)
                if k % 2 == 0 and 0 <= (k - 4) // 2 < B:
                    project((k - 4) // 2)
                for j, p in AT[k]:
                    stage(j, p)

            keep_warm(7, 22)
            for q in range(4):
                pe.wait_ge(s[f"back{q}"], 16)
                for i in range(4):
                    last = t.transpose(ps[XD_BANK[q]][:, i * CAP:(i + 1) * CAP], xd[:, 4 * q + i, 0:D], ident[0:CAP, 0:CAP])
                last.then_inc(s["xdT_ps"], 1)

            def hidden(e):
                if e % 4 == 0:
                    pe.wait_ge(s["xdT_sb"], min(e // 4 + 2, 4))
                if e == 0:
                    pe.wait_ge(s["xd_pad"], 1)
                if e % 4 == 0:
                    pe.wait_ge(s["l_w1"], 16 * 4)
                if e >= 3:
                    pe.wait_ge(s["hid_sb"], e - 2)
                for c in range(4):
                    last = t.matmul(ps[5 + e % 3][:, c * CW:(c + 1) * CW], w1s[:, e, c * 128:(c + 1) * 128],
                                    xdT[:, e * CAP:e * CAP + CW], start=True, stop=True)
                last.then_inc(s["hid_ps"], 1)

            def expert_out(e):
                pe.wait_ge(s["hid_sb"], e + 1)
                if e == 0:
                    pe.wait_ge(s["xdT_sb"], 4)
                    pe.wait_ge(s["l_w2"], 16 * 4)
                if e >= 3:
                    pe.wait_ge(s["eo_sb"], e - 2)
                for c in range(4):
                    last = t.matmul(ps[EO_BANK[e % 3]][0:CAP, 0:128], hT[:, e % 3, c, :], w2s[:, e, c, :],
                                    start=(c == 0), stop=(c == 3))
                last.then_inc(s["eo_ps"], 1)

            for e in range(NE + 1):
                if e < NE:
                    hidden(e)
                if e:
                    expert_out(e - 1)


_INS = ['x', 'ctx_1024', 'mask_BxSxS2_fk0'] + ['L0_attn_' + n for n in (
    'Wq', 'bq', 'Wk', 'bk', 'Wv', 'bv', 'Wc2q', 'bc2q', 'Wo', 'bo', 'g1', 'beta1', 'g2', 'beta2', 'W1', 'b1',
    'Wm', 'bm', 'Wqo', 'bqo', 'W2', 'b2')] + ['L0_ffn_gate_w', 'L0_ffn_w1', 'L0_ffn_w2']


def kernel(**inputs):
    import concourse.bacc as _bacc
    from concourse.bass_utils import run_bass_kernel_spmd as _run

    nc = _bacc.Bacc("TRN2", target_bir_lowering=False, num_devices=1)
    arrays, args = {}, []
    for name in _INS:
        a = np.ascontiguousarray(inputs[name])
        arrays[f"in_{name}"] = a
        args.append(nc.dram_tensor(f"in_{name}", a.shape, mybir.dt.from_np(a.dtype), kind="ExternalInput").ap())
    out = nc.dram_tensor("out_0", (B, S, D), F32, kind="ExternalOutput").ap()
    decoder_block(nc, *args, out)
    r = _run(nc, [arrays], core_ids=[0])
    return r.results[0]["out_0"]
```
